# Optimizing a Trainium2 kernel written in Bass

```python
import numpy as np
import jax
import jax.numpy as jnp

def _softmax(x, axis=-1):
    return jax.nn.softmax(x, axis=axis)
def _gelu(x):
    return jax.nn.gelu(x, approximate=True)
def _silu(x):
    return jax.nn.silu(x)
def _sigmoid(x):
    return jax.nn.sigmoid(x)
def _layernorm(x, axis=-1, eps=1e-5):
    m = jnp.mean(x, axis=axis, keepdims=True)
    v = jnp.var(x, axis=axis, keepdims=True)
    return (x - m) / jnp.sqrt(v + eps)
def _scatter_add(tgt, idx, src, axis=0):
    return tgt.at[idx].add(src)
def _segment_sum(src, seg, n):
    return jax.ops.segment_sum(src, seg, n)

kernel_name = 'mk_conv_seq_d4_conv_nchw128_a60b3b'

def setup_inputs(seed: int = 0):
    np.random.seed(seed)
    _w = jnp.asarray
    def _rec_inputs():
        import jax
        import jax.numpy as jnp
        _gk = jax.random.key(seed)
        x = -0.0002023 + 1 * jax.random.normal(jax.random.fold_in(_gk, 1), (16, 128, 56, 56), jnp.float32)
        return x
    x = _rec_inputs()
    def _L0_conv_setup():
        import jax, jax.numpy as jnp
        import numpy as np
        B, C, H, W = (16, 128, 56, 56)
        QK, HEADS, NWIN, TOPK, MLPR = (128, 4, 7, 4, 3)
        HD_Q, HD_V = (QK // HEADS, C // HEADS)
        WH, WW = (H // NWIN, W // NWIN)
        P2, W2 = (NWIN * NWIN, WH * WW)
        SCALE = QK ** (-0.5)

        def _dwconv(x, w, b):
            y = jax.lax.conv_general_dilated(x, w, (1, 1), 'SAME', feature_group_count=x.shape[1], dimension_numbers=('NCHW', 'OIHW', 'NCHW'))
            return y + b[None, :, None, None]

        def _ln(x, g, b):
            m = x.mean(-1, keepdims=True)
            v = ((x - m) ** 2).mean(-1, keepdims=True)
            return (x - m) * jax.lax.rsqrt(v + 1e-06) * g + b

        def _win(t):
            b, _, _, c = t.shape
            return t.reshape(b, NWIN, WH, NWIN, WW, c).transpose(0, 1, 3, 2, 4, 5).reshape(b, P2, WH, WW, c)

        def _unwin(t):
            b, c = (t.shape[0], t.shape[-1])
            return t.reshape(b, NWIN, NWIN, WH, WW, c).transpose(0, 1, 3, 2, 4, 5).reshape(b, H, W, c)
        key = jax.random.key(seed)
        ks = jax.random.split(key, 8)
        p = lambda k, sh: (0.02 * jax.random.normal(k, sh)).astype(jnp.float32)
        return {'x': jax.random.normal(ks[0], (B, C, H, W), dtype=jnp.float32), 'pos_w': p(ks[1], (C, 1, 3, 3)), 'pos_b': jnp.zeros((C,), jnp.float32), 'ln1_g': jnp.ones((C,), jnp.float32), 'ln1_b': jnp.zeros((C,), jnp.float32), 'qkv_w': p(ks[2], (C, 2 * QK + C)), 'qkv_b': jnp.zeros((2 * QK + C,), jnp.float32), 'lepe_w': p(ks[3], (C, 1, 5, 5)), 'lepe_b': jnp.zeros((C,), jnp.float32), 'wo_w': p(ks[4], (C, C)), 'wo_b': jnp.zeros((C,), jnp.float32), 'ln2_g': jnp.ones((C,), jnp.float32), 'ln2_b': jnp.zeros((C,), jnp.float32), 'mlp_w1': p(ks[5], (C, MLPR * C)), 'mlp_b1': jnp.zeros((MLPR * C,), jnp.float32), 'mlp_w2': p(ks[6], (MLPR * C, C)), 'mlp_b2': jnp.zeros((C,), jnp.float32)}
    _L0_conv_all = _L0_conv_setup()
    _L0_conv_in = {k: v for k, v in _L0_conv_all.items() if k in ('pos_w', 'pos_b', 'ln1_g', 'ln1_b', 'qkv_w', 'qkv_b', 'lepe_w', 'lepe_b', 'wo_w', 'wo_b', 'ln2_g', 'ln2_b', 'mlp_w1', 'mlp_b1', 'mlp_w2', 'mlp_b2', )}
    del _L0_conv_all

    def _L1_conv_setup():
        import jax, jax.numpy as jnp
        import numpy as np
        GN_GROUPS = 32
        GN_EPS = 1e-05

        def _conv3x3(x, w, b):
            y = jax.lax.conv_general_dilated(x, w, (1, 1), [(1, 1), (1, 1)], dimension_numbers=('NCHW', 'OIHW', 'NCHW'))
            return y + b[None, :, None, None]

        def _bilinear(x, py, px):
            N, C, H, W = x.shape
            y0 = jnp.floor(py)
            x0 = jnp.floor(px)
            wy = py - y0
            wx = px - x0
            xf = x.reshape(N, C, H * W)
            out = jnp.zeros((N, C, H, W), x.dtype)
            corners = ((y0, x0, (1 - wy) * (1 - wx)), (y0, x0 + 1, (1 - wy) * wx), (y0 + 1, x0, wy * (1 - wx)), (y0 + 1, x0 + 1, wy * wx))
            for yy, xx, w in corners:
                valid = ((yy >= 0) & (yy <= H - 1) & (xx >= 0) & (xx <= W - 1)).astype(x.dtype)
                yi = jnp.clip(yy, 0, H - 1).astype(jnp.int32)
                xi = jnp.clip(xx, 0, W - 1).astype(jnp.int32)
                idx = (yi * W + xi).reshape(N, 1, H * W)
                g = jnp.take_along_axis(xf, idx, axis=2).reshape(N, C, H, W)
                out = out + g * (w * valid)[:, None]
            return out
        key = jax.random.key(seed)
        ks = jax.random.split(key, 8)
        N, C, H, W = (4, 128, 160, 160)
        s = 0.05
        return {'x': jax.random.normal(ks[0], (N, C, H, W), jnp.float32), 'w_tm': jax.random.normal(ks[1], (4, C, 3, 3), jnp.float32) * s, 'b_tm': jax.random.normal(ks[2], (4,), jnp.float32) * s, 'w_tr': jax.random.normal(ks[3], (2, C, 3, 3), jnp.float32) * s, 'b_tr': jax.random.normal(ks[4], (2,), jnp.float32) * s, 'w_dcn': jax.random.normal(ks[5], (C, C, 3, 3), jnp.float32) * s, 'gn_gamma': jnp.ones((C,), jnp.float32), 'gn_beta': jnp.zeros((C,), jnp.float32)}
    _L1_conv_all = _L1_conv_setup()
    _L1_conv_in = {k: v for k, v in _L1_conv_all.items() if k in ('w_tm', 'b_tm', 'w_tr', 'b_tr', 'w_dcn', 'gn_gamma', 'gn_beta', )}
    del _L1_conv_all

    def _L2_conv_setup():
        import jax, jax.numpy as jnp
        import numpy as np
        HIDDEN = 128
        NUM_BLOCKS = 8
        BLOCK = HIDDEN // NUM_BLOCKS
        HSF = 1
        LAMBDA = 0.01
        SCALE = 0.02

        def softshrink(v, lam):
            return jnp.sign(v) * jnp.maximum(jnp.abs(v) - lam, 0.0)
        key = jax.random.key(seed)
        k0, k1, k2, k3, k4 = jax.random.split(key, 5)
        x = jax.random.normal(k0, (4, HIDDEN, 256, 256), dtype=jnp.float32)
        w1 = SCALE * jax.random.normal(k1, (2, NUM_BLOCKS, BLOCK, BLOCK * HSF), dtype=jnp.float32)
        b1 = SCALE * jax.random.normal(k2, (2, NUM_BLOCKS, BLOCK * HSF), dtype=jnp.float32)
        w2 = SCALE * jax.random.normal(k3, (2, NUM_BLOCKS, BLOCK * HSF, BLOCK), dtype=jnp.float32)
        b2 = SCALE * jax.random.normal(k4, (2, NUM_BLOCKS, BLOCK), dtype=jnp.float32)
        return {'x': x, 'w1': w1, 'b1': b1, 'w2': w2, 'b2': b2}
    _L2_conv_all = _L2_conv_setup()
    _L2_conv_in = {k: v for k, v in _L2_conv_all.items() if k in ('w1', 'b1', 'w2', 'b2', )}
    del _L2_conv_all

    def _L3_conv_setup():
        import jax, jax.numpy as jnp
        import numpy as np
        DN = ('NCHW', 'OIHW', 'NCHW')

        def fake_quant(x, bits):
            qmax = float(2 ** (bits - 1) - 1)
            scale = jnp.maximum(jnp.max(jnp.abs(x)) / qmax, 1e-08)
            q = jnp.clip(jnp.round(x / scale), -qmax - 1.0, qmax) * scale
            return x + jax.lax.stop_gradient(q - x)

        def qconv(x, w, b, groups, pad):
            xq = fake_quant(x, 8)
            wq = fake_quant(w, 4)
            y = jax.lax.conv_general_dilated(xq, wq, window_strides=(1, 1), padding=[(pad, pad), (pad, pad)], feature_group_count=groups, dimension_numbers=DN)
            return y + b[None, :, None, None]
        key = jax.random.key(seed)
        ks = jax.random.split(key, 9)
        B, C, H, W = (8, 128, 192, 192)
        x = jax.random.normal(ks[0], (B, C, H, W), dtype=jnp.float32)
        s3 = 1.0 / np.sqrt(9.0)
        s1 = 1.0 / np.sqrt(float(C))
        w1 = jax.random.uniform(ks[1], (C, 1, 3, 3), jnp.float32, -s3, s3)
        b1 = jax.random.uniform(ks[2], (C,), jnp.float32, -s3, s3)
        p1 = jax.random.uniform(ks[3], (C, C, 1, 1), jnp.float32, -s1, s1)
        pb1 = jax.random.uniform(ks[4], (C,), jnp.float32, -s1, s1)
        w2 = jax.random.uniform(ks[5], (C, 1, 3, 3), jnp.float32, -s3, s3)
        b2 = jax.random.uniform(ks[6], (C,), jnp.float32, -s3, s3)
        p2 = jax.random.uniform(ks[7], (C, C, 1, 1), jnp.float32, -s1, s1)
        pb2 = jax.random.uniform(ks[8], (C,), jnp.float32, -s1, s1)
        return {'x': x, 'w1': w1, 'b1': b1, 'p1': p1, 'pb1': pb1, 'w2': w2, 'b2': b2, 'p2': p2, 'pb2': pb2}
    _L3_conv_all = _L3_conv_setup()
    _L3_conv_in = {k: v for k, v in _L3_conv_all.items() if k in ('w1', 'b1', 'p1', 'pb1', 'w2', 'b2', 'p2', 'pb2', )}
    del _L3_conv_all

    return {
        "x": x,
        "L0_conv_pos_w": _L0_conv_in["pos_w"],
        "L0_conv_pos_b": _L0_conv_in["pos_b"],
        "L0_conv_ln1_g": _L0_conv_in["ln1_g"],
        "L0_conv_ln1_b": _L0_conv_in["ln1_b"],
        "L0_conv_qkv_w": _L0_conv_in["qkv_w"],
        "L0_conv_qkv_b": _L0_conv_in["qkv_b"],
        "L0_conv_lepe_w": _L0_conv_in["lepe_w"],
        "L0_conv_lepe_b": _L0_conv_in["lepe_b"],
        "L0_conv_wo_w": _L0_conv_in["wo_w"],
        "L0_conv_wo_b": _L0_conv_in["wo_b"],
        "L0_conv_ln2_g": _L0_conv_in["ln2_g"],
        "L0_conv_ln2_b": _L0_conv_in["ln2_b"],
        "L0_conv_mlp_w1": _L0_conv_in["mlp_w1"],
        "L0_conv_mlp_b1": _L0_conv_in["mlp_b1"],
        "L0_conv_mlp_w2": _L0_conv_in["mlp_w2"],
        "L0_conv_mlp_b2": _L0_conv_in["mlp_b2"],
        "L1_conv_w_tm": _L1_conv_in["w_tm"],
        "L1_conv_b_tm": _L1_conv_in["b_tm"],
        "L1_conv_w_tr": _L1_conv_in["w_tr"],
        "L1_conv_b_tr": _L1_conv_in["b_tr"],
        "L1_conv_w_dcn": _L1_conv_in["w_dcn"],
        "L1_conv_gn_gamma": _L1_conv_in["gn_gamma"],
        "L1_conv_gn_beta": _L1_conv_in["gn_beta"],
        "L2_conv_w1": _L2_conv_in["w1"],
        "L2_conv_b1": _L2_conv_in["b1"],
        "L2_conv_w2": _L2_conv_in["w2"],
        "L2_conv_b2": _L2_conv_in["b2"],
        "L3_conv_w1": _L3_conv_in["w1"],
        "L3_conv_b1": _L3_conv_in["b1"],
        "L3_conv_p1": _L3_conv_in["p1"],
        "L3_conv_pb1": _L3_conv_in["pb1"],
        "L3_conv_w2": _L3_conv_in["w2"],
        "L3_conv_b2": _L3_conv_in["b2"],
        "L3_conv_p2": _L3_conv_in["p2"],
        "L3_conv_pb2": _L3_conv_in["pb2"],
    }

def reference(x, L0_conv_pos_w, L0_conv_pos_b, L0_conv_ln1_g, L0_conv_ln1_b, L0_conv_qkv_w, L0_conv_qkv_b, L0_conv_lepe_w, L0_conv_lepe_b, L0_conv_wo_w, L0_conv_wo_b, L0_conv_ln2_g, L0_conv_ln2_b, L0_conv_mlp_w1, L0_conv_mlp_b1, L0_conv_mlp_w2, L0_conv_mlp_b2, L1_conv_w_tm, L1_conv_b_tm, L1_conv_w_tr, L1_conv_b_tr, L1_conv_w_dcn, L1_conv_gn_gamma, L1_conv_gn_beta, L2_conv_w1, L2_conv_b1, L2_conv_w2, L2_conv_b2, L3_conv_w1, L3_conv_b1, L3_conv_p1, L3_conv_pb1, L3_conv_w2, L3_conv_b2, L3_conv_p2, L3_conv_pb2):
    import jax
    import jax.numpy as jnp
    def _L0_conv_ref(x, pos_w, pos_b, ln1_g, ln1_b, qkv_w, qkv_b, lepe_w, lepe_b, wo_w, wo_b, ln2_g, ln2_b, mlp_w1, mlp_b1, mlp_w2, mlp_b2):
        import jax, jax.numpy as jnp
        import numpy as np
        B, C, H, W = (16, 128, 56, 56)
        QK, HEADS, NWIN, TOPK, MLPR = (128, 4, 7, 4, 3)
        HD_Q, HD_V = (QK // HEADS, C // HEADS)
        WH, WW = (H // NWIN, W // NWIN)
        P2, W2 = (NWIN * NWIN, WH * WW)
        SCALE = QK ** (-0.5)

        def _dwconv(x, w, b):
            y = jax.lax.conv_general_dilated(x, w, (1, 1), 'SAME', feature_group_count=x.shape[1], dimension_numbers=('NCHW', 'OIHW', 'NCHW'))
            return y + b[None, :, None, None]

        def _ln(x, g, b):
            m = x.mean(-1, keepdims=True)
            v = ((x - m) ** 2).mean(-1, keepdims=True)
            return (x - m) * jax.lax.rsqrt(v + 1e-06) * g + b

        def _win(t):
            b, _, _, c = t.shape
            return t.reshape(b, NWIN, WH, NWIN, WW, c).transpose(0, 1, 3, 2, 4, 5).reshape(b, P2, WH, WW, c)

        def _unwin(t):
            b, c = (t.shape[0], t.shape[-1])
            return t.reshape(b, NWIN, NWIN, WH, WW, c).transpose(0, 1, 3, 2, 4, 5).reshape(b, H, W, c)
        x = x + _dwconv(x, pos_w, pos_b)
        xh = x.transpose(0, 2, 3, 1)
        y = _ln(xh, ln1_g, ln1_b)
        qkv = y @ qkv_w + qkv_b
        q, kv = (qkv[..., :QK], qkv[..., QK:])
        qw, kvw = (_win(q), _win(kv))
        q_win = jax.lax.stop_gradient(qw.mean((2, 3)))
        k_win = jax.lax.stop_gradient(kvw[..., :QK].mean((2, 3)))
        logits = jnp.einsum('bpc,bqc->bpq', q_win * SCALE, k_win)
        _, idx = jax.lax.top_k(logits, TOPK)
        kv_pix = kvw.reshape(B, P2, W2, QK + C)
        kv_sel = jax.vmap(lambda t, i: t[i])(kv_pix, idx)
        k_sel = kv_sel[..., :QK].reshape(B, P2, TOPK * W2, HEADS, HD_Q)
        v_sel = kv_sel[..., QK:].reshape(B, P2, TOPK * W2, HEADS, HD_V)
        q_pix = qw.reshape(B, P2, W2, HEADS, HD_Q)
        att = jnp.einsum('bpqhd,bpkhd->bphqk', q_pix * SCALE, k_sel)
        att = jax.nn.softmax(att, axis=-1)
        o = jnp.einsum('bphqk,bpkhd->bpqhd', att, v_sel).reshape(B, P2, W2, C)
        o = _unwin(o)
        v_img = kv[..., QK:].transpose(0, 3, 1, 2)
        lepe = _dwconv(v_img, lepe_w, lepe_b).transpose(0, 2, 3, 1)
        o = (o + lepe) @ wo_w + wo_b
        xh = xh + o
        z = _ln(xh, ln2_g, ln2_b)
        z = jax.nn.gelu(z @ mlp_w1 + mlp_b1, approximate=False) @ mlp_w2 + mlp_b2
        xh = xh + z
        return xh.transpose(0, 3, 1, 2)

    def _L1_conv_ref(x, w_tm, b_tm, w_tr, b_tr, w_dcn, gn_gamma, gn_beta):
        import jax, jax.numpy as jnp
        import numpy as np
        GN_GROUPS = 32
        GN_EPS = 1e-05

        def _conv3x3(x, w, b):
            y = jax.lax.conv_general_dilated(x, w, (1, 1), [(1, 1), (1, 1)], dimension_numbers=('NCHW', 'OIHW', 'NCHW'))
            return y + b[None, :, None, None]

        def _bilinear(x, py, px):
            N, C, H, W = x.shape
            y0 = jnp.floor(py)
            x0 = jnp.floor(px)
            wy = py - y0
            wx = px - x0
            xf = x.reshape(N, C, H * W)
            out = jnp.zeros((N, C, H, W), x.dtype)
            corners = ((y0, x0, (1 - wy) * (1 - wx)), (y0, x0 + 1, (1 - wy) * wx), (y0 + 1, x0, wy * (1 - wx)), (y0 + 1, x0 + 1, wy * wx))
            for yy, xx, w in corners:
                valid = ((yy >= 0) & (yy <= H - 1) & (xx >= 0) & (xx <= W - 1)).astype(x.dtype)
                yi = jnp.clip(yy, 0, H - 1).astype(jnp.int32)
                xi = jnp.clip(xx, 0, W - 1).astype(jnp.int32)
                idx = (yi * W + xi).reshape(N, 1, H * W)
                g = jnp.take_along_axis(xf, idx, axis=2).reshape(N, C, H, W)
                out = out + g * (w * valid)[:, None]
            return out
        N, C, H, W = x.shape
        Cout = w_dcn.shape[0]
        R = jnp.array([[-1.0, -1.0, -1.0, 0.0, 0.0, 0.0, 1.0, 1.0, 1.0], [-1.0, 0.0, 1.0, -1.0, 0.0, 1.0, -1.0, 0.0, 1.0]], x.dtype)
        tm = _conv3x3(x, w_tm, b_tm)
        tr = _conv3x3(x, w_tr, b_tr)
        tmm = tm.transpose(0, 2, 3, 1).reshape(N, H, W, 2, 2)
        off = jnp.einsum('nhwij,jk->nhwik', tmm, R) - R
        dy = off[:, :, :, 0, :] + tr[:, 0][..., None]
        dx = off[:, :, :, 1, :] + tr[:, 1][..., None]
        hh = jnp.arange(H, dtype=x.dtype)[None, :, None, None]
        ww = jnp.arange(W, dtype=x.dtype)[None, None, :, None]
        kk = jnp.arange(9)
        ky = (kk // 3).astype(x.dtype)
        kx = (kk % 3).astype(x.dtype)
        py = hh - 1.0 + ky + dy
        px = ww - 1.0 + kx + dx
        wk = w_dcn.reshape(Cout, C, 9)
        out = jnp.zeros((N, Cout, H, W), x.dtype)
        for k in range(9):
            s = _bilinear(x, py[..., k], px[..., k])
            out = out + jnp.einsum('nchw,oc->nohw', s, wk[:, :, k])
        og = out.reshape(N, GN_GROUPS, Cout // GN_GROUPS * H * W)
        mu = og.mean(axis=2, keepdims=True)
        var = og.var(axis=2, keepdims=True)
        og = (og - mu) * jax.lax.rsqrt(var + GN_EPS)
        out = og.reshape(N, Cout, H, W) * gn_gamma[None, :, None, None] + gn_beta[None, :, None, None]
        return jax.nn.relu(out + x)

    def _L2_conv_ref(x, w1, b1, w2, b2):
        import jax, jax.numpy as jnp
        import numpy as np
        HIDDEN = 128
        NUM_BLOCKS = 8
        BLOCK = HIDDEN // NUM_BLOCKS
        HSF = 1
        LAMBDA = 0.01
        SCALE = 0.02

        def softshrink(v, lam):
            return jnp.sign(v) * jnp.maximum(jnp.abs(v) - lam, 0.0)
        bias = x
        B, C, H, W = x.shape
        xf = jnp.fft.rfft2(x.astype(jnp.float32), axes=(2, 3), norm='ortho')
        Wf = xf.shape[3]
        xb = xf.reshape(B, NUM_BLOCKS, BLOCK, H, Wf)
        xr, xi = (xb.real, xb.imag)
        mm = lambda a, w: jnp.einsum('bkihw,kio->bkohw', a, w)
        o1r = jax.nn.relu(mm(xr, w1[0]) - mm(xi, w1[1]) + b1[0][None, :, :, None, None])
        o1i = jax.nn.relu(mm(xi, w1[0]) + mm(xr, w1[1]) + b1[1][None, :, :, None, None])
        o2r = mm(o1r, w2[0]) - mm(o1i, w2[1]) + b2[0][None, :, :, None, None]
        o2i = mm(o1i, w2[0]) + mm(o1r, w2[1]) + b2[1][None, :, :, None, None]
        sr = softshrink(o2r, LAMBDA)
        si = softshrink(o2i, LAMBDA)
        xc = (sr + 1j * si).reshape(B, C, H, Wf) * xf
        out = jnp.fft.irfft2(xc, s=(H, W), axes=(2, 3), norm='ortho').astype(x.dtype)
        return out + bias

    def _L3_conv_ref(x, w1, b1, p1, pb1, w2, b2, p2, pb2):
        import jax, jax.numpy as jnp
        import numpy as np
        DN = ('NCHW', 'OIHW', 'NCHW')

        def fake_quant(x, bits):
            qmax = float(2 ** (bits - 1) - 1)
            scale = jnp.maximum(jnp.max(jnp.abs(x)) / qmax, 1e-08)
            q = jnp.clip(jnp.round(x / scale), -qmax - 1.0, qmax) * scale
            return x + jax.lax.stop_gradient(q - x)

        def qconv(x, w, b, groups, pad):
            xq = fake_quant(x, 8)
            wq = fake_quant(w, 4)
            y = jax.lax.conv_general_dilated(xq, wq, window_strides=(1, 1), padding=[(pad, pad), (pad, pad)], feature_group_count=groups, dimension_numbers=DN)
            return y + b[None, :, None, None]
        C = x.shape[1]
        y = qconv(x, w1, b1, groups=C, pad=1)
        y = qconv(y, p1, pb1, groups=1, pad=0)
        y = jax.nn.relu(y)
        y = qconv(y, w2, b2, groups=C, pad=1)
        y = qconv(y, p2, pb2, groups=1, pad=0)
        return jax.nn.relu(y) + x

    def _gn(v, G=32, eps=1e-5):
        B_, C_, H_, W_ = v.shape
        g = v.reshape(B_, G, C_ // G, H_, W_)
        m = jnp.mean(g, axis=(2, 3, 4), keepdims=True)
        s = jnp.var(g, axis=(2, 3, 4), keepdims=True)
        return ((g - m) / jnp.sqrt(s + eps)).reshape(v.shape)

    def _ln_c(v, eps=1e-6):
        m = jnp.mean(v, axis=1, keepdims=True)
        s = jnp.var(v, axis=1, keepdims=True)
        return (v - m) / jnp.sqrt(s + eps)

    def _ln_t(v, eps=1e-5):
        m = jnp.mean(v, axis=-1, keepdims=True)
        s = jnp.var(v, axis=-1, keepdims=True)
        return (v - m) / jnp.sqrt(s + eps)

    def _to_tokens(v):
        B_, C_, H_, W_ = v.shape
        return v.reshape(B_, C_, H_ * W_).transpose(0, 2, 1)
    def _from_tokens(t, like):
        B_, C_, H_, W_ = like.shape
        return t.transpose(0, 2, 1).reshape(B_, C_, H_, W_)

    x = _L0_conv_ref(x, L0_conv_pos_w, L0_conv_pos_b, L0_conv_ln1_g, L0_conv_ln1_b, L0_conv_qkv_w, L0_conv_qkv_b, L0_conv_lepe_w, L0_conv_lepe_b, L0_conv_wo_w, L0_conv_wo_b, L0_conv_ln2_g, L0_conv_ln2_b, L0_conv_mlp_w1, L0_conv_mlp_b1, L0_conv_mlp_w2, L0_conv_mlp_b2)
    x = _L1_conv_ref(x, L1_conv_w_tm, L1_conv_b_tm, L1_conv_w_tr, L1_conv_b_tr, L1_conv_w_dcn, L1_conv_gn_gamma, L1_conv_gn_beta)
    x = _L2_conv_ref(x, L2_conv_w1, L2_conv_b1, L2_conv_w2, L2_conv_b2)
    x = _L3_conv_ref(x, L3_conv_w1, L3_conv_b1, L3_conv_p1, L3_conv_pb1, L3_conv_w2, L3_conv_b2, L3_conv_p2, L3_conv_pb2)
    return x


_drawn_inputs = setup_inputs


def setup_inputs(seed=0):
    import zlib

    import numpy as np

    out = dict(_drawn_inputs(seed))
    spreads = {'L0_conv_pos_b': (0.0, 0.1),
     'L0_conv_ln1_g': (1.0, 0.6),
     'L0_conv_ln1_b': (0.0, 0.333),
     'L0_conv_qkv_b': (0.0, 0.1),
     'L0_conv_lepe_b': (0.0, 0.1),
     'L0_conv_wo_b': (0.0, 0.1),
     'L0_conv_ln2_g': (1.0, 0.2),
     'L0_conv_ln2_b': (0.0, 0.335),
     'L0_conv_mlp_b1': (0.0, 0.1),
     'L0_conv_mlp_b2': (0.0, 0.1),
     'L1_conv_gn_gamma': (1.0, 0.2),
     'L1_conv_gn_beta': (0.0, 0.1)}
    factors = {'L2_conv_b1': 32.468, 'L2_conv_b2': 3.152, 'L3_conv_b1': 3.81, 'L3_conv_pb1': 7.801}
    for name, (base, spread) in spreads.items():
        noise = np.random.default_rng([zlib.crc32(name.encode()), seed]).standard_normal(out[name].shape)
        drawn = base * np.exp(spread * noise) if base else spread * noise
        out[name] = jnp.asarray(drawn.astype(out[name].dtype))
    for name, factor in factors.items():
        out[name] = (out[name] * factor).astype(out[name].dtype)
    return out
```

```python
from contextlib import ExitStack, contextmanager

import concourse.bass as bass
from concourse import mybir

F32 = mybir.dt.float32
BF16 = mybir.dt.bfloat16
I32 = mybir.dt.int32
I16 = mybir.dt.int16
U32 = mybir.dt.uint32
ALU = mybir.AluOpType
ACT = mybir.ActivationFunctionType
AX = mybir.AxisListType

C = 128
H = W = 56
HW = H * W
HP = H + 2
CH_ROWS = 8
NCK = H // CH_ROWS
CPX = CH_ROWS * W
TPX = 2 * W
TILES = CPX // TPX
TW = W + 1
TROWS = TW * TW
ROUND = 12582912.0
GN_EPS = 1e-5
START = 8


def at(i):
    return START + i


@contextmanager
def cleared_semaphore(nc, name):
    handle = nc.alloc_semaphore(name=name)
    yield handle
    nc.clear_and_free_semaphores([handle])


def spread_phase(nc, B, x_img, ident_d, windows, table):
    with ExitStack() as ctx:
        sb = lambda name, shape, dt=F32: ctx.enter_context(nc.sbuf_tensor(name, shape, dt))
        ps = lambda name, shape, dt=F32: ctx.enter_context(nc.psum_tensor(name, shape, dt))
        sem = lambda name: ctx.enter_context(nc.semaphore(name))
        ident = sb("sp_ident", [C, C])
        flat = sb("sp_flat", [C, 2, HW])
        padded = sb("sp_padded", [C, 2, HP, HP])
        turned = sb("sp_turned", [TPX, 2, HW // TPX, C])
        zeros = sb("sp_zeros", [B, TW, 2 * C])
        bank = [ps(f"sp_bank{k}", [TPX, 4, C]) for k in range(4)]
        s_const, s_zero, s_bank, s_turned, s_padded, s_edge, s_bfree = map(
            sem, ["sp_const", "sp_zero", "sp_bank", "sp_turned", "sp_padded", "sp_edge", "sp_bfree"])
        s_loaded, s_table, s_win = ([sem(f"sp_{n}{j}") for j in range(2)] for n in ("loaded", "table", "win"))
        GROUPS = HW // TPX // 4
        tab = table.rearrange("(b y x) (k c) -> b y x k c", b=B, y=TW, k=4)
        block = ctx.enter_context(nc.Block())

        @block.sync
        def _(sp):
            sp.dma_start(ident[:], ident_d).then_inc(s_const, 16)
            with sp.Fori(0, B // 2) as pair:
                b = pair * 2
                for j in range(2):
                    sp.wait_ge(s_turned, at(b + j - 1))
                    sp.wait_ge(s_padded, at(b + j - 1))
                    sp.dma_start(flat[:, j, :], x_img[bass.ds(b + j, 1)].rearrange("o c n -> (o c) n")).then_inc(s_loaded[j], 16)

        @block.tensor
        def _(pe):
            pe.wait_ge(s_const, 16)
            with pe.Fori(0, B // 2) as pair:
                b = pair * 2
                for j in range(2):
                    pe.wait_ge(s_loaded[j], 16 * pair + 16)
                    for g in range(GROUPS):
                        pe.wait_ge(s_bfree, (b + j) * GROUPS + g + 1)
                        for k in range(4):
                            t = 4 * g + k
                            last = pe.transpose(bank[(j * GROUPS + g) % 2][:, k, :], flat[:, j, t * TPX:(t + 1) * TPX], ident[:])
                        last.then_inc(s_bank, 1)

        @block.vector
        def _(dve):
            dve.sem_inc(s_bfree, 2)
            dve.sem_inc(s_turned, START)
            with dve.Fori(0, B // 2) as pair:
                b = pair * 2
                for j in range(2):
                    dve.wait_ge(s_table[j], at(128 * pair))
                    for g in range(GROUPS):
                        dve.wait_ge(s_bank, (b + j) * GROUPS + g + 1)
                        last = dve.tensor_copy(turned[:, j, 4 * g:4 * g + 4, :], bank[(j * GROUPS + g) % 2][:])
                        last.then_inc(s_bfree, 1)
                    dve.wait_ge(s_bfree, 2 + (b + j + 1) * GROUPS)
                    dve.sem_inc(s_turned, 1)

        @block.scalar
        def _(act):
            act.wait_ge(s_zero, 2)
            act.sem_inc(s_padded, START)
            for j in range(2):
                act.sem_inc(s_win[j], START)
                act.sem_inc(s_table[j], START)
            with act.Fori(0, B // 2) as pair:
                b = pair * 2
                for j in range(2):
                    act.wait_ge(s_loaded[j], 16 * pair + 16)
                    act.wait_ge(s_win[j], at(16 * NCK * pair))
                    act.activation(padded[:, j, 1:H + 1, 1:W + 1],
                                   flat[:, j, :].rearrange("c (h w) -> c h w", w=W), ACT.Copy).then_inc(s_padded, 1)
                    act.wait_ge(s_padded, at(b + j + 1))
                    for c in range(NCK):
                        act.dma_start(windows[bass.ds((b + j) * NCK + c, 1)].rearrange("o c n -> (o c) n"),
                                      padded[:, j, CH_ROWS * c:CH_ROWS * c + 10, :].rearrange("c h w -> c (h w)")).then_inc(s_win[j], 16)
                    act.wait_ge(s_turned, at(b + j + 1))
                    for dy in range(2):
                        for dx in range(2):
                            for r in range(2):
                                rows = tab[bass.ds(b + j, 1), r + 1 - dy:r + 1 - dy + H - 1:2, 1 - dx:1 - dx + W, 2 * dy + dx, :]
                                act.dma_start(rows.rearrange("o y x c -> x (o y) c"),
                                               turned[r * W:(r + 1) * W, j, :, :]).then_inc(s_table[j], 16)
            for j in range(2):
                act.wait_ge(s_win[j], at(16 * NCK * B // 2))
                act.wait_ge(s_table[j], at(128 * B // 2))

        @block.gpsimd
        def _(pool):
            pool.memset(zeros[:], 0.0).then_inc(s_zero, 1)
            pool.memset(padded[:], 0.0).then_inc(s_zero, 1)
            pool.wait_ge(s_zero, 2)
            for y, x, k in ((0, slice(0, TW), slice(0, 2)), (H, slice(0, TW), slice(2, 4))):
                pool.dma_start(tab[:, y, x, k, :].rearrange("b x k c -> b x (k c)"), zeros[:, :, :]).then_inc(s_edge, 16)
            for x, k, y0 in ((0, 0, 1), (0, 2, 0), (W, 1, 1), (W, 3, 0)):
                pool.dma_start(tab[:, y0:y0 + H, x, k, :], zeros[:, 0:H, 0:C]).then_inc(s_edge, 16)
            pool.wait_ge(s_edge, 96)


def deform_phase(nc, N, windows, table, base_d, ident_d, woff_d, boff_d, wdcn_d, conv_out):
    with ExitStack() as ctx:
        sb = lambda name, shape, dt=F32: ctx.enter_context(nc.sbuf_tensor(name, shape, dt))
        ps = lambda name, shape, dt=F32: ctx.enter_context(nc.psum_tensor(name, shape, dt))
        sem = lambda name: ctx.enter_context(nc.semaphore(name))
        ident = sb("df_ident", [C, C])
        woff = sb("df_woff", [C, 9, 6])
        boff = sb("df_boff", [TPX, 6])
        wdcn = sb("df_wdcn", [C, 9, C])
        win = sb("df_win", [C, CH_ROWS + 2, HP])
        shifted = sb("df_shifted", [C, 3, (CH_ROWS + 2) * W])
        base = sb("df_base", [TPX, 9])
        off = sb("df_off", [TPX, 3, TILES, 2])
        ctr = sb("df_ctr", [TPX, TILES, 2])
        row = sb("df_row", [TPX, 3, TILES, 2])
        pos = sb("df_pos", [TPX, 3, 3, TILES, 2])
        cell = sb("df_cell", [TPX, 9, TILES, 2])
        frac = sb("df_frac", [TPX, 9, TILES, 2])
        rest = sb("df_rest", [TPX, 9, TILES, 2])
        lin = sb("df_lin", [TPX, 9, TILES])
        idx_next = sb("df_idx_next", [TPX, TILES, 9], I32)
        wt_next = sb("df_wt_next", [TPX, TILES, 9, 4])
        idx = sb("df_idx", [TPX, TILES, 9], I32)
        wt = sb("df_wt", [TPX, TILES, 9, 4])
        got = sb("df_got", [TPX, TILES, 9, 4 * C])
        diag = sb("df_diag", [TPX, 2, 9, 4, TPX])
        samp = sb("df_samp", [C, 9, CPX])
        yout = sb("df_yout", [C, 2, CPX])
        p_off = ps("df_p_off", [TPX, TILES, 3, 2])
        p_samp = [ps(f"df_p_samp{k}", [C, 3, TPX]) for k in range(3)]
        p_conv = ps("df_p_conv", [C, CPX])
        s_const, s_win, s_offs, s_prep, s_idx, s_diag = map(sem, ["df_const", "df_win_in", "df_offs", "df_prep", "df_idx_ready", "df_diag_ready"])
        s_got = [sem(f"df_got{t}") for t in range(TILES)]
        s_tile, s_sampled, s_copied, s_conv, s_y, s_stored, s_chain, s_shift, s_issue = map(
            sem, ["df_tile_done", "df_sampled", "df_copied", "df_conv_done", "df_y", "df_stored", "df_chain", "df_shift", "df_issue"])
        PREP = 19
        block = ctx.enter_context(nc.Block())

        @block.sync
        def _(sp):
            sp.dma_start(ident[:], ident_d).then_inc(s_const, 16)
            sp.dma_start(woff[:], woff_d).then_inc(s_const, 16)
            sp.dma_start(boff[:], boff_d).then_inc(s_const, 16)
            sp.dma_start(wdcn[:], wdcn_d).then_inc(s_const, 16)

            def load(i):
                sp.dma_start(win[:].rearrange("c h w -> c (h w)"), windows[bass.ds(i, 1)].rearrange("o c n -> (o c) n")).then_inc(s_win, 16)
                sp.dma_start(base[:], base_d[bass.ds(i, 1)].rearrange("o p n -> (o p) n")).then_inc(s_win, 16)

            load(0)
            with sp.Fori(0, N - 1) as i:
                sp.wait_ge(s_prep, at(i + 1))
                sp.wait_ge(s_shift, 3 * i + 3)
                load(i + 1)

        @block.tensor
        def _(pe):
            pe.sem_inc(s_tile, TILES)
            pe.sem_inc(s_offs, START)
            pe.sem_inc(s_conv, START)
            pe.wait_ge(s_const, 64)

            def offsets(i):
                pe.wait_ge(s_shift, 3 * i + 3)
                pe.wait_ge(s_prep, at(i))
                for t in range(TILES):
                    for k in range(9):
                        dy, dx = k // 3, k % 3
                        last = pe.matmul(p_off[:, t, :, :].rearrange("p a b -> p (a b)"),
                                         shifted[:, dx, (2 * t + dy) * W:(2 * t + dy + 2) * W], woff[:, k, :],
                                         start=(k == 0), stop=(k == 8))
                last.then_inc(s_offs, 1)

            def tiles(i):
                for t in range(TILES):
                    pe.wait_ge(s_got[t], 144 * i + 144)
                    pe.wait_ge(s_diag, TILES * i + t + 1)
                    for g in range(3):
                        pe.wait_ge(s_copied, 12 * i + 3 * t + g + 1)
                        for k in range(3):
                            for c in range(4):
                                last = pe.matmul(p_samp[g][:, k, :], got[:, t, 3 * g + k, c * C:(c + 1) * C],
                                                 diag[:, t % 2, 3 * g + k, c, :], start=(c == 0), stop=(c == 3))
                        last.then_inc(s_sampled, 1)
                    pe.wait_ge(s_sampled, 12 * i + 3 * t + 3)
                    pe.sem_inc(s_tile, 1)

            def conv(i):
                pe.wait_ge(s_copied, 3 + 12 * i + 12)
                pe.wait_ge(s_y, at(i))
                for k in range(9):
                    last = pe.matmul(p_conv[:], wdcn[:, k, :], samp[:, k, :], start=(k == 0), stop=(k == 8))
                last.then_inc(s_conv, 1)

            offsets(0)
            with pe.Fori(0, N - 1) as i:
                offsets(i + 1)
                tiles(i)
                conv(i)
            tiles(N - 1)
            conv(N - 1)

        @block.vector
        def _(dve):
            dve.wait_ge(s_const, 64)
            dve.sem_inc(s_prep, START)

            def prepare(i):
                n = [0]

                def step(instruction):
                    n[0] += 1
                    instruction.then_inc(s_chain, 1)
                    dve.wait_ge(s_chain, PREP * i + n[0])

                dve.wait_ge(s_offs, at(i + 1))
                dve.wait_ge(s_win, 32 * i + 32)
                step(dve.tensor_tensor(off[:].rearrange("p k t j -> p t k j"), p_off[:],
                                       boff[:].rearrange("p (k j) -> p k j", j=2).unsqueeze(1).to_broadcast([TPX, TILES, 3, 2]), ALU.add))
                step(dve.tensor_tensor(ctr[:], off[:, 2], base[:, 0:8].rearrange("p (t j) -> p t j", j=2), ALU.add))
                step(dve.tensor_tensor(row[:, 0], ctr[:], off[:, 0], ALU.subtract))
                step(dve.tensor_copy(row[:, 1], ctr[:]))
                step(dve.tensor_tensor(row[:, 2], ctr[:], off[:, 0], ALU.add))
                rows = row[:].rearrange("p k t j -> p k (t j)")
                side = off[:, 1].rearrange("p t j -> p (t j)").unsqueeze(1).to_broadcast([TPX, 3, 2 * TILES])
                for kx, op in ((0, ALU.subtract), (2, ALU.add)):
                    step(dve.tensor_tensor(pos[:, :, kx].rearrange("p k t j -> p k (t j)"), rows, side, op))
                step(dve.tensor_copy(pos[:, :, 1].rearrange("p k t j -> p k (t j)"), rows))
                flat = lambda a: a.rearrange("p a t j -> p (a t j)")
                p = pos[:].rearrange("p a b t j -> p (a b t j)")
                step(dve.tensor_scalar(p, p, 0.0, float(W + 1), ALU.max, ALU.min))
                step(dve.tensor_scalar(flat(cell[:]), p, 0.5, 0.0, ALU.subtract, ALU.max))
                step(dve.tensor_scalar(flat(cell[:]), flat(cell[:]), ROUND, ROUND, ALU.add, ALU.subtract))
                step(dve.tensor_tensor(flat(frac[:]), p, flat(cell[:]), ALU.subtract))
                step(dve.tensor_scalar(flat(rest[:]), flat(frac[:]), -1.0, 1.0, ALU.mult, ALU.add))
                step(dve.scalar_tensor_tensor(out=lin[:], in0=cell[:, :, :, 0], scalar=float(TW), in1=cell[:, :, :, 1], op0=ALU.mult, op1=ALU.add))
                step(dve.tensor_scalar(idx_next[:].rearrange("p t k -> p k t"), lin[:], base[:, 8:9], None, ALU.add))
                for c, (a, b) in enumerate(((rest, rest), (rest, frac), (frac, rest), (frac, frac))):
                    step(dve.tensor_tensor(wt_next[:, :, :, c].rearrange("p t k -> p k t"), a[:, :, :, 0], b[:, :, :, 1], ALU.mult))
                assert n[0] == PREP
                dve.sem_inc(s_prep, 1)

            def publish(i, t):
                dve.tensor_copy(idx[:, t, :], idx_next[:, t, :]).then_inc(s_idx, 1)
                dve.tensor_copy(wt[:, t], wt_next[:, t]).then_inc(s_idx, 1)

            def diagonals(i, t):
                dve.wait_ge(s_idx, 2 * (TILES * i + t) + 2)
                dve.wait_ge(s_tile, TILES * i + t + 3)
                for k in range(9):
                    for c in range(4):
                        last = dve.tensor_scalar(diag[:, t % 2, k, c, :], ident[0:TPX, 0:TPX], wt[:, t, k, c:c + 1], None, ALU.mult)
                last.then_inc(s_diag, 1)

            prepare(0)
            for t in range(TILES):
                publish(0, t)
            with dve.Fori(0, N - 1) as i:
                for t in range(TILES):
                    diagonals(i, t)
                    if t == 0:
                        prepare(i + 1)
                    else:
                        dve.wait_ge(s_got[t - 1], 144 * i + 144)
                        dve.wait_ge(s_diag, TILES * i + t)
                        publish(i + 1, t - 1)
                dve.wait_ge(s_got[TILES - 1], 144 * i + 144)
                dve.wait_ge(s_diag, TILES * i + TILES)
                publish(i + 1, TILES - 1)
            for t in range(TILES):
                diagonals(N - 1, t)

        @block.gpsimd
        def _(pool):
            with pool.Fori(0, N) as i:
                for t in range(TILES):
                    pool.wait_ge(s_idx, 2 * (TILES * i + t) + 1)
                    pool.wait_ge(s_tile, TILES * i + t + 1)
                    pool.sem_inc(s_issue, 1)
                    for k in range(9):
                        pool.indirect_dma_start(out=got[:, t, k, :], out_offset=None, in_=table[:, :],
                                                in_offset=bass.IndirectOffsetOnAxis(ap=idx[:, t, k:k + 1], axis=0)).then_inc(s_got[t], 16)

        @block.scalar
        def _(act):
            act.sem_inc(s_copied, 3)
            act.sem_inc(s_y, START)
            act.sem_inc(s_stored, START)

            def shift(i):
                act.wait_ge(s_win, 32 * i + 32)
                act.wait_ge(s_offs, at(i))
                for dx in range(3):
                    act.activation(shifted[:, dx, :].rearrange("c (h w) -> c h w", w=W), win[:, :, dx:dx + W], ACT.Copy).then_inc(s_shift, 1)

            def chunk(i, par):
                for t in range(TILES):
                    for g in range(3):
                        act.wait_ge(s_sampled, 12 * i + 3 * t + g + 1)
                        if t == 0 and g == 0:
                            act.wait_ge(s_conv, at(i))
                        act.activation(samp[:, 3 * g:3 * g + 3, t * TPX:(t + 1) * TPX], p_samp[g][:], ACT.Copy).then_inc(s_copied, 1)
                act.wait_ge(s_conv, at(i + 1))
                act.wait_ge(s_stored, at(16 * i))
                act.activation(yout[:, par, :], p_conv[:], ACT.Copy).then_inc(s_y, 1)
                act.wait_ge(s_y, at(i + 1))
                act.dma_start(conv_out[bass.ds(i, 1)].rearrange("o c n -> (o c) n"), yout[:, par, :]).then_inc(s_stored, 16)

            shift(0)
            with act.Fori(0, N - 1) as i:
                shift(i + 1)
                chunk(i, 0)
            chunk(N - 1, 0)
            act.wait_ge(s_stored, at(16 * N))


def chunk_bases(B):
    import numpy as np
    base = np.zeros((B * NCK, TPX, 9), np.float32)
    p = np.arange(TPX)
    for i in range(B * NCK):
        b, c = divmod(i, NCK)
        for t in range(TILES):
            base[i, :, 2 * t] = CH_ROWS * c + 2 * t + p // W + 1
            base[i, :, 2 * t + 1] = p % W + 1
        base[i, :, 8] = b * TROWS
    return base
WIN = 8
NWIN = H // WIN
NW = NWIN * NWIN
WPX = WIN * WIN
HEADS = 4
HD = C // HEADS
TOPK = 4
HID = 3
LN_EPS = 1e-6
QSCALE = float(C) ** -0.5


def attention_phase(nc, B, x_d, w, out_img):
    with ExitStack() as ctx:
        ctx.callback(nc.all_engine_barrier)
        sb = lambda name, shape, dt=F32: ctx.enter_context(nc.sbuf_tensor("at_" + name, shape, dt))
        ps = lambda name, shape, dt=F32: ctx.enter_context(nc.psum_tensor("at_" + name, shape, dt))
        sem = lambda name: ctx.enter_context(cleared_semaphore(nc, "at_" + name))
        ident = sb("ident", [C, C])
        mean_of = sb("mean_of", [C, C])
        vec = sb("vec", [C, len(VEC0)])
        taps3 = sb("taps3", [C, 9])
        taps5 = sb("taps5", [C, 25])
        diag3 = sb("diag3", [C, 9, C])
        diag5 = sb("diag5", [C, 25, C])
        wqkv = sb("wqkv", [C, 3 * C])
        wo = sb("wo", [C, C])
        w1 = sb("w1", [C, HID * C])
        w2 = sb("w2", [C, HID, C])
        eps = sb("eps", [C, 1])
        flat = sb("flat", [C, HW])
        padded = sb("padded", [C, HP, HP])
        x1 = sb("x1", [C, HW])
        dev = sb("dev", [C, HW])
        y = sb("y", [C, NW, WPX])
        kv = sb("kv", [C, NW, 2, WPX])
        vpad = sb("vpad", [C, H + 4, W + 4])
        oimg = sb("oimg", [C, HW])
        sq = sb("sq", [C, 2, CPX])
        std = sb("std", [C, 2, CPX])
        ysum = sb("ysum", [C, NW])
        qm = sb("qm", [C, NW])
        km = sb("km", [C, NW])
        logit = sb("logit", [NW, NW])
        top = sb("top", [NW, 8])
        top_at = sb("top_at", [NW, 8], U32)
        chosen = sb("chosen", [1, NW * TOPK], U32)
        qz = sb("qz", [C, NWIN, HEADS, WPX])
        kvsel = sb("kvsel", [C, 2, 2, TOPK, WPX])
        prob = sb("prob", [C, 2, 2, TOPK * WPX])
        probT = sb("probT", [C, 2, 4, C])
        vT = sb("vT", [C, 2, 2, C])
        nmax = sb("nmax", [C, 2, 2])
        tot = sb("tot", [C, 2, 2])
        inv = sb("inv", [C, 2, 2])
        orow = sb("orow", [C, WIN, W])
        hid = sb("hid", [C, 2, HID, CPX])
        bank = [ps(f"bank{k}", [C, 512]) for k in range(8)]

        names = ("const zero diag load padfree pad conv x1 mean dev sq var std rs rn y kv kcopy vcopy vpad ysum qkm qkmc logit lcopy "
                 "top topidx issue sel q qz s vt vtc nb exp rec pn pt ptc pv oc lepe orow osum wo x2 mean2 dev2 sq2 var2 std2 rs2 rn2 z "
                 "m1 gelu m2 fin stored chosen").split()
        S = {n: sem(n) for n in names}
        block = ctx.enter_context(nc.Block())

        def before(w):
            return {0: 1, 1: 3}.get(w, 2)

        def ck(c):
            return slice(c * CPX, (c + 1) * CPX)

        V = {n: vec[:, k:k + 1] for k, n in enumerate(VEC0)}

        @block.sync
        def _(sp):
            for dst, src in ((ident, w["ident"]), (mean_of, w["mean_of"]), (vec, w["vec0"]), (taps3, w["taps3"]), (taps5, w["taps5"]),
                             (wqkv, w["wqkv"]), (wo, w["wo"]), (w1, w["w1"]), (w2, w["w2"])):
                sp.dma_start(dst[:], src).then_inc(S["const"], 16)
            with sp.Fori(0, B) as b:
                sp.wait_ge(S["padfree"], at(b))
                sp.dma_start(flat[:], x_d[bass.ds(b, 1)].rearrange("o c n -> (o c) n")).then_inc(S["load"], 16)
                sp.wait_ge(S["topidx"], at(b + 1))
                sp.dma_start(chosen[:].rearrange("o (w k) -> o w k", k=TOPK), top_at[:, 0:TOPK]).then_inc(S["chosen"], 16)
                sp.wait_ge(S["fin"], at(NCK * (b + 1)))
                sp.dma_start(out_img[bass.ds(b, 1)].rearrange("o c n -> (o c) n"), oimg[:]).then_inc(S["stored"], 16)
            sp.wait_ge(S["stored"], 16 * B + START)

        @block.gpsimd
        def _(pool):
            pool.memset(vpad[:], 0.0).then_inc(S["zero"], 1)
            pool.memset(padded[:], 0.0).then_inc(S["zero"], 1)
            pool.memset(qz[:], 0.0).then_inc(S["zero"], 1)
            pool.memset(eps[:], LN_EPS).then_inc(S["zero"], 1)
            pool.sem_inc(S["sel"], START)
            pool.sem_inc(S["stored"], START)
            with pool.Fori(0, B) as b:
                pool.wait_ge(S["chosen"], 16 * b + 16)
                pool.wait_ge(S["vcopy"], at(NCK * (b + 1)))
                pool.sem_inc(S["issue"], 1)
                with pool.Fori(0, NWIN) as r:
                    for v in range(NWIN):
                        n = b * NW + r * NWIN + v
                        pool.wait_ge(S["vt"], at(n - before(v) + 1))
                        pool.sem_inc(S["issue"], 1)
                        for k in range(TOPK):
                            src = pool.value_load(chosen[0:1, bass.ds(r * (NWIN * TOPK) + (v * TOPK + k), 1)], min_val=0, max_val=NW - 1)
                            last = pool.tensor_copy(kvsel[:, v % 2, :, k, :], kv[:, bass.ds(src, 1), :, :].rearrange("c o t p -> c (o t) p"))
                        last.then_inc(S["sel"], 1)

        @block.tensor
        def _(pe):
            for n in ("conv mean var kv qkm logit q s vt pt pv lepe wo mean2 var2 m1 m2".split()):
                pe.sem_inc(S[n], START)
            pe.wait_ge(S["diag"], 34)
            pe.wait_ge(S["const"], 144)

            def conv(b, c):
                if c >= 2:
                    pe.wait_ge(S["x1"], at(NCK * b + c - 1))
                for k in range(9):
                    last = pe.matmul(bank[c % 2][:, 0:CPX], diag3[:, k, :],
                                     padded[:, WIN * c + k // 3:WIN * c + k // 3 + WIN, k % 3:k % 3 + W], start=(k == 0), stop=(k == 8))
                last.then_inc(S["conv"], 1)

            def mean(b, c):
                pe.wait_ge(S["x1"], at(NCK * b + c + 1))
                if c >= 2:
                    pe.wait_ge(S["dev"], at(NCK * b + c - 1))
                pe.matmul(bank[2 + c % 2][:, 0:CPX], mean_of[:], x1[:, ck(c)], start=True, stop=True).then_inc(S["mean"], 1)

            def var(b, c):
                pe.wait_ge(S["sq"], at(NCK * b + c + 1))
                if c >= 2:
                    pe.wait_ge(S["std"], at(NCK * b + c - 1))
                pe.matmul(bank[4 + c % 2][:, 0:CPX], mean_of[:], sq[:, c % 2, :], start=True, stop=True).then_inc(S["var"], 1)

            def keys_values(b, c):
                pe.wait_ge(S["y"], at(NCK * b + c + 1))
                if c >= 1:
                    pe.wait_ge(S["vcopy"], at(NCK * b + c))
                    pe.wait_ge(S["vpad"], at(NCK * b + c))
                for t in range(2):
                    last = pe.matmul(bank[6 + t][:, 0:CPX], wqkv[:, (1 + t) * C:(2 + t) * C],
                                     y[:, NWIN * c:NWIN * (c + 1), :], start=True, stop=True)
                last.then_inc(S["kv"], 1)

            def choose(b):
                pe.wait_ge(S["ysum"], at(b + 1))
                for t in range(2):
                    last = pe.matmul(bank[t][:, 0:NW], wqkv[:, t * C:(t + 1) * C], ysum[:], start=True, stop=True)
                last.then_inc(S["qkm"], 1)
                pe.wait_ge(S["qkmc"], at(2 * b + 2))
                pe.matmul(bank[2][0:NW, 0:NW], qm[:], km[:], start=True, stop=True).then_inc(S["logit"], 1)

            def scores(b, r, v):
                n = b * NW + r * NWIN + v
                pe.wait_ge(S["sel"], at(n + 1))
                pe.wait_ge(S["exp"], at(n - before(v) + 1))
                for g in range(2):
                    last = pe.matmul(bank[1 + v % 2][:, g * 256:(g + 1) * 256], qz[:, v, 2 * g:2 * g + 2, :].rearrange("c h p -> c (h p)"),
                                     kvsel[:, v % 2, 0, :, :].rearrange("c k p -> c (k p)"), start=True, stop=True)
                last.then_inc(S["s"], 1)
                pe.wait_ge(S["vtc"], at(n))
                for g in range(2):
                    last = pe.transpose(bank[3][:, g * C:(g + 1) * C],
                                        kvsel[:, v % 2, 1, 2 * g:2 * g + 2, :].rearrange("c k p -> c (k p)"), ident[:])
                last.then_inc(S["vt"], 1)

            def turn_probs(b, r, v):
                n = b * NW + r * NWIN + v
                pe.wait_ge(S["pn"], at(n + 1))
                pe.wait_ge(S["ptc"], at(n - before(v) + 1))
                for kh in range(2):
                    for g in range(2):
                        last = pe.transpose(bank[4 + v % 2][:, (2 * kh + g) * C:(2 * kh + g + 1) * C],
                                            prob[:, v % 2, g, kh * C:(kh + 1) * C], ident[:])
                last.then_inc(S["pt"], 1)

            def weigh_values(b, r, v):
                n = b * NW + r * NWIN + v
                pe.wait_ge(S["ptc"], at(n + 1))
                pe.wait_ge(S["vtc"], at(n + 1))
                pe.wait_ge(S["oc"], at(n))
                for kh in range(2):
                    last = pe.matmul(bank[6][:, 0:256], vT[:, v % 2, kh, :],
                                     probT[:, v % 2, 2 * kh:2 * kh + 2, :].rearrange("c g p -> c (g p)"), start=(kh == 0), stop=(kh == 1))
                last.then_inc(S["pv"], 1)

            def lepe(b, r, k):
                if k == 0:
                    pe.wait_ge(S["osum"], at(NCK * b + r))
                mm = pe.matmul(bank[7][:, 0:CPX], diag5[:, k, :], vpad[:, bass.ds(r * WIN + k // 5, WIN), k % 5:k % 5 + W],
                               start=(k == 0), stop=(k == 24))
                if k == 24:
                    mm.then_inc(S["lepe"], 1)

            def out_proj(b, c):
                if c >= 2:
                    pe.wait_ge(S["x2"], at(NCK * b + c - 1))
                pe.matmul(bank[c % 2][:, 0:CPX], wo[:], oimg[:, ck(c)], start=True, stop=True).then_inc(S["wo"], 1)

            def mean2(b, c):
                pe.wait_ge(S["x2"], at(NCK * b + c + 1))
                if c >= 1:
                    pe.wait_ge(S["dev2"], at(NCK * b + c))
                pe.matmul(bank[2][:, 0:CPX], mean_of[:], dev[:, ck(c)], start=True, stop=True).then_inc(S["mean2"], 1)

            def var2(b, c):
                pe.wait_ge(S["sq2"], at(NCK * b + c + 1))
                if c >= 2:
                    pe.wait_ge(S["std2"], at(NCK * b + c - 1))
                pe.matmul(bank[3 + c % 2][:, 0:CPX], mean_of[:], sq[:, c % 2, :], start=True, stop=True).then_inc(S["var2"], 1)

            z = y[:].rearrange("c w p -> c (w p)")

            def mlp_in(b, c):
                if c >= 1:
                    pe.wait_ge(S["gelu"], at(NCK * b + c))
                for j in range(HID):
                    last = pe.matmul(bank[4 + j][:, 0:CPX], w1[:, j * C:(j + 1) * C], z[:, ck(c)], start=True, stop=True)
                last.then_inc(S["m1"], 1)

            def mlp_out(b, c):
                pe.wait_ge(S["gelu"], at(NCK * b + c + 1))
                if c >= 2:
                    pe.wait_ge(S["fin"], at(NCK * b + c - 1))
                for j in range(HID):
                    last = pe.matmul(bank[7 if c % 2 else 0][:, 0:CPX], w2[:, j, :], hid[:, c % 2, j, :], start=(j == 0), stop=(j == HID - 1))
                last.then_inc(S["m2"], 1)

            with pe.Fori(0, B) as b:
                pe.wait_ge(S["pad"], b + 1)
                pe.wait_ge(S["fin"], at(NCK * b))
                for c in range(NCK + 3):
                    if c < NCK:
                        conv(b, c)
                    if 1 <= c <= NCK:
                        mean(b, c - 1)
                    if 2 <= c <= NCK + 1:
                        var(b, c - 2)
                    if c >= 3:
                        keys_values(b, c - 3)
                choose(b)
                pe.wait_ge(S["vcopy"], at(NCK * (b + 1)))
                pe.wait_ge(S["vpad"], at(NCK * (b + 1)))
                pe.sem_inc(S["issue"], 1)
                with pe.Fori(0, NWIN) as r:
                    pe.wait_ge(S["qz"], at(NCK * b + r))
                    pe.matmul(bank[0][:, 0:CPX], wqkv[:, 0:C],
                              y[:, bass.ds(r * NWIN, NWIN), :], start=True, stop=True).then_inc(S["q"], 1)
                    pe.wait_ge(S["qz"], at(NCK * b + r + 1))
                    tap = 0
                    for v in range(NWIN + 2):
                        if v < NWIN:
                            scores(b, r, v)
                        while tap < min(25, 3 * (v + 1)):
                            lepe(b, r, tap)
                            tap += 1
                        if 1 <= v <= NWIN:
                            turn_probs(b, r, v - 1)
                        if v >= 2:
                            weigh_values(b, r, v - 2)
                pe.wait_ge(S["osum"], at(NCK * (b + 1)))
                for c in range(NCK + 2):
                    if c < NCK:
                        out_proj(b, c)
                    if 1 <= c <= NCK:
                        mean2(b, c - 1)
                    if c >= 2:
                        var2(b, c - 2)
                pe.wait_ge(S["z"], at(NCK * (b + 1)))
                for c in range(NCK + 1):
                    if c < NCK:
                        mlp_in(b, c)
                    if c >= 1:
                        mlp_out(b, c - 1)

        @block.vector
        def _(dve):
            for n in ("x1 dev rs rn y vpad ysum qkmc lcopy top topidx qz vtc nb rec pn oc orow osum x2 dev2 rs2 rn2 z fin".split()):
                dve.sem_inc(S[n], START)
            dve.wait_ge(S["const"], 144)
            for k in range(9):
                dve.tensor_scalar(diag3[:, k, :], ident[:], taps3[:, k:k + 1], None, ALU.mult).then_inc(S["diag"], 1)
            for k in range(25):
                dve.tensor_scalar(diag5[:, k, :], ident[:], taps5[:, k:k + 1], None, ALU.mult).then_inc(S["diag"], 1)
            dve.wait_ge(S["zero"], 4)

            rows = lambda a, c: a[:, ck(c)].rearrange("c (h w) -> c h w", w=W)
            z = y[:].rearrange("c w p -> c (w p)")

            def residual(b, c):
                dve.wait_ge(S["conv"], at(NCK * b + c + 1))
                dve.scalar_tensor_tensor(out=rows(x1, c), in0=bank[c % 2][:, 0:CPX].rearrange("c (h w) -> c h w", w=W), scalar=V["pos_b"],
                                         in1=padded[:, WIN * c + 1:WIN * c + 1 + WIN, 1:W + 1], op0=ALU.add, op1=ALU.add).then_inc(S["x1"], 1)

            def deviation(b, c):
                dve.wait_ge(S["mean"], at(NCK * b + c + 1))
                dve.tensor_tensor(dev[:, ck(c)], x1[:, ck(c)], bank[2 + c % 2][:, 0:CPX], ALU.subtract).then_inc(S["dev"], 1)

            def norm(b, c):
                i = NCK * b + c + 1
                dve.wait_ge(S["std"], at(i))
                dve.reciprocal(std[:, c % 2, :], std[:, c % 2, :]).then_inc(S["rs"], 1)
                dve.wait_ge(S["rs"], at(i))
                dve.tensor_tensor(dev[:, ck(c)], dev[:, ck(c)], std[:, c % 2, :], ALU.mult).then_inc(S["rn"], 1)
                dve.wait_ge(S["rn"], at(i))
                dve.tensor_scalar(y[:, NWIN * c:NWIN * (c + 1), :].rearrange("c v (r q) -> c v r q", q=WIN),
                                  dev[:, ck(c)].rearrange("c (r v q) -> c v r q", r=WIN, v=NWIN),
                                  V["ln1_g"], V["ln1_b"], ALU.mult, ALU.add).then_inc(S["y"], 1)

            def image_values(b, c):
                dve.wait_ge(S["vcopy"], at(NCK * b + c + 1))
                dve.tensor_scalar(vpad[:, WIN * c + 2:WIN * (c + 1) + 2, 2:W + 2].rearrange("c r (v q) -> c v r q", q=WIN),
                                  bank[7][:, 0:CPX].rearrange("c (v r q) -> c v r q", r=WIN, q=WIN), V["v_b"], None, ALU.add).then_inc(S["vpad"], 1)

            def choose(b):
                dve.wait_ge(S["y"], at(NCK * (b + 1)))
                dve.tensor_reduce(ysum[:], y[:], AX.X, ALU.add).then_inc(S["ysum"], 1)
                dve.wait_ge(S["qkm"], at(b + 1))
                dve.tensor_scalar(qm[:], bank[0][:, 0:NW], 1.0 / WPX, V["q_b"], ALU.mult, ALU.add).then_inc(S["qkmc"], 1)
                dve.tensor_scalar(km[:], bank[1][:, 0:NW], 1.0 / WPX, V["k_b"], ALU.mult, ALU.add).then_inc(S["qkmc"], 1)
                dve.wait_ge(S["logit"], at(b + 1))
                dve.tensor_scalar(logit[:], bank[2][0:NW, 0:NW], QSCALE, None, ALU.mult).then_inc(S["lcopy"], 1)
                dve.wait_ge(S["lcopy"], at(b + 1))
                dve.sem_inc(S["issue"], 1)
                dve.max(top[:], logit[:]).then_inc(S["top"], 1)
                dve.wait_ge(S["top"], at(b + 1))
                dve.sem_inc(S["issue"], 1)
                dve.max_index(top_at[:], top[:], logit[:]).then_inc(S["topidx"], 1)

            def queries(b, r):
                dve.wait_ge(S["q"], at(NCK * b + r + 1))
                dve.wait_ge(S["s"], at(NW * b + NWIN * r))
                for h in range(HEADS):
                    p = slice(HD * h, HD * (h + 1))
                    last = dve.tensor_scalar(qz[p, :, h, :], bank[0][p, 0:CPX].rearrange("c (v p) -> c v p", p=WPX),
                                             vec[p, VEC0.index("q_b"):VEC0.index("q_b") + 1], QSCALE, ALU.add, ALU.mult)
                last.then_inc(S["qz"], 1)

            def score_max(b, r, v):
                n = b * NW + r * NWIN + v
                dve.wait_ge(S["s"], at(n + 1))
                dve.wait_ge(S["exp"], at(n - before(v) + 1))
                dve.tensor_reduce(nmax[:, v % 2, :], bank[1 + v % 2][:].rearrange("c (g k) -> c g k", g=2), AX.X, ALU.max,
                                  negate=True).then_inc(S["nb"], 1)

            def turned_values(b, r, v):
                n = b * NW + r * NWIN + v
                dve.wait_ge(S["vt"], at(n + 1))
                dve.wait_ge(S["pv"], at(n - before(v) + 1))
                dve.tensor_copy(vT[:, v % 2].rearrange("c g p -> c (g p)"), bank[3][:, 0:2 * C]).then_inc(S["vtc"], 1)

            def normalise(b, r, v):
                n = b * NW + r * NWIN + v
                dve.wait_ge(S["exp"], at(n + 1))
                dve.reciprocal(inv[:, v % 2, :], tot[:, v % 2, :]).then_inc(S["rec"], 1)
                dve.wait_ge(S["rec"], at(n + 1))
                for g in range(2):
                    last = dve.tensor_scalar(prob[:, v % 2, g, :], prob[:, v % 2, g, :], inv[:, v % 2, g:g + 1], None, ALU.mult)
                last.then_inc(S["pn"], 1)

            def outputs(b, r, v):
                n = b * NW + r * NWIN + v
                dve.wait_ge(S["pv"], at(n + 1))
                for h in range(HEADS):
                    p = slice(HD * h, HD * (h + 1))
                    last = dve.tensor_copy(orow[p, :, WIN * v:WIN * (v + 1)],
                                           bank[6][p, h * WPX:(h + 1) * WPX].rearrange("c (r q) -> c r q", q=WIN))
                last.then_inc(S["oc"], 1)

            def row_sum(b, r):
                dve.wait_ge(S["lepe"], at(NCK * b + r + 1))
                dve.wait_ge(S["oc"], at(NW * b + NWIN * r + NWIN))
                dve.scalar_tensor_tensor(out=oimg[:, bass.ds(r * CPX, CPX)], in0=bank[7][:, 0:CPX], scalar=V["lepe_b"],
                                         in1=orow[:].rearrange("c r w -> c (r w)"), op0=ALU.add, op1=ALU.add).then_inc(S["osum"], 1)

            def residual2(b, c):
                dve.wait_ge(S["wo"], at(NCK * b + c + 1))
                dve.scalar_tensor_tensor(out=dev[:, ck(c)], in0=bank[c % 2][:, 0:CPX], scalar=V["wo_b"], in1=x1[:, ck(c)],
                                         op0=ALU.add, op1=ALU.add).then_inc(S["x2"], 1)

            def deviation2(b, c):
                dve.wait_ge(S["mean2"], at(NCK * b + c + 1))
                dve.tensor_tensor(z[:, ck(c)], dev[:, ck(c)], bank[2][:, 0:CPX], ALU.subtract).then_inc(S["dev2"], 1)

            def norm2(b, c):
                i = NCK * b + c + 1
                dve.wait_ge(S["std2"], at(i))
                dve.reciprocal(std[:, c % 2, :], std[:, c % 2, :]).then_inc(S["rs2"], 1)
                dve.wait_ge(S["rs2"], at(i))
                dve.tensor_tensor(z[:, ck(c)], z[:, ck(c)], std[:, c % 2, :], ALU.mult).then_inc(S["rn2"], 1)
                dve.wait_ge(S["rn2"], at(i))
                dve.tensor_scalar(z[:, ck(c)], z[:, ck(c)], V["ln2_g"], V["ln2_b"], ALU.mult, ALU.add).then_inc(S["z"], 1)

            def finish(b, c):
                dve.wait_ge(S["m2"], at(NCK * b + c + 1))
                dve.scalar_tensor_tensor(out=oimg[:, ck(c)], in0=bank[7 if c % 2 else 0][:, 0:CPX], scalar=V["mlp_b2"], in1=dev[:, ck(c)],
                                         op0=ALU.add, op1=ALU.add).then_inc(S["fin"], 1)

            with dve.Fori(0, B) as b:
                dve.wait_ge(S["pad"], b + 1)
                for c in range(NCK + 3):
                    if c < NCK:
                        residual(b, c)
                    if 1 <= c <= NCK:
                        deviation(b, c - 1)
                    if 2 <= c <= NCK + 1:
                        norm(b, c - 2)
                    if c >= 3:
                        image_values(b, c - 3)
                choose(b)
                with dve.Fori(0, NWIN) as r:
                    queries(b, r)
                    for v in range(NWIN + 2):
                        if v < NWIN:
                            score_max(b, r, v)
                        if 1 <= v <= NWIN:
                            normalise(b, r, v - 1)
                        if v < NWIN:
                            turned_values(b, r, v)
                        if v >= 2:
                            outputs(b, r, v - 2)
                    dve.wait_ge(S["stored"], 16 * b + START)
                    dve.sem_inc(S["issue"], 1)
                    row_sum(b, r)
                for c in range(NCK + 2):
                    if c < NCK:
                        residual2(b, c)
                    if 1 <= c <= NCK:
                        deviation2(b, c - 1)
                    if c >= 2:
                        norm2(b, c - 2)
                for c in range(NCK):
                    finish(b, c)

        @block.scalar
        def _(act):
            for n in ("sq std kcopy vcopy exp ptc sq2 std2 gelu padfree".split()):
                act.sem_inc(S[n], START)
            act.wait_ge(S["zero"], 4)
            act.wait_ge(S["const"], 144)
            z = y[:].rearrange("c w p -> c (w p)")

            def square(b, c):
                act.wait_ge(S["dev"], at(NCK * b + c + 1))
                if c >= 2:
                    act.wait_ge(S["var"], at(NCK * b + c - 1))
                act.activation(sq[:, c % 2, :], dev[:, ck(c)], ACT.Square).then_inc(S["sq"], 1)

            def deviate(b, c):
                act.wait_ge(S["var"], at(NCK * b + c + 1))
                if c >= 2:
                    act.wait_ge(S["rn"], at(NCK * b + c - 1))
                act.activation(std[:, c % 2, :], bank[4 + c % 2][:, 0:CPX], ACT.Sqrt, bias=eps[:]).then_inc(S["std"], 1)

            def copy_kv(b, c):
                act.wait_ge(S["kv"], at(NCK * b + c + 1))
                for t, s, bias in ((0, "kcopy", "k_b"), (1, "vcopy", "v_b")):
                    act.activation(kv[:, NWIN * c:NWIN * (c + 1), t, :], bank[6 + t][:, 0:CPX].rearrange("c (v p) -> c v p", p=WPX),
                                   ACT.Identity, bias=V[bias]).then_inc(S[s], 1)

            def exponent(b, r, v):
                n = b * NW + r * NWIN + v
                act.wait_ge(S["nb"], at(n + 1))
                act.wait_ge(S["pt"], at(n - before(v) + 1))
                for g in range(2):
                    last = act.activation(prob[:, v % 2, g, :], bank[1 + v % 2][:, g * 256:(g + 1) * 256], ACT.Exp,
                                          bias=nmax[:, v % 2, g:g + 1], accum_out=tot[:, v % 2, g:g + 1])
                last.then_inc(S["exp"], 1)

            def copy_probs(b, r, v):
                n = b * NW + r * NWIN + v
                act.wait_ge(S["pt"], at(n + 1))
                act.wait_ge(S["pv"], at(n - before(v) + 1))
                act.activation(probT[:, v % 2].rearrange("c g p -> c (g p)"), bank[4 + v % 2][:], ACT.Copy).then_inc(S["ptc"], 1)

            def square2(b, c):
                act.wait_ge(S["dev2"], at(NCK * b + c + 1))
                if c >= 2:
                    act.wait_ge(S["var2"], at(NCK * b + c - 1))
                act.activation(sq[:, c % 2, :], z[:, ck(c)], ACT.Square).then_inc(S["sq2"], 1)

            def deviate2(b, c):
                act.wait_ge(S["var2"], at(NCK * b + c + 1))
                if c >= 2:
                    act.wait_ge(S["rn2"], at(NCK * b + c - 1))
                act.activation(std[:, c % 2, :], bank[3 + c % 2][:, 0:CPX], ACT.Sqrt, bias=eps[:]).then_inc(S["std2"], 1)

            def gelu(b, c):
                act.wait_ge(S["m1"], at(NCK * b + c + 1))
                if c >= 2:
                    act.wait_ge(S["m2"], at(NCK * b + c - 1))
                for j in range(HID):
                    last = act.activation(hid[:, c % 2, j, :], bank[4 + j][:, 0:CPX], ACT.Gelu, bias=V[f"mlp_b1_{j}"])
                last.then_inc(S["gelu"], 1)

            with act.Fori(0, B) as b:
                act.wait_ge(S["load"], 16 * b + 16)
                act.wait_ge(S["fin"], at(NCK * b))
                act.activation(padded[:, 1:H + 1, 1:W + 1], flat[:].rearrange("c (h w) -> c h w", w=W), ACT.Copy).then_inc(S["pad"], 1)
                act.wait_ge(S["pad"], b + 1)
                act.sem_inc(S["padfree"], 1)
                for c in range(NCK + 3):
                    if 1 <= c <= NCK:
                        square(b, c - 1)
                    if 2 <= c <= NCK + 1:
                        deviate(b, c - 2)
                    if c >= 3:
                        copy_kv(b, c - 3)
                with act.Fori(0, NWIN) as r:
                    for v in range(NWIN + 1):
                        if v < NWIN:
                            exponent(b, r, v)
                        if v >= 1:
                            copy_probs(b, r, v - 1)
                for c in range(NCK + 2):
                    if 1 <= c <= NCK:
                        square2(b, c - 1)
                    if c >= 2:
                        deviate2(b, c - 2)
                for c in range(NCK):
                    gelu(b, c)


VEC0 = ["pos_b", "ln1_g", "ln1_b", "q_b", "k_b", "v_b", "lepe_b", "wo_b", "ln2_g", "ln2_b", "mlp_b2", "mlp_b1_0", "mlp_b1_1", "mlp_b1_2"]
KX = W // 2 + 1
SHRINK = 0.01
KXG = [(0, 8), (8, 8), (16, 8), (24, KX - 24)]
STAGES = [("fw", HW // TPX), ("fh", KX), ("ih", KX), ("iw", HW // TPX)]


def groups_of_four(units):
    return [(k, min(4, units - k)) for k in range(0, units, 4)]


def fourier_phase(nc, B, conv_d, x_img, w, out_img, peak_d):
    with ExitStack() as ctx:
        sb = lambda name, shape, dt=F32: ctx.enter_context(nc.sbuf_tensor("fo_" + name, shape, dt))
        ps = lambda name, shape, dt=F32: ctx.enter_context(nc.psum_tensor("fo_" + name, shape, dt))
        sem = lambda name: ctx.enter_context(nc.semaphore("fo_" + name))
        ident = sb("ident", [C, C])
        group_mean = sb("group_mean", [C, C])
        vec = sb("vec", [C, len(VEC2)])
        V = {n: vec[:, k:k + 1] for k, n in enumerate(VEC2)}
        mats = {"fw": sb("m_fw", [2 * W, 4 * KX]), "fh": sb("m_fh", [2 * H, 2 * H]), "ih": sb("m_ih", [2 * H, 2 * H]), "iw": sb("m_iw", [4 * KX, 2 * W])}
        blocks = sb("blocks", [C, 4, C])
        minus = sb("minus", [C, 2, C])
        eps = sb("eps", [C, 1])
        conv = sb("conv", [C, NCK, CPX])
        xin = sb("xin", [C, HW])
        scratch = sb("scratch", [C, HW])
        img = sb("img", [C, HW])
        half = sb("half", [C, KX * H * 2])
        freq = sb("freq", [C, 2, KX, H])
        mixed = sb("mixed", [C, KX, 2, H])
        res = sb("res", [C, HW])
        turned = sb("turned", [C, 2, 4, C])
        hid = sb("hid", [C, 2, 2, 448])
        val = sb("val", [C, 2, 2, 448])
        cut = sb("cut", [C, 2, 448])
        pro = sb("pro", [C, 2, 448])
        prx = sb("prx", [C, 2, 448])
        stat = sb("stat", [C, 8])
        peak = sb("peak", [C, 2])
        bank = [ps(f"bank{k}", [C, 512]) for k in range(8)]
        names = ("const zero load loadfree sum sq m1 m2 small gn relu turn turnc prod prodc l1 relu1 l2 val shrunk cut pr yr px yi "
                 "peak stored neg issue root").split()
        S = {n: sem(n) for n in names}
        block = ctx.enter_context(nc.Block())
        GR = sum(len(groups_of_four(u)) for _, u in STAGES)
        first = {}
        k = 0
        for name, u in STAGES:
            first[name] = k
            k += len(groups_of_four(u))
        MX = len(KXG)

        def dest(name, g0, m):
            if name == "fw":
                return half[:].rearrange("c (k h p) -> c k (h p)", k=KX, p=2)[:, :, 4 * g0:4 * (g0 + m)].rearrange("c k (t q) -> c t k q", q=4)
            if name == "fh":
                return freq[:, :, g0:g0 + m, :].rearrange("c p k y -> c k p y")
            if name == "ih":
                return half[:].rearrange("c (h k p) -> c k h p", k=KX, p=2)[:, g0:g0 + m, :, :]

        def columns(name, g, m):
            n = mats[name].shape[1]
            b = bank[2 + (first[name] + g) % 2][:, 0:m * n]
            if name == "fw":
                return b.rearrange("c (t k q) -> c t k q", t=m, q=4)
            if name == "fh":
                return b.rearrange("c (k p y) -> c k p y", k=m, p=2)
            if name == "ih":
                return b.rearrange("c (k h p) -> c k h p", k=m, p=2)
            return b

        def unit(name, t):
            if name == "fw":
                return img[:, t * TPX:(t + 1) * TPX]
            if name == "fh":
                return half[:, t * 2 * H:(t + 1) * 2 * H]
            if name == "ih":
                return mixed[:, t, :, :].rearrange("c p y -> c (p y)")
            return half[:, t * 4 * KX:(t + 1) * 4 * KX]

        @block.sync
        def _(sp):
            for dst, src in ((ident, "ident"), (group_mean, "group_mean"), (vec, "vec2"), (mats["fw"], "dft_fw"), (mats["fh"], "dft_fh"),
                             (mats["ih"], "dft_ih"), (mats["iw"], "dft_iw"), (blocks, "blocks")):
                sp.dma_start(dst[:], w[src]).then_inc(S["const"], 16)
            with sp.Fori(0, B) as b:
                sp.wait_ge(S["gn"], at(b))
                sp.dma_start(conv[:], conv_d[bass.ds(b, 1)].rearrange("o k c n -> c (o k) n")).then_inc(S["load"], 16)
                sp.dma_start(xin[:], x_img[bass.ds(b, 1)].rearrange("o c n -> (o c) n")).then_inc(S["load"], 16)

        @block.gpsimd
        def _(pool):
            pool.memset(eps[:], GN_EPS).then_inc(S["zero"], 1)
            pool.memset(peak[:], 0.0).then_inc(S["zero"], 1)
            pool.sem_inc(S["px"], START)
            pool.sem_inc(S["yi"], START)
            with pool.Fori(0, B) as b:
                for m, (k0, kn) in enumerate(KXG):
                    n = kn * H
                    part = lambda a: a.rearrange("c k y -> c (k y)")
                    pool.wait_ge(S["shrunk"], at(MX * b + m + 1))
                    pool.wait_ge(S["yi"], at(MX * b + m))
                    pool.tensor_tensor(prx[:, 0, 0:n], val[:, m % 2, 0, 0:n], part(freq[:, 1, k0:k0 + kn, :]), ALU.mult)
                    pool.tensor_tensor(prx[:, 1, 0:n], val[:, m % 2, 1, 0:n], part(freq[:, 0, k0:k0 + kn, :]), ALU.mult).then_inc(S["px"], 1)
                    pool.wait_ge(S["px"], at(MX * b + m + 1))
                    pool.tensor_tensor(mixed[:, k0:k0 + kn, 1, :], prx[:, 0, 0:n].rearrange("c (k y) -> c k y", y=H),
                                       prx[:, 1, 0:n].rearrange("c (k y) -> c k y", y=H), ALU.add).then_inc(S["yi"], 1)

        @block.tensor
        def _(pe):
            for n in "m1 m2 turn prod l1 l2".split():
                pe.sem_inc(S[n], START)
            pe.wait_ge(S["const"], 128)
            pe.wait_ge(S["neg"], 1)

            def turn(b, name, g):
                n = GR * b + first[name] + g
                g0, m = groups_of_four(dict(STAGES)[name])[g]
                pe.wait_ge(S["turnc"], at(n - 1))
                for k in range(m):
                    src = unit(name, g0 + k)
                    last = pe.transpose(bank[(first[name] + g) % 2][0:src.shape[1], k * C:(k + 1) * C], src, ident[:])
                last.then_inc(S["turn"], 1)

            def product(b, name, g):
                n = GR * b + first[name] + g
                g0, m = groups_of_four(dict(STAGES)[name])[g]
                rows, cols = mats[name].shape
                pe.wait_ge(S["turnc"], at(n + 1))
                pe.wait_ge(S["prodc"], at(n - 1))
                for k in range(m):
                    last = pe.matmul(bank[2 + (first[name] + g) % 2][:, k * cols:(k + 1) * cols],
                                     turned[0:rows, (first[name] + g) % 2, k, :], mats[name][:], start=True, stop=True)
                last.then_inc(S["prod"], 1)

            def transform(b, name):
                G = len(groups_of_four(dict(STAGES)[name]))
                for g in range(G + 1):
                    if g < G:
                        turn(b, name, g)
                    if g >= 1:
                        product(b, name, g - 1)

            def mix_first(b, m):
                k0, kn = KXG[m]
                n = kn * H
                part = lambda p: freq[:, p, k0:k0 + kn, :].rearrange("c k y -> c (k y)")
                pe.wait_ge(S["relu1"], at(MX * b + m))
                for o, terms in enumerate((((blocks[:, 0], 0), (minus[:, 0], 1)), ((blocks[:, 0], 1), (blocks[:, 1], 0)))):
                    for k, (mat, p) in enumerate(terms):
                        last = pe.matmul(bank[4 + o][:, 0:n], mat, part(p), start=(k == 0), stop=(k == 1))
                last.then_inc(S["l1"], 1)

            def mix_second(b, m):
                k0, kn = KXG[m]
                n = kn * H
                pe.wait_ge(S["relu1"], at(MX * b + m + 1))
                pe.wait_ge(S["val"], at(MX * b + m))
                for o, terms in enumerate((((blocks[:, 2], 0), (minus[:, 1], 1)), ((blocks[:, 2], 1), (blocks[:, 3], 0)))):
                    for k, (mat, p) in enumerate(terms):
                        last = pe.matmul(bank[6 + o][:, 0:n], mat, hid[:, m % 2, p, 0:n], start=(k == 0), stop=(k == 1))
                last.then_inc(S["l2"], 1)

            with pe.Fori(0, B) as b:
                pe.wait_ge(S["sum"], at(b + 1))
                pe.wait_ge(S["peak"], at(b))
                pe.matmul(bank[4][:, 0:1], group_mean[:], stat[:, 0:1], start=True, stop=True).then_inc(S["m1"], 1)
                pe.wait_ge(S["sq"], at(b + 1))
                pe.matmul(bank[5][:, 0:1], group_mean[:], stat[:, 2:3], start=True, stop=True).then_inc(S["m2"], 1)
                pe.wait_ge(S["relu"], at(b + 1))
                transform(b, "fw")
                pe.wait_ge(S["prodc"], at(GR * b + first["fh"]))
                transform(b, "fh")
                pe.wait_ge(S["prodc"], at(GR * b + first["ih"]))
                for m in range(MX + 1):
                    if m < MX:
                        mix_first(b, m)
                    if m >= 1:
                        mix_second(b, m - 1)
                pe.wait_ge(S["yr"], at(MX * (b + 1)))
                pe.wait_ge(S["yi"], at(MX * (b + 1)))
                transform(b, "ih")
                pe.wait_ge(S["prodc"], at(GR * b + first["iw"]))
                transform(b, "iw")

        @block.vector
        def _(dve):
            for n in "small gn prodc shrunk cut pr yr peak".split():
                dve.sem_inc(S[n], START)
            dve.wait_ge(S["const"], 128)
            dve.wait_ge(S["zero"], 2)
            dve.tensor_scalar(minus[:, 0], blocks[:, 1], -1.0, None, ALU.mult)
            dve.tensor_scalar(minus[:, 1], blocks[:, 3], -1.0, None, ALU.mult).then_inc(S["neg"], 1)

            def collect(b, name):
                for g, (g0, m) in enumerate(groups_of_four(dict(STAGES)[name])):
                    n = GR * b + first[name] + g
                    dve.wait_ge(S["prod"], at(n + 1))
                    if name == "iw":
                        px = slice(g0 * TPX, (g0 + m) * TPX)
                        dve.tensor_tensor(res[:, px], columns(name, g, m), img[:, px], ALU.add).then_inc(S["prodc"], 1)
                    else:
                        dve.tensor_copy(dest(name, g0, m), columns(name, g, m)).then_inc(S["prodc"], 1)

            def shrink(b, m):
                k0, kn = KXG[m]
                n = kn * H
                i = MX * b + m + 1
                v = val[:, m % 2, :, 0:n]
                dve.wait_ge(S["val"], at(i))
                dve.tensor_scalar(cut[:, :, 0:n], v, SHRINK, -SHRINK, ALU.min, ALU.max).then_inc(S["cut"], 1)
                dve.wait_ge(S["cut"], at(i))
                dve.tensor_tensor(v, v, cut[:, :, 0:n], ALU.subtract).then_inc(S["shrunk"], 1)
                dve.wait_ge(S["shrunk"], at(i))
                dve.tensor_tensor(pro[:, :, 0:n], v, freq[:, :, k0:k0 + kn, :].rearrange("c p k y -> c p (k y)"), ALU.mult).then_inc(S["pr"], 1)
                dve.wait_ge(S["pr"], at(i))
                dve.tensor_tensor(mixed[:, k0:k0 + kn, 0, :], pro[:, 0, 0:n].rearrange("c (k y) -> c k y", y=H),
                                  pro[:, 1, 0:n].rearrange("c (k y) -> c k y", y=H), ALU.subtract).then_inc(S["yr"], 1)

            with dve.Fori(0, B) as b:
                def small(k, instruction):
                    instruction.then_inc(S["small"], 1)
                    dve.wait_ge(S["small"], at(5 * b + k))

                dve.wait_ge(S["m1"], at(b + 1))
                small(1, dve.tensor_scalar(stat[:, 1:2], bank[4][:, 0:1], -1.0, None, ALU.mult))
                dve.wait_ge(S["relu"], at(b))
                dve.wait_ge(S["load"], 32 * b + 32)
                dve.wait_ge(S["m2"], at(b + 1))
                dve.wait_ge(S["root"], b + 1)
                small(2, dve.reciprocal(stat[:, 4:5], stat[:, 3:4]))
                small(3, dve.tensor_tensor(stat[:, 5:6], stat[:, 4:5], V["gamma"], ALU.mult))
                small(4, dve.scalar_tensor_tensor(out=stat[:, 6:7], in0=stat[:, 5:6], scalar=stat[:, 1:2], in1=V["beta"], op0=ALU.mult, op1=ALU.add))
                dve.scalar_tensor_tensor(out=img[:], in0=conv[:].rearrange("c k n -> c (k n)"), scalar=stat[:, 5:6], in1=xin[:],
                                         op0=ALU.mult, op1=ALU.add).then_inc(S["gn"], 1)
                collect(b, "fw")
                collect(b, "fh")
                for m in range(MX):
                    shrink(b, m)
                collect(b, "ih")
                dve.wait_ge(S["stored"], 16 * b + START)
                collect(b, "iw")
                dve.wait_ge(S["prodc"], at(GR * (b + 1)))
                small(5, dve.tensor_reduce(peak[:, 1:2], res[:], AX.X, ALU.max, apply_absolute_value=True))
                dve.tensor_tensor(peak[:, 0:1], peak[:, 0:1], peak[:, 1:2], ALU.max).then_inc(S["peak"], 1)

        @block.scalar
        def _(act):
            for n in "sum sq relu turnc relu1 val stored".split():
                act.sem_inc(S[n], START)
            act.wait_ge(S["const"], 128)
            act.wait_ge(S["zero"], 2)

            def copy_turned(b, name):
                for g, (g0, m) in enumerate(groups_of_four(dict(STAGES)[name])):
                    n = GR * b + first[name] + g
                    rows = mats[name].shape[0]
                    act.wait_ge(S["turn"], at(n + 1))
                    act.wait_ge(S["prod"], at(n - 1))
                    act.activation(turned[0:rows, (first[name] + g) % 2, 0:m, :], bank[(first[name] + g) % 2][0:rows, 0:m * C].rearrange("r (k c) -> r k c", c=C),
                                   ACT.Copy).then_inc(S["turnc"], 1)

            def mix(b):
                for m in range(MX + 1):
                    if m < MX:
                        n = KXG[m][1] * H
                        act.wait_ge(S["l1"], at(MX * b + m + 1))
                        if m >= 2:
                            act.wait_ge(S["l2"], at(MX * b + m - 1))
                        act.activation(hid[:, m % 2, 0, 0:n], bank[4][:, 0:n], ACT.Relu, bias=V["b1r"])
                        act.activation(hid[:, m % 2, 1, 0:n], bank[5][:, 0:n], ACT.Relu, bias=V["b1i"]).then_inc(S["relu1"], 1)
                    if m >= 1:
                        j = m - 1
                        n = KXG[j][1] * H
                        act.wait_ge(S["l2"], at(MX * b + j + 1))
                        if j >= 2:
                            act.wait_ge(S["yr"], at(MX * b + j - 1))
                            act.wait_ge(S["yi"], at(MX * b + j - 1))
                        act.activation(val[:, j % 2, 0, 0:n], bank[6][:, 0:n], ACT.Identity, bias=V["b2r"])
                        act.activation(val[:, j % 2, 1, 0:n], bank[7][:, 0:n], ACT.Identity, bias=V["b2i"]).then_inc(S["val"], 1)

            with act.Fori(0, B) as b:
                act.wait_ge(S["load"], 32 * b + 32)
                act.activation(scratch[:], conv[:].rearrange("c k n -> c (k n)"), ACT.Copy, accum_out=stat[:, 0:1]).then_inc(S["sum"], 1)
                act.wait_ge(S["small"], at(5 * b + 1))
                act.wait_ge(S["sum"], at(b + 1))
                act.activation(scratch[:], conv[:].rearrange("c k n -> c (k n)"), ACT.Square, bias=stat[:, 1:2], accum_out=stat[:, 2:3]).then_inc(S["sq"], 1)
                act.wait_ge(S["m2"], at(b + 1))
                act.activation(stat[:, 3:4], bank[5][:, 0:1], ACT.Sqrt, bias=eps[:]).then_inc(S["root"], 1)
                act.wait_ge(S["gn"], at(b + 1))
                act.activation(img[:], img[:], ACT.Relu, bias=stat[:, 6:7]).then_inc(S["relu"], 1)
                copy_turned(b, "fw")
                copy_turned(b, "fh")
                mix(b)
                copy_turned(b, "ih")
                copy_turned(b, "iw")
                act.wait_ge(S["prodc"], at(GR * (b + 1)))
                act.dma_start(out_img[bass.ds(b, 1)].rearrange("o c n -> (o c) n"), res[:]).then_inc(S["stored"], 16)
            act.wait_ge(S["peak"], at(B))
            act.wait_ge(S["stored"], 16 * B + START)
            act.dma_start(peak_d, peak[:, 0:1]).then_inc(S["stored"], 16)
            act.wait_ge(S["stored"], 16 * B + 16 + START)


VEC2 = ["gamma", "beta", "b1r", "b1i", "b2r", "b2i"]


def transform_matrices():
    import numpy as np
    n = np.arange(W)
    root = np.sqrt(float(W))
    fw = np.zeros((2, W, KX, 2, 2))
    ang = 2 * np.pi * np.outer(n, np.arange(KX)) / W
    for r in range(2):
        fw[r, :, :, r, 0] = np.cos(ang) / root
        fw[r, :, :, r, 1] = -np.sin(ang) / root
    ang = 2 * np.pi * np.outer(n, n) / H
    co, si = np.cos(ang) / root, np.sin(ang) / root
    fh = np.zeros((H, 2, 2, H))
    fh[:, 0, 0], fh[:, 0, 1], fh[:, 1, 0], fh[:, 1, 1] = co, -si, si, co
    ih = np.zeros((2, H, H, 2))
    ih[0, :, :, 0], ih[0, :, :, 1], ih[1, :, :, 0], ih[1, :, :, 1] = co, si, -si, co
    iw = np.zeros((2, KX, 2, 2, W))
    ang = 2 * np.pi * np.outer(np.arange(KX), n) / W
    weight = np.full((KX, 1), 2.0)
    weight[0] = weight[-1] = 1.0
    sine = np.sin(ang)
    sine[0] = sine[-1] = 0.0
    for r in range(2):
        iw[r, :, 0, r] = weight * np.cos(ang) / root
        iw[r, :, 1, r] = -weight * sine / root
    f = lambda a, r, c: np.ascontiguousarray(a.reshape(r, c).astype(np.float32))
    return {"dft_fw": f(fw, 2 * W, 4 * KX), "dft_fh": f(fh, 2 * H, 2 * H), "dft_ih": f(ih, 2 * H, 2 * H), "dft_iw": f(iw, 4 * KX, 2 * W)}
Q8, Q4 = 127.0, 7.0
VEC3 = ["b1", "pb1", "b2", "pb2"]


def quantised_phase(nc, B, x_img, peak_d, w, out_img):
    with ExitStack() as ctx:
        sb = lambda name, shape, dt=F32: ctx.enter_context(nc.sbuf_tensor("qu_" + name, shape, dt))
        ps = lambda name, shape, dt=F32: ctx.enter_context(nc.psum_tensor("qu_" + name, shape, dt))
        ident = sb("ident", [C, C])
        vec = sb("vec", [C, len(VEC3)])
        V = {n: vec[:, k:k + 1] for k, n in enumerate(VEC3)}
        raw = {"w1": sb("raw_w1", [C, 9]), "p1": sb("raw_p1", [C, C]), "w2": sb("raw_w2", [C, 9]), "p2": sb("raw_p2", [C, C])}
        whole = {n: sb("whole_" + n, list(a.shape)) for n, a in raw.items()}
        point = {n: sb("point_" + n, [C, C], BF16) for n in ("p1", "p2")}
        diag = {n: sb("diag_" + n, [C, 9, C], BF16) for n in ("w1", "w2")}
        peaks = sb("peaks", [C, 5])
        tops = sb("tops", [C, 5])
        scale = sb("scale", [C, 5])
        inv = sb("inv", [C, 5])
        hi = sb("hi", [C, 2])
        lo = sb("lo", [C, 2])
        few = sb("few", [C, 16])
        held = sb("held", [C, B * HW], I16)
        held_q = held[:].bitcast(BF16)
        xin = sb("xin", [C, 2, HW])
        real = sb("real", [C, 2, HW])
        padded = sb("padded", [C, 2, HP, HP], BF16)
        quant = sb("quant", [C, 2, HW], BF16)
        relued = sb("relued", [C, 4, CPX])
        chunk_hi = sb("chunk_hi", [C, NCK])
        bank = [ps(f"bank{k}", [C, 512]) for k in range(8)]
        ck = lambda c: slice(c * CPX, (c + 1) * CPX)
        back4 = lambda c: {0: 3, 1: 3, 2: 3, 3: NCK}.get(c, 4)
        img = lambda b: bass.ds(b * HW, HW)
        rows = lambda a: a.rearrange("c (h w) -> c h w", w=W)

        def scales(name, program):
            with ExitStack() as inner:
                s_step = inner.enter_context(nc.semaphore(f"qu_{name}_step"))
                s_ask = inner.enter_context(nc.semaphore(f"qu_{name}_ask"))
                s_top = inner.enter_context(nc.semaphore(f"qu_{name}_top"))
                s_in = inner.enter_context(nc.semaphore(f"qu_{name}_in"))
                block = inner.enter_context(nc.Block())
                loads, before, width, after = program

                @block.sync
                def _(sp):
                    for dst, src in loads:
                        sp.dma_start(dst, src).then_inc(s_in, 16)

                @block.gpsimd
                def _(pool):
                    if name == "start":
                        pool.memset(padded[:], 0.0).then_inc(s_in, 1)
                    pool.wait_ge(s_ask, 1)
                    pool.partition_all_reduce(tops[:, 0:width], peaks[:, 0:width], C, bass.bass_isa.ReduceOp.max).then_inc(s_top, 1)

                @block.vector
                def _(dve):
                    count = [0]

                    def step(instruction):
                        count[0] += 1
                        instruction.then_inc(s_step, 1)
                        dve.wait_ge(s_step, count[0])

                    dve.wait_ge(s_in, 16 * len(loads) + (name == "start"))
                    before(dve, step)
                    dve.sem_inc(s_ask, 1)
                    dve.wait_ge(s_top, 1)
                    after(dve, step)

        def start_before(dve, step):
            for k, n in enumerate(("w1", "p1", "w2", "p2")):
                step(dve.tensor_reduce(peaks[:, k + 1:k + 2], raw[n][:], AX.X, ALU.max, apply_absolute_value=True))

        def start_after(dve, step):
            step(dve.tensor_scalar(scale[:, 0:1], tops[:, 0:1], 1.0 / Q8, 1e-8, ALU.mult, ALU.max))
            step(dve.tensor_scalar(scale[:, 1:5], tops[:, 1:5], 1.0 / Q4, 1e-8, ALU.mult, ALU.max))
            step(dve.reciprocal(inv[:], scale[:]))
            for k, n in enumerate(("w1", "p1", "w2", "p2")):
                q = whole[n][:]
                step(dve.tensor_scalar(q, raw[n][:], inv[:, k + 1:k + 2], ROUND, ALU.mult, ALU.add))
                step(dve.tensor_scalar(q, q, ROUND, Q4, ALU.subtract, ALU.min))
                if n in point:
                    step(dve.tensor_scalar(point[n][:], q, -Q4 - 1.0, None, ALU.max))
                else:
                    step(dve.tensor_scalar(q, q, -Q4 - 1.0, None, ALU.max))
                    for t in range(9):
                        step(dve.tensor_scalar(diag[n][:, t, :], ident[:], q[:, t:t + 1], None, ALU.mult))
            step(dve.tensor_tensor(few[:, 0:1], scale[:, 0:1], scale[:, 1:2], ALU.mult))

        def ends_before(bias):
            def before(dve, step):
                step(dve.scalar_tensor_tensor(out=few[:, 2:3], in0=hi[:, 0:1], scalar=few[:, 0:1], in1=V[bias], op0=ALU.mult, op1=ALU.add))
                step(dve.scalar_tensor_tensor(out=few[:, 3:4], in0=lo[:, 0:1], scalar=few[:, 0:1], in1=V[bias], op0=ALU.mult, op1=ALU.add))
                step(dve.tensor_reduce(peaks[:, 0:1], few[:, 2:4], AX.X, ALU.max, apply_absolute_value=True))
            return before

        def relu_before(bias):
            def before(dve, step):
                step(dve.scalar_tensor_tensor(out=few[:, 2:3], in0=hi[:, 0:1], scalar=few[:, 0:1], in1=V[bias], op0=ALU.mult, op1=ALU.add))
                step(dve.tensor_scalar(peaks[:, 0:1], few[:, 2:3], 0.0, None, ALU.max))
            return before

        def next_after(bias, k):
            def after(dve, step):
                step(dve.tensor_scalar(scale[:, 0:1], tops[:, 0:1], 1.0 / Q8, 1e-8, ALU.mult, ALU.max))
                step(dve.reciprocal(inv[:, 0:1], scale[:, 0:1]))
                step(dve.tensor_tensor(few[:, 4:5], few[:, 0:1], inv[:, 0:1], ALU.mult))
                step(dve.tensor_tensor(few[:, 5:6], V[bias], inv[:, 0:1], ALU.mult))
                step(dve.tensor_tensor(few[:, 0:1], scale[:, 0:1], scale[:, k:k + 1], ALU.mult))
            return after

        def sums_pass(first):
            with ExitStack() as inner:
                tag = "a" if first else "c"
                names = "load real quant sums copied point best free issue".split()
                S = {n: inner.enter_context(nc.semaphore(f"qu_{tag}_{n}")) for n in names}
                s_load = [inner.enter_context(nc.semaphore(f"qu_{tag}_load{j}")) for j in range(2)]
                block = inner.enter_context(nc.Block())
                dw = diag["w1" if first else "w2"]

                if first:
                    @block.sync
                    def _(sp):
                        with sp.Fori(0, B // 2) as pair:
                            for j in range(2):
                                b = pair * 2 + j
                                sp.wait_ge(S["real"], at(b - 1))
                                sp.dma_start(xin[:, j, :], x_img[bass.ds(b, 1)].rearrange("o c n -> (o c) n")).then_inc(s_load[j], 16)

                @block.tensor
                def _(pe):
                    pe.sem_inc(S["sums"], START)
                    pe.sem_inc(S["point"], START)
                    with pe.Fori(0, B // 2) as pair:
                        for j in range(2):
                            b = pair * 2 + j
                            if not first:
                                for c in range(NCK):
                                    pe.wait_ge(S["real"], at(NCK * b + c - back4(c) + 1))
                                    pe.matmul(bank[c % 4][:, 0:CPX], point["p1"][:], held_q[:, bass.ds(b * HW + c * CPX, CPX)],
                                              start=True, stop=True).then_inc(S["point"], 1)
                            pe.wait_ge(S["quant"], at((b + 1) * (1 if first else NCK)))
                            for c in range(NCK):
                                pe.wait_ge(S["copied"], at(NCK * b + c - back4(c) + 1))
                                for k in range(9):
                                    last = pe.matmul(bank[4 + c % 4][:, 0:CPX], dw[:, k, :],
                                                     padded[:, j, WIN * c + k // 3:WIN * c + k // 3 + WIN, k % 3:k % 3 + W], start=(k == 0), stop=(k == 8))
                                last.then_inc(S["sums"], 1)

                @block.scalar
                def _(act):
                    act.sem_inc(S["real"], START)
                    act.sem_inc(S["copied"], START)

                    def collect(b):
                        act.wait_ge(S["best"], at(b))
                        for c in range(NCK):
                            act.wait_ge(S["sums"], at(NCK * b + c + 1))
                            act.sem_inc(S["issue"], 1)
                            act.activation(held[:, bass.ds(b * HW + c * CPX, CPX)], bank[4 + c % 4][:, 0:CPX], ACT.Copy).then_inc(S["copied"], 1)

                    with act.Fori(0, B // 2) as pair:
                        for j in range(2):
                            b = pair * 2 + j
                            if first:
                                act.wait_ge(s_load[j], 16 * pair + 16)
                                act.wait_ge(S["quant"], at(b - 1))
                                act.activation(real[:, j, :], xin[:, j, :], ACT.Copy, scale=inv[:, 0:1]).then_inc(S["real"], 1)
                            else:
                                for c in range(NCK):
                                    act.wait_ge(S["point"], at(NCK * b + c + 1))
                                    act.wait_ge(S["quant"], at(NCK * b + c - NCK + 1))
                                    act.activation(real[:, 0, ck(c)], bank[c % 4][:, 0:CPX], ACT.Relu, bias=few[:, 5:6], scale=few[:, 4:5]).then_inc(S["real"], 1)
                            collect(b)

                @block.vector
                def _(dve):
                    dve.sem_inc(S["quant"], START)
                    dve.sem_inc(S["best"], START)
                    dve.memset(hi[:], -3.0e38).then_inc(S["free"], 1)
                    dve.memset(lo[:], 3.0e38).then_inc(S["free"], 1)
                    dve.wait_ge(S["free"], 2)

                    def search(b):
                        dve.wait_ge(S["copied"], at(NCK * (b + 1)))
                        dve.tensor_reduce(hi[:, 1:2], held[:, img(b)], AX.X, ALU.max).then_inc(S["free"], 1)
                        dve.tensor_reduce(lo[:, 1:2], held[:, img(b)], AX.X, ALU.min).then_inc(S["free"], 1)
                        dve.wait_ge(S["free"], 4 * b + 4)
                        dve.tensor_tensor(hi[:, 0:1], hi[:, 0:1], hi[:, 1:2], ALU.max).then_inc(S["free"], 1)
                        dve.tensor_tensor(lo[:, 0:1], lo[:, 0:1], lo[:, 1:2], ALU.min).then_inc(S["free"], 1)
                        dve.wait_ge(S["free"], 4 * b + 6)
                        dve.sem_inc(S["best"], 1)

                    with dve.Fori(0, B // 2) as pair:
                        for j in range(2):
                            b = pair * 2 + j
                            dve.wait_ge(S["sums"], at(NCK * b - NCK))
                            if first:
                                dve.wait_ge(S["real"], at(b + 1))
                                dve.tensor_scalar(padded[:, j, 1:H + 1, 1:W + 1], rows(real[:, j, :]), ROUND, ROUND, ALU.add, ALU.subtract).then_inc(S["quant"], 1)
                            else:
                                for c in range(NCK):
                                    dve.wait_ge(S["real"], at(NCK * b + c + 1))
                                    dve.tensor_scalar(padded[:, j, WIN * c + 1:WIN * (c + 1) + 1, 1:W + 1], rows(real[:, 0, ck(c)]),
                                                      ROUND, ROUND, ALU.add, ALU.subtract).then_inc(S["quant"], 1)
                            search(b)

        def peak_pass():
            with ExitStack() as inner:
                S = {n: inner.enter_context(nc.semaphore(f"qu_b_{n}")) for n in "real quant point best free issue".split()}
                block = inner.enter_context(nc.Block())

                @block.scalar
                def _(act):
                    act.sem_inc(S["real"], START)
                    with act.Fori(0, B // 2) as pair:
                        for j in range(2):
                            b = pair * 2 + j
                            act.wait_ge(S["quant"], at(b - 1))
                            act.sem_inc(S["issue"], 1)
                            act.activation(real[:, j, :], held[:, img(b)], ACT.Identity, bias=few[:, 5:6], scale=few[:, 4:5]).then_inc(S["real"], 1)

                @block.tensor
                def _(pe):
                    pe.sem_inc(S["point"], START)
                    with pe.Fori(0, B) as b:
                        pe.wait_ge(S["quant"], at(b + 1))
                        for c in range(NCK):
                            pe.wait_ge(S["best"], at(NCK * b + c - NCK + 1))
                            pe.matmul(bank[c][:, 0:CPX], point["p1"][:], held_q[:, bass.ds(b * HW + c * CPX, CPX)],
                                      start=True, stop=True).then_inc(S["point"], 1)

                @block.vector
                def _(dve):
                    dve.sem_inc(S["quant"], START)
                    dve.sem_inc(S["best"], START)
                    dve.memset(hi[:], -3.0e38).then_inc(S["free"], 1)
                    dve.wait_ge(S["free"], 1)
                    with dve.Fori(0, B // 2) as pair:
                        for j in range(2):
                            b = pair * 2 + j
                            dve.wait_ge(S["real"], at(b + 1))
                            dve.tensor_scalar(held_q[:, img(b)], real[:, j, :], ROUND, ROUND, ALU.add, ALU.subtract).then_inc(S["quant"], 1)
                            for c in range(NCK):
                                dve.wait_ge(S["point"], at(NCK * b + c + 1))
                                dve.tensor_reduce(chunk_hi[:, c:c + 1], bank[c][:, 0:CPX], AX.X, ALU.max).then_inc(S["best"], 1)
                            dve.wait_ge(S["best"], at(NCK * (b + 1)))
                            dve.tensor_reduce(hi[:, 1:2], chunk_hi[:], AX.X, ALU.max).then_inc(S["free"], 1)
                            dve.wait_ge(S["free"], 2 * b + 2)
                            dve.tensor_tensor(hi[:, 0:1], hi[:, 0:1], hi[:, 1:2], ALU.max).then_inc(S["free"], 1)
                            dve.wait_ge(S["free"], 2 * b + 3)

        def last_pass():
            with ExitStack() as inner:
                S = {n: inner.enter_context(nc.semaphore(f"qu_d_{n}")) for n in "real quant point relued added issue".split()}
                s_load = [inner.enter_context(nc.semaphore(f"qu_d_load{j}")) for j in range(2)]
                s_stored = [inner.enter_context(nc.semaphore(f"qu_d_stored{j}")) for j in range(2)]
                block = inner.enter_context(nc.Block())

                @block.gpsimd
                def _(pool):
                    for j in range(2):
                        pool.sem_inc(s_stored[j], START)
                    with pool.Fori(0, B // 2) as pair:
                        for j in range(2):
                            b = pair * 2 + j
                            pool.wait_ge(s_stored[j], at(16 * pair))
                            pool.sem_inc(S["issue"], 1)
                            pool.dma_start(xin[:, j, :], x_img[bass.ds(b, 1)].rearrange("o c n -> (o c) n")).then_inc(s_load[j], 16)

                @block.scalar
                def _(act):
                    act.sem_inc(S["real"], START)
                    act.sem_inc(S["relued"], START)

                    def scaled(b, j):
                        act.wait_ge(S["quant"], at(b - 1))
                        act.sem_inc(S["issue"], 1)
                        act.activation(real[:, j, :], held[:, img(b)], ACT.Identity, bias=few[:, 5:6], scale=few[:, 4:5]).then_inc(S["real"], 1)

                    with act.Fori(0, B // 2) as pair:
                        for j in range(2):
                            b = pair * 2 + j
                            scaled(b, j)
                            for c in range(NCK):
                                act.wait_ge(S["point"], at(NCK * b + c + 1))
                                act.wait_ge(S["added"], at(NCK * b + c - back4(c) + 1))
                                act.activation(relued[:, c % 4, :], bank[c][:, 0:CPX], ACT.Relu, bias=V["pb2"], scale=few[:, 0:1]).then_inc(S["relued"], 1)

                @block.tensor
                def _(pe):
                    pe.sem_inc(S["point"], START)
                    with pe.Fori(0, B // 2) as pair:
                        for j in range(2):
                            b = pair * 2 + j
                            pe.wait_ge(S["quant"], at(b + 1))
                            for c in range(NCK):
                                pe.wait_ge(S["relued"], at(NCK * b + c - NCK + 1))
                                pe.matmul(bank[c][:, 0:CPX], point["p2"][:], quant[:, j, ck(c)], start=True, stop=True).then_inc(S["point"], 1)

                @block.vector
                def _(dve):
                    dve.sem_inc(S["quant"], START)
                    dve.sem_inc(S["added"], START)
                    with dve.Fori(0, B // 2) as pair:
                        for j in range(2):
                            b = pair * 2 + j
                            dve.wait_ge(S["real"], at(b + 1))
                            dve.wait_ge(S["point"], at(NCK * b - NCK))
                            dve.tensor_scalar(quant[:, j, :], real[:, j, :], ROUND, ROUND, ALU.add, ALU.subtract).then_inc(S["quant"], 1)
                            dve.wait_ge(s_load[j], 16 * pair + 16)
                            for c in range(NCK):
                                dve.wait_ge(S["relued"], at(NCK * b + c + 1))
                                dve.tensor_tensor(xin[:, j, ck(c)], xin[:, j, ck(c)], relued[:, c % 4, :], ALU.add).then_inc(S["added"], 1)

                @block.sync
                def _(sp):
                    with sp.Fori(0, B // 2) as pair:
                        for j in range(2):
                            b = pair * 2 + j
                            sp.wait_ge(S["added"], at(NCK * (b + 1)))
                            sp.dma_start(out_img[bass.ds(b, 1)].rearrange("o c n -> (o c) n"), xin[:, j, :]).then_inc(s_stored[j], 16)
                    for j in range(2):
                        sp.wait_ge(s_stored[j], at(16 * (B // 2)))

        loads = [(ident[:], w["ident"]), (vec[:], w["vec3"]), (peaks[:, 0:1], peak_d)] + [(raw[n][:], w["q_" + n]) for n in raw]
        scales("start", (loads, start_before, 5, start_after))
        sums_pass(True)
        scales("one", ([], ends_before("b1"), 1, next_after("b1", 2)))
        peak_pass()
        scales("two", ([], relu_before("pb1"), 1, next_after("pb1", 3)))
        sums_pass(False)
        scales("three", ([], ends_before("b2"), 1, next_after("b2", 4)))
        last_pass()


def program(nc, d, out):
    B = d["x"].shape[0]
    scratch = lambda name, shape: nc.dram_tensor("scratch_" + name, shape, F32).ap()
    after0 = scratch("after0", [B, C, HW])
    windows = scratch("windows", [B * NCK, C, (CH_ROWS + 2) * HP])
    table = scratch("table", [B * TROWS, 4 * C])
    conv = scratch("conv", [B * NCK, C, CPX])
    after2 = scratch("after2", [B, C, HW])
    peak = scratch("peak", [C, 1])
    attention_phase(nc, B, d["x"], d, after0)
    spread_phase(nc, B, after0, d["ident"], windows, table)
    deform_phase(nc, B * NCK, windows, table, d["base"], d["ident"], d["woff"], d["boff"], d["wdcn"], conv)
    fourier_phase(nc, B, conv.rearrange("(b k) c n -> b k c n", k=NCK), after0, d, after2, peak)
    quantised_phase(nc, B, after2, peak, d, out)


def lay_out(i):
    import numpy as np
    L0, L1, L2, L3 = ({k[8:]: v for k, v in i.items() if k.startswith(f"L{n}_conv_")} for n in range(4))
    B = i["x"].shape[0]
    third = lambda a: [a[k * C:(k + 1) * C] for k in range(3)]
    named0 = dict(L0, mlp_b1_0=third(L0["mlp_b1"])[0], mlp_b1_1=third(L0["mlp_b1"])[1], mlp_b1_2=third(L0["mlp_b1"])[2],
                  q_b=third(L0["qkv_b"])[0], k_b=third(L0["qkv_b"])[1], v_b=third(L0["qkv_b"])[2])
    tm, tr = L1["w_tm"].reshape(4, C, 9), L1["w_tr"].reshape(2, C, 9)
    order = lambda m, r: np.stack([m[0], m[2], m[1], m[3], r[0], r[1]])

    def block_diagonal(a):
        whole, n = np.zeros((C, C), np.float32), a.shape[1]
        for k in range(a.shape[0]):
            whole[k * n:(k + 1) * n, k * n:(k + 1) * n] = a[k]
        return whole

    group = np.arange(C) // 4
    named2 = {"gamma": L1["gn_gamma"], "beta": L1["gn_beta"], "b1r": L2["b1"][0].ravel(), "b1i": L2["b1"][1].ravel(),
              "b2r": L2["b2"][0].ravel(), "b2i": L2["b2"][1].ravel()}
    return {
        "x": i["x"].reshape(B, C, HW),
        "ident": np.eye(C, dtype=np.float32),
        "mean_of": np.full((C, C), 1.0 / C, np.float32),
        "vec0": np.stack([named0[n] for n in VEC0], 1),
        "taps3": L0["pos_w"].reshape(C, 9),
        "taps5": L0["lepe_w"].reshape(C, 25),
        "wqkv": L0["qkv_w"], "wo": L0["wo_w"], "w1": L0["mlp_w1"],
        "w2": L0["mlp_w2"].reshape(HID, C, C).transpose(1, 0, 2),
        "base": chunk_bases(B),
        "woff": order(tm, tr).transpose(1, 2, 0),
        "boff": np.broadcast_to(order(L1["b_tm"], L1["b_tr"]), (TPX, 6)),
        "wdcn": L1["w_dcn"].reshape(C, C, 9).transpose(1, 2, 0),
        "group_mean": ((group[:, None] == group) / (4.0 * HW)).astype(np.float32),
        "vec2": np.stack([named2[n] for n in VEC2], 1),
        "blocks": np.stack([block_diagonal(L2[n][p]) for n in ("w1", "w2") for p in range(2)], 1),
        **transform_matrices(),
        "vec3": np.stack([L3[n] for n in VEC3], 1),
        "q_w1": L3["w1"].reshape(C, 9), "q_w2": L3["w2"].reshape(C, 9),
        "q_p1": L3["p1"].reshape(C, C).T, "q_p2": L3["p2"].reshape(C, C).T,
    }


def kernel(**inputs):
    import numpy as np
    import concourse.bacc as bacc
    from concourse.bass_utils import run_bass_kernel_spmd

    nc = bacc.Bacc("TRN2", target_bir_lowering=False, num_devices=1)
    arrays = {n: np.ascontiguousarray(a) for n, a in lay_out({n: np.ascontiguousarray(a) for n, a in inputs.items()}).items()}
    d = {n: nc.dram_tensor("in_" + n, a.shape, mybir.dt.from_np(a.dtype), kind="ExternalInput").ap() for n, a in arrays.items()}
    shape = inputs["x"].shape
    out = nc.dram_tensor("out", shape, F32, kind="ExternalOutput").ap()
    program(nc, d, out.rearrange("b c h w -> b c (h w)"))
    r = run_bass_kernel_spmd(nc, [{"in_" + n: a for n, a in arrays.items()}], core_ids=[0])
    return r.results[0]["out"]
```

```python
from contextlib import ExitStack, contextmanager

import concourse.bass as bass
from concourse import mybir

F32 = mybir.dt.float32
BF16 = mybir.dt.bfloat16
I32 = mybir.dt.int32
I16 = mybir.dt.int16
U32 = mybir.dt.uint32
ALU = mybir.AluOpType
ACT = mybir.ActivationFunctionType
AX = mybir.AxisListType

C = 128
H = W = 56
HW = H * W
HP = H + 2
CH_ROWS = 8
NCK = H // CH_ROWS
CPX = CH_ROWS * W
TPX = 2 * W
TILES = CPX // TPX
TW = W + 1
TROWS = TW * TW
ROUND = 12582912.0
GN_EPS = 1e-5
START = 8


def at(i):
    return START + i


@contextmanager
def cleared_semaphore(nc, name):
    handle = nc.alloc_semaphore(name=name)
    yield handle
    nc.clear_and_free_semaphores([handle])


def spread_phase(nc, B, x_img, ident_d, windows, table):
    with ExitStack() as ctx:
        sb = lambda name, shape, dt=F32: ctx.enter_context(nc.sbuf_tensor(name, shape, dt))
        ps = lambda name, shape, dt=F32: ctx.enter_context(nc.psum_tensor(name, shape, dt))
        sem = lambda name: ctx.enter_context(nc.semaphore(name))
        ident = sb("sp_ident", [C, C])
        flat = sb("sp_flat", [C, 2, HW])
        padded = sb("sp_padded", [C, 2, HP, HP])
        turned = sb("sp_turned", [TPX, 2, HW // TPX, C])
        zeros = sb("sp_zeros", [B, TW, 2 * C])
        bank = [ps(f"sp_bank{k}", [TPX, 4, C]) for k in range(4)]
        s_const, s_zero, s_bank, s_turned, s_padded, s_edge, s_bfree = map(
            sem, ["sp_const", "sp_zero", "sp_bank", "sp_turned", "sp_padded", "sp_edge", "sp_bfree"])
        s_loaded, s_table, s_win = ([sem(f"sp_{n}{j}") for j in range(2)] for n in ("loaded", "table", "win"))
        GROUPS = HW // TPX // 4
        tab = table.rearrange("(b y x) (k c) -> b y x k c", b=B, y=TW, k=4)
        block = ctx.enter_context(nc.Block())

        @block.sync
        def _(sp):
            sp.dma_start(ident[:], ident_d).then_inc(s_const, 16)
            with sp.Fori(0, B // 2) as pair:
                b = pair * 2
                for j in range(2):
                    sp.wait_ge(s_turned, at(b + j - 1))
                    sp.wait_ge(s_padded, at(b + j - 1))
                    sp.dma_start(flat[:, j, :], x_img[bass.ds(b + j, 1)].rearrange("o c n -> (o c) n")).then_inc(s_loaded[j], 16)

        @block.tensor
        def _(pe):
            pe.wait_ge(s_const, 16)
            with pe.Fori(0, B // 2) as pair:
                b = pair * 2
                for j in range(2):
                    pe.wait_ge(s_loaded[j], 16 * pair + 16)
                    for g in range(GROUPS):
                        pe.wait_ge(s_bfree, (b + j) * GROUPS + g + 1)
                        for k in range(4):
                            t = 4 * g + k
                            last = pe.transpose(bank[(j * GROUPS + g) % 2][:, k, :], flat[:, j, t * TPX:(t + 1) * TPX], ident[:])
                        last.then_inc(s_bank, 1)

        @block.vector
        def _(dve):
            dve.sem_inc(s_bfree, 2)
            dve.sem_inc(s_turned, START)
            with dve.Fori(0, B // 2) as pair:
                b = pair * 2
                for j in range(2):
                    dve.wait_ge(s_table[j], at(128 * pair))
                    for g in range(GROUPS):
                        dve.wait_ge(s_bank, (b + j) * GROUPS + g + 1)
                        last = dve.tensor_copy(turned[:, j, 4 * g:4 * g + 4, :], bank[(j * GROUPS + g) % 2][:])
                        last.then_inc(s_bfree, 1)
                    dve.wait_ge(s_bfree, 2 + (b + j + 1) * GROUPS)
                    dve.sem_inc(s_turned, 1)

        @block.scalar
        def _(act):
            act.wait_ge(s_zero, 2)
            act.sem_inc(s_padded, START)
            for j in range(2):
                act.sem_inc(s_win[j], START)
                act.sem_inc(s_table[j], START)
            with act.Fori(0, B // 2) as pair:
                b = pair * 2
                for j in range(2):
                    act.wait_ge(s_loaded[j], 16 * pair + 16)
                    act.wait_ge(s_win[j], at(16 * NCK * pair))
                    act.activation(padded[:, j, 1:H + 1, 1:W + 1],
                                   flat[:, j, :].rearrange("c (h w) -> c h w", w=W), ACT.Copy).then_inc(s_padded, 1)
                    act.wait_ge(s_padded, at(b + j + 1))
                    for c in range(NCK):
                        act.dma_start(windows[bass.ds((b + j) * NCK + c, 1)].rearrange("o c n -> (o c) n"),
                                      padded[:, j, CH_ROWS * c:CH_ROWS * c + 10, :].rearrange("c h w -> c (h w)")).then_inc(s_win[j], 16)
                    act.wait_ge(s_turned, at(b + j + 1))
                    for dy in range(2):
                        for dx in range(2):
                            for r in range(2):
                                rows = tab[bass.ds(b + j, 1), r + 1 - dy:r + 1 - dy + H - 1:2, 1 - dx:1 - dx + W, 2 * dy + dx, :]
                                act.dma_start(rows.rearrange("o y x c -> x (o y) c"),
                                               turned[r * W:(r + 1) * W, j, :, :]).then_inc(s_table[j], 16)
            for j in range(2):
                act.wait_ge(s_win[j], at(16 * NCK * B // 2))
                act.wait_ge(s_table[j], at(128 * B // 2))

        @block.gpsimd
        def _(pool):
            pool.memset(zeros[:], 0.0).then_inc(s_zero, 1)
            pool.memset(padded[:], 0.0).then_inc(s_zero, 1)
            pool.wait_ge(s_zero, 2)
            for y, x, k in ((0, slice(0, TW), slice(0, 2)), (H, slice(0, TW), slice(2, 4))):
                pool.dma_start(tab[:, y, x, k, :].rearrange("b x k c -> b x (k c)"), zeros[:, :, :]).then_inc(s_edge, 16)
            for x, k, y0 in ((0, 0, 1), (0, 2, 0), (W, 1, 1), (W, 3, 0)):
                pool.dma_start(tab[:, y0:y0 + H, x, k, :], zeros[:, 0:H, 0:C]).then_inc(s_edge, 16)
            pool.wait_ge(s_edge, 96)


PE_TAPS = 6
ACT_DIAGS = 13


def deform_phase(nc, N, windows, table, base_d, ident_d, woff_d, boff_d, wdcn_d, conv_out):
    with ExitStack() as ctx:
        sb = lambda name, shape, dt=F32: ctx.enter_context(nc.sbuf_tensor("df_" + name, shape, dt))
        ps = lambda name, shape, dt=F32: ctx.enter_context(nc.psum_tensor("df_" + name, shape, dt))
        ident = sb("ident", [C, C])
        woff = sb("woff", [C, 9, 6])
        boff = sb("boff", [TPX, 6])
        wdcn = sb("wdcn", [C, 9, C])
        win = sb("win", [C, CH_ROWS + 2, HP])
        base = sb("base", [TPX, 9])
        off_rows = sb("off_rows", [6, CPX])
        off = sb("off", [TPX, 3, TILES, 2])
        ctr = sb("ctr", [TPX, TILES, 2])
        row = sb("row", [TPX, 3, TILES, 2])
        pos = sb("pos", [TPX, 3, 3, TILES, 2])
        cell = sb("cell", [TPX, 9, TILES, 2])
        frac = sb("frac", [TPX, 9, TILES, 2])
        rest = sb("rest", [TPX, 9, TILES, 2])
        lin = sb("lin", [TPX, 9, TILES])
        idx_next = sb("idx_next", [TPX, TILES, 9], I32)
        wt_next = sb("wt_next", [TPX, TILES, 9, 4])
        idx = sb("idx", [TPX, TILES, 9], I32)
        wt = sb("wt", [TPX, TILES, 9, 4])
        got = sb("got", [TPX, TILES, 9, 4 * C])
        diag = sb("diag", [TPX, 2, PE_TAPS * 4, TPX])
        part = sb("part", [TPX, 2, 9 - PE_TAPS, C])
        samp = sb("samp", [C, 9, CPX])
        yout = sb("yout", [C, CPX])
        p_rows = ps("p_rows", [6, CPX])
        p_off = ps("p_off", [TPX, TILES, 3, 2])
        p_samp = [ps(f"p_samp{k}", [C, 3, TPX]) for k in range(3)]
        p_conv = ps("p_conv", [C, CPX])
        names = "const win rows rowsc offs prep idx diag diag_act parts tile sampled copied conv y stored chain issue".split()
        S = {n: ctx.enter_context(nc.semaphore("df_" + n)) for n in names}
        s_got = [ctx.enter_context(nc.semaphore(f"df_got{t}")) for t in range(TILES)]
        s_turnstile = ctx.enter_context(nc.semaphore("df_turnstile"))
        PREP = 19
        block = ctx.enter_context(nc.Block())
        count = lambda i, t: TILES * i + t

        def over_chunks(eng, body):
            with eng.Fori(0, N - 2) as i:
                body(i, 2)
            body(N - 2, 1)
            body(N - 1, 0)

        @block.sync
        def _(sp):
            for dst, src in ((ident, ident_d), (woff, woff_d), (boff, boff_d), (wdcn, wdcn_d)):
                sp.dma_start(dst[:], src).then_inc(S["const"], 16)

            def load(i):
                sp.dma_start(win[:].rearrange("c h w -> c (h w)"), windows[bass.ds(i, 1)].rearrange("o c n -> (o c) n")).then_inc(S["win"], 16)
                sp.dma_start(base[:], base_d[bass.ds(i, 1)].rearrange("o p n -> (o p) n")).then_inc(S["win"], 16)

            load(0)
            with sp.Fori(0, N - 1) as i:
                sp.wait_ge(S["prep"], at(i + 1))
                load(i + 1)

        @block.tensor
        def _(pe):
            pe.sem_inc(S["tile"], TILES)
            for n in "rows offs conv".split():
                pe.sem_inc(S[n], START)
            pe.wait_ge(S["const"], 64)

            def offset_rows(i):
                pe.wait_ge(S["win"], 32 * i + 32)
                pe.wait_ge(S["rowsc"], at(i))
                for k in range(9):
                    last = pe.matmul(p_rows[:], woff[:, k, :], win[:, k // 3:k // 3 + CH_ROWS, k % 3:k % 3 + W], start=(k == 0), stop=(k == 8))
                last.then_inc(S["rows"], 1)

            def offset_turn(i):
                pe.wait_ge(S["rowsc"], at(i + 1))
                pe.wait_ge(S["prep"], at(i))
                for t in range(TILES):
                    last = pe.matmul(p_off[:, t, :, :].rearrange("p a b -> p (a b)"), off_rows[:, t * TPX:(t + 1) * TPX], ident[0:6, 0:6],
                                     start=True, stop=True)
                last.then_inc(S["offs"], 1)

            def tile(i, t):
                n = count(i, t)
                pe.wait_ge(s_got[t], 144 * i + 144)
                pe.wait_ge(S["diag"], n + 1)
                pe.wait_ge(S["diag_act"], n + 1)
                for g in range(3):
                    pe.wait_ge(S["copied"], 3 * n + g + 1)
                    if g == PE_TAPS // 3:
                        pe.wait_ge(S["parts"], n + 1)
                    for k in range(3):
                        tap = 3 * g + k
                        if tap < PE_TAPS:
                            for c in range(4):
                                last = pe.matmul(p_samp[g][:, k, :], got[:, t, tap, c * C:(c + 1) * C], diag[:, t % 2, 4 * tap + c, :],
                                                 start=(c == 0), stop=(c == 3))
                        else:
                            last = pe.transpose(p_samp[g][:, k, :], part[:, t % 2, tap - PE_TAPS, :], ident[0:TPX, 0:TPX])
                    last.then_inc(S["sampled"], 1)
                pe.wait_ge(S["sampled"], 3 * n + 3)
                pe.sem_inc(S["tile"], 1)

            def conv(i):
                pe.wait_ge(S["copied"], 3 + 12 * i + 12)
                pe.wait_ge(S["y"], at(i))
                for k in range(9):
                    last = pe.matmul(p_conv[:], wdcn[:, k, :], samp[:, k, :], start=(k == 0), stop=(k == 8))
                last.then_inc(S["conv"], 1)

            def chunk(i, ahead):
                tile(i, 0)
                tile(i, 1)
                if ahead == 2:
                    offset_rows(i + 2)
                tile(i, 2)
                if ahead == 2:
                    offset_turn(i + 2)
                tile(i, 3)
                conv(i)

            for i in range(2):
                offset_rows(i)
                offset_turn(i)
            over_chunks(pe, chunk)

        @block.vector
        def _(dve):
            dve.wait_ge(S["const"], 64)
            dve.sem_inc(S["prep"], START)

            def prepare(i):
                n = [0]

                def step(instruction):
                    n[0] += 1
                    instruction.then_inc(S["chain"], 1)
                    dve.wait_ge(S["chain"], PREP * i + n[0])

                dve.wait_ge(S["offs"], at(i + 1))
                dve.wait_ge(S["win"], 32 * i + 32)
                step(dve.tensor_tensor(off[:].rearrange("p k t j -> p t k j"), p_off[:],
                                       boff[:].rearrange("p (k j) -> p k j", j=2).unsqueeze(1).to_broadcast([TPX, TILES, 3, 2]), ALU.add))
                step(dve.tensor_tensor(ctr[:], off[:, 2], base[:, 0:8].rearrange("p (t j) -> p t j", j=2), ALU.add))
                step(dve.tensor_tensor(row[:, 0], ctr[:], off[:, 0], ALU.subtract))
                step(dve.tensor_copy(row[:, 1], ctr[:]))
                step(dve.tensor_tensor(row[:, 2], ctr[:], off[:, 0], ALU.add))
                rows = row[:].rearrange("p k t j -> p k (t j)")
                side = off[:, 1].rearrange("p t j -> p (t j)").unsqueeze(1).to_broadcast([TPX, 3, 2 * TILES])
                for kx, op in ((0, ALU.subtract), (2, ALU.add)):
                    step(dve.tensor_tensor(pos[:, :, kx].rearrange("p k t j -> p k (t j)"), rows, side, op))
                step(dve.tensor_copy(pos[:, :, 1].rearrange("p k t j -> p k (t j)"), rows))
                flat = lambda a: a.rearrange("p a t j -> p (a t j)")
                p = pos[:].rearrange("p a b t j -> p (a b t j)")
                step(dve.tensor_scalar(p, p, 0.0, float(W + 1), ALU.max, ALU.min))
                step(dve.tensor_scalar(flat(cell[:]), p, 0.5, 0.0, ALU.subtract, ALU.max))
                step(dve.tensor_scalar(flat(cell[:]), flat(cell[:]), ROUND, ROUND, ALU.add, ALU.subtract))
                step(dve.tensor_tensor(flat(frac[:]), p, flat(cell[:]), ALU.subtract))
                step(dve.tensor_scalar(flat(rest[:]), flat(frac[:]), -1.0, 1.0, ALU.mult, ALU.add))
                step(dve.scalar_tensor_tensor(out=lin[:], in0=cell[:, :, :, 0], scalar=float(TW), in1=cell[:, :, :, 1], op0=ALU.mult, op1=ALU.add))
                step(dve.tensor_scalar(idx_next[:].rearrange("p t k -> p k t"), lin[:], base[:, 8:9], None, ALU.add))
                for c, (a, b) in enumerate(((rest, rest), (rest, frac), (frac, rest), (frac, frac))):
                    step(dve.tensor_tensor(wt_next[:, :, :, c].rearrange("p t k -> p k t"), a[:, :, :, 0], b[:, :, :, 1], ALU.mult))
                assert n[0] == PREP
                dve.sem_inc(S["prep"], 1)

            def publish(i, t):
                dve.tensor_copy(idx[:, t, :], idx_next[:, t, :]).then_inc(S["idx"], 1)
                dve.tensor_copy(wt[:, t], wt_next[:, t]).then_inc(S["idx"], 1)

            def diagonals(i, t):
                n = count(i, t)
                dve.wait_ge(S["idx"], 2 * n + 2)
                dve.wait_ge(S["tile"], n + 3)
                for m in range(ACT_DIAGS, 4 * PE_TAPS):
                    last = dve.tensor_scalar(diag[:, t % 2, m, :], ident[0:TPX, 0:TPX], wt[:, t, m // 4, m % 4:m % 4 + 1], None, ALU.mult)
                last.then_inc(S["diag"], 1)

            def weigh(i, t):
                n = count(i, t)
                K = 9 - PE_TAPS
                dve.wait_ge(s_got[t], 144 * i + 144)
                dve.wait_ge(S["tile"], n + 3)
                for c in range(4):
                    for k in range(K):
                        tap = PE_TAPS + k
                        src, weight = got[:, t, tap, c * C:(c + 1) * C], wt[:, t, tap, c:c + 1]
                        if c == 0:
                            last = dve.tensor_scalar(part[:, t % 2, k, :], src, weight, None, ALU.mult)
                        else:
                            last = dve.scalar_tensor_tensor(out=part[:, t % 2, k, :], in0=src, scalar=weight, in1=part[:, t % 2, k, :],
                                                            op0=ALU.mult, op1=ALU.add)
                    if c < 3:
                        last.then_inc(S["issue"], 1)
                        dve.wait_ge(S["issue"], 3 * n + c + 1)
                last.then_inc(S["parts"], 1)

            def chunk(i, ahead):
                for t in range(TILES):
                    weigh(i, t)
                    if t + 1 < TILES:
                        diagonals(i, t + 1)
                    elif ahead:
                        diagonals(i + 1, 0)
                    if ahead:
                        dve.wait_ge(S["parts"], count(i, t) + 1)
                        dve.wait_ge(S["diag_act"], count(i, t) + 1)
                        publish(i + 1, t)
                if ahead == 2:
                    dve.wait_ge(S["idx"], 2 * count(i + 2, 0))
                    prepare(i + 2)

            prepare(0)
            for t in range(TILES):
                publish(0, t)
            dve.wait_ge(S["idx"], 2 * TILES)
            prepare(1)
            diagonals(0, 0)
            over_chunks(dve, chunk)

        @block.gpsimd
        def _(pool):
            with pool.Fori(0, N) as i:
                for t in range(TILES):
                    pool.wait_ge(S["idx"], 2 * count(i, t) + 1)
                    pool.wait_ge(S["tile"], count(i, t) + 1)
                    pool.sem_inc(s_turnstile, 1)
                    for k in range(9):
                        pool.indirect_dma_start(out=got[:, t, k, :], out_offset=None, in_=table[:, :],
                                                in_offset=bass.IndirectOffsetOnAxis(ap=idx[:, t, k:k + 1], axis=0)).then_inc(s_got[t], 16)

        @block.scalar
        def _(act):
            act.sem_inc(S["copied"], 3)
            for n in "y stored rowsc".split():
                act.sem_inc(S[n], START)
            act.wait_ge(S["const"], 64)

            def diagonals(i, t):
                n = count(i, t)
                act.wait_ge(S["idx"], 2 * n + 2)
                act.wait_ge(S["tile"], n + 3)
                for m in range(ACT_DIAGS):
                    last = act.activation(diag[:, t % 2, m, :], ident[0:TPX, 0:TPX], ACT.Copy, scale=wt[:, t, m // 4, m % 4:m % 4 + 1])
                last.then_inc(S["diag_act"], 1)

            def copy_rows(i):
                act.wait_ge(S["rows"], at(i + 1))
                act.wait_ge(S["offs"], at(i))
                act.activation(off_rows[:], p_rows[:], ACT.Copy).then_inc(S["rowsc"], 1)

            def copy_samples(i, t):
                for g in range(3):
                    act.wait_ge(S["sampled"], 3 * count(i, t) + g + 1)
                    if t == 0 and g == 0:
                        act.wait_ge(S["conv"], at(i))
                    act.activation(samp[:, 3 * g:3 * g + 3, t * TPX:(t + 1) * TPX], p_samp[g][:], ACT.Copy).then_inc(S["copied"], 1)

            def chunk(i, ahead):
                for t in range(TILES):
                    if t + 1 < TILES:
                        diagonals(i, t + 1)
                    copy_samples(i, t)
                    if t == 1 and ahead == 2:
                        copy_rows(i + 2)
                if ahead:
                    diagonals(i + 1, 0)
                act.wait_ge(S["conv"], at(i + 1))
                act.wait_ge(S["stored"], at(16 * i))
                act.activation(yout[:], p_conv[:], ACT.Copy).then_inc(S["y"], 1)
                act.wait_ge(S["y"], at(i + 1))
                act.dma_start(conv_out[bass.ds(i, 1)].rearrange("o c n -> (o c) n"), yout[:]).then_inc(S["stored"], 16)

            for i in range(2):
                copy_rows(i)
            diagonals(0, 0)
            over_chunks(act, chunk)
            act.wait_ge(S["stored"], at(16 * N))


def chunk_bases(B):
    import numpy as np
    base = np.zeros((B * NCK, TPX, 9), np.float32)
    p = np.arange(TPX)
    for i in range(B * NCK):
        b, c = divmod(i, NCK)
        for t in range(TILES):
            base[i, :, 2 * t] = CH_ROWS * c + 2 * t + p // W + 1
            base[i, :, 2 * t + 1] = p % W + 1
        base[i, :, 8] = b * TROWS
    return base
WIN = 8
NWIN = H // WIN
NW = NWIN * NWIN
WPX = WIN * WIN
HEADS = 4
HD = C // HEADS
TOPK = 4
DVE_TAPS = 11
HID = 3
LN_EPS = 1e-6
QSCALE = float(C) ** -0.5


def attention_phase(nc, B, x_d, w, out_img):
    with ExitStack() as ctx:
        ctx.callback(nc.all_engine_barrier)
        sb = lambda name, shape, dt=F32: ctx.enter_context(nc.sbuf_tensor("at_" + name, shape, dt))
        ps = lambda name, shape, dt=F32: ctx.enter_context(nc.psum_tensor("at_" + name, shape, dt))
        sem = lambda name: ctx.enter_context(cleared_semaphore(nc, "at_" + name))
        ident = sb("ident", [C, C])
        mean_of = sb("mean_of", [C, C])
        vec = sb("vec", [C, len(VEC0)])
        taps3 = sb("taps3", [C, 9])
        taps5 = sb("taps5", [C, 25])
        diag3 = sb("diag3", [C, 9, C])
        diag5 = sb("diag5", [C, 25, C])
        wqkv = sb("wqkv", [C, 3 * C])
        wo = sb("wo", [C, C])
        w1 = sb("w1", [C, HID * C])
        w2 = sb("w2", [C, HID, C])
        eps = sb("eps", [C, 1])
        flat = sb("flat", [C, HW])
        padded = sb("padded", [C, HP, HP])
        x1 = sb("x1", [C, HW])
        dev = sb("dev", [C, HW])
        y = sb("y", [C, NW, WPX])
        kv = sb("kv", [C, NW, 2, WPX])
        vpad = sb("vpad", [C, H + 4, W + 4])
        oimg = sb("oimg", [C, HW])
        sq = sb("sq", [C, 2, CPX])
        std = sb("std", [C, 2, CPX])
        ysum = sb("ysum", [C, NW])
        qm = sb("qm", [C, NW])
        km = sb("km", [C, NW])
        logit = sb("logit", [NW, NW])
        top = sb("top", [NW, 8])
        top_at = sb("top_at", [NW, 8], U32)
        chosen = sb("chosen", [1, NW * TOPK], U32)
        qz = sb("qz", [C, NWIN, HEADS, WPX])
        kvsel = sb("kvsel", [C, 2, 2, TOPK, WPX])
        prob = sb("prob", [C, 2, 2, TOPK * WPX])
        probT = sb("probT", [C, 2, 4, C])
        vT = sb("vT", [C, 2, 2, C])
        nmax = sb("nmax", [C, 2, 2])
        tot = sb("tot", [C, 2, 2])
        inv = sb("inv", [C, 2, 2])
        orow = sb("orow", [C, WIN, W])
        hid = sb("hid", [C, 2, HID, CPX])
        bank = [ps(f"bank{k}", [C, 512]) for k in range(8)]

        names = ("const zero log log2 tapped diag load padfree pad conv x1 mean dev sq var std rn y kv kcopy vcopy vpad ysum qkm qkmc logit lcopy "
                 "top topidx issue sel q qz s vt vtc nb exp rec pn pt ptc pv oc lepe orow osum wo x2 mean2 dev2 sq2 var2 std2 rn2 z "
                 "m1 gelu m2 fin stored chosen").split()
        S = {n: sem(n) for n in names}
        block = ctx.enter_context(nc.Block())

        def before(w):
            return {0: 1, 1: 3}.get(w, 2)

        def ck(c):
            return slice(c * CPX, (c + 1) * CPX)

        V = {n: vec[:, k:k + 1] for k, n in enumerate(VEC0)}

        @block.sync
        def _(sp):
            for dst, src in ((ident, w["ident"]), (mean_of, w["mean_of"]), (vec, w["vec0"]), (taps3, w["taps3"]), (taps5, w["taps5"]),
                             (wqkv, w["wqkv"]), (wo, w["wo"]), (w1, w["w1"]), (w2, w["w2"])):
                sp.dma_start(dst[:], src).then_inc(S["const"], 16)
            def load(b):
                sp.dma_start(flat[:], x_d[bass.ds(b, 1)].rearrange("o c n -> (o c) n")).then_inc(S["load"], 16)

            load(0)

            def serve(b, more):
                if more:
                    sp.wait_ge(S["padfree"], at(b + 1))
                    load(b + 1)
                sp.wait_ge(S["topidx"], at(b + 1))
                sp.dma_start(chosen[:].rearrange("o (w k) -> o w k", k=TOPK), top_at[:, 0:TOPK]).then_inc(S["chosen"], 16)
                sp.wait_ge(S["fin"], at(NCK * (b + 1)))
                sp.dma_start(out_img[bass.ds(b, 1)].rearrange("o c n -> (o c) n"), oimg[:]).then_inc(S["stored"], 16)

            with sp.Fori(0, B - 1) as b:
                serve(b, True)
            serve(B - 1, False)
            sp.wait_ge(S["stored"], 16 * B + START)

        @block.gpsimd
        def _(pool):
            pool.memset(vpad[:], 0.0).then_inc(S["zero"], 1)
            pool.memset(padded[:], 0.0).then_inc(S["zero"], 1)
            pool.memset(qz[:], 0.0).then_inc(S["zero"], 1)
            pool.memset(eps[:], LN_EPS).then_inc(S["zero"], 1)
            pool.sem_inc(S["sel"], START)
            pool.sem_inc(S["stored"], START)
            with pool.Fori(0, B) as b:
                pool.wait_ge(S["chosen"], 16 * b + 16)
                pool.wait_ge(S["vcopy"], at(NCK * (b + 1)))
                pool.sem_inc(S["issue"], 1)
                with pool.Fori(0, NWIN) as r:
                    for v in range(NWIN):
                        n = b * NW + r * NWIN + v
                        pool.wait_ge(S["vt"], at(n - before(v) + 1))
                        pool.sem_inc(S["issue"], 1)
                        for k in range(TOPK):
                            src = pool.value_load(chosen[0:1, bass.ds(r * (NWIN * TOPK) + (v * TOPK + k), 1)], min_val=0, max_val=NW - 1)
                            last = pool.tensor_copy(kvsel[:, v % 2, :, k, :], kv[:, bass.ds(src, 1), :, :].rearrange("c o t p -> c (o t) p"))
                        last.then_inc(S["sel"], 1)

        @block.tensor
        def _(pe):
            for n in ("conv mean var kv qkm logit q s vt pt pv lepe wo mean2 var2 m1 m2".split()):
                pe.sem_inc(S[n], START)
            pe.wait_ge(S["diag"], 34)
            pe.wait_ge(S["const"], 144)

            def conv(b, c):
                if c >= 2:
                    pe.wait_ge(S["x1"], at(NCK * b + c - 1))
                for k in range(9):
                    last = pe.matmul(bank[c % 2][:, 0:CPX], diag3[:, k, :],
                                     padded[:, WIN * c + k // 3:WIN * c + k // 3 + WIN, k % 3:k % 3 + W], start=(k == 0), stop=(k == 8))
                last.then_inc(S["conv"], 1)

            def mean(b, c):
                pe.wait_ge(S["x1"], at(NCK * b + c + 1))
                if c >= 2:
                    pe.wait_ge(S["dev"], at(NCK * b + c - 1))
                pe.matmul(bank[2 + c % 2][:, 0:CPX], mean_of[:], x1[:, ck(c)], start=True, stop=True).then_inc(S["mean"], 1)

            def var(b, c):
                pe.wait_ge(S["sq"], at(NCK * b + c + 1))
                if c >= 2:
                    pe.wait_ge(S["std"], at(NCK * b + c - 1))
                pe.matmul(bank[4 + c % 2][:, 0:CPX], mean_of[:], sq[:, c % 2, :], start=True, stop=True).then_inc(S["var"], 1)

            def keys_values(b, c):
                pe.wait_ge(S["y"], at(NCK * b + c + 1))
                if c >= 1:
                    pe.wait_ge(S["vcopy"], at(NCK * b + c))
                    pe.wait_ge(S["vpad"], at(NCK * b + c))
                for t in range(2):
                    last = pe.matmul(bank[6 + t][:, 0:CPX], wqkv[:, (1 + t) * C:(2 + t) * C],
                                     y[:, NWIN * c:NWIN * (c + 1), :], start=True, stop=True)
                last.then_inc(S["kv"], 1)

            def choose(b):
                pe.wait_ge(S["ysum"], at(b + 1))
                for t in range(2):
                    last = pe.matmul(bank[t][:, 0:NW], wqkv[:, t * C:(t + 1) * C], ysum[:], start=True, stop=True)
                last.then_inc(S["qkm"], 1)
                pe.wait_ge(S["qkmc"], at(2 * b + 2))
                pe.matmul(bank[2][0:NW, 0:NW], qm[:], km[:], start=True, stop=True).then_inc(S["logit"], 1)

            def scores(b, r, v):
                n = b * NW + r * NWIN + v
                pe.wait_ge(S["sel"], at(n + 1))
                pe.wait_ge(S["exp"], at(n - before(v) + 1))
                for g in range(2):
                    last = pe.matmul(bank[1 + v % 2][:, g * 256:(g + 1) * 256], qz[:, v, 2 * g:2 * g + 2, :].rearrange("c h p -> c (h p)"),
                                     kvsel[:, v % 2, 0, :, :].rearrange("c k p -> c (k p)"), start=True, stop=True)
                last.then_inc(S["s"], 1)
                pe.wait_ge(S["vtc"], at(n))
                for g in range(2):
                    last = pe.transpose(bank[3][:, g * C:(g + 1) * C],
                                        kvsel[:, v % 2, 1, 2 * g:2 * g + 2, :].rearrange("c k p -> c (k p)"), ident[:])
                last.then_inc(S["vt"], 1)

            def turn_probs(b, r, v):
                n = b * NW + r * NWIN + v
                pe.wait_ge(S["pn"], at(n + 1))
                pe.wait_ge(S["ptc"], at(n - before(v) + 1))
                for kh in range(2):
                    for g in range(2):
                        last = pe.transpose(bank[4 + v % 2][:, (2 * kh + g) * C:(2 * kh + g + 1) * C],
                                            prob[:, v % 2, g, kh * C:(kh + 1) * C], ident[:])
                last.then_inc(S["pt"], 1)

            def weigh_values(b, r, v):
                n = b * NW + r * NWIN + v
                pe.wait_ge(S["ptc"], at(n + 1))
                pe.wait_ge(S["vtc"], at(n + 1))
                pe.wait_ge(S["oc"], at(n))
                for kh in range(2):
                    last = pe.matmul(bank[6][:, 0:256], vT[:, v % 2, kh, :],
                                     probT[:, v % 2, 2 * kh:2 * kh + 2, :].rearrange("c g p -> c (g p)"), start=(kh == 0), stop=(kh == 1))
                last.then_inc(S["pv"], 1)

            def lepe(b, r, k):
                if k == DVE_TAPS:
                    pe.wait_ge(S["osum"], at(NCK * b + r))
                mm = pe.matmul(bank[7][:, 0:CPX], diag5[:, k, :], vpad[:, bass.ds(r * WIN + k // 5, WIN), k % 5:k % 5 + W],
                               start=(k == DVE_TAPS), stop=(k == 24))
                if k == 24:
                    mm.then_inc(S["lepe"], 1)

            def out_proj(b, c):
                if c >= 2:
                    pe.wait_ge(S["x2"], at(NCK * b + c - 1))
                pe.matmul(bank[c % 2][:, 0:CPX], wo[:], oimg[:, ck(c)], start=True, stop=True).then_inc(S["wo"], 1)

            def mean2(b, c):
                pe.wait_ge(S["x2"], at(NCK * b + c + 1))
                if c >= 1:
                    pe.wait_ge(S["dev2"], at(NCK * b + c))
                pe.matmul(bank[2][:, 0:CPX], mean_of[:], dev[:, ck(c)], start=True, stop=True).then_inc(S["mean2"], 1)

            def var2(b, c):
                pe.wait_ge(S["sq2"], at(NCK * b + c + 1))
                if c >= 2:
                    pe.wait_ge(S["std2"], at(NCK * b + c - 1))
                pe.matmul(bank[3 + c % 2][:, 0:CPX], mean_of[:], sq[:, c % 2, :], start=True, stop=True).then_inc(S["var2"], 1)

            z = y[:].rearrange("c w p -> c (w p)")

            def mlp_in(b, c):
                if c >= 1:
                    pe.wait_ge(S["gelu"], at(NCK * b + c))
                for j in range(HID):
                    last = pe.matmul(bank[4 + j][:, 0:CPX], w1[:, j * C:(j + 1) * C], z[:, ck(c)], start=True, stop=True)
                last.then_inc(S["m1"], 1)

            def mlp_out(b, c):
                pe.wait_ge(S["gelu"], at(NCK * b + c + 1))
                if c >= 2:
                    pe.wait_ge(S["fin"], at(NCK * b + c - 1))
                for j in range(HID):
                    last = pe.matmul(bank[7 if c % 2 else 3][:, 0:CPX], w2[:, j, :], hid[:, c % 2, j, :], start=(j == 0), stop=(j == HID - 1))
                last.then_inc(S["m2"], 1)

            with pe.Fori(0, B) as b:
                pe.wait_ge(S["pad"], b + 1)
                for c in range(NCK + 3):
                    if c < NCK:
                        conv(b, c)
                    if c == 1:
                        pe.wait_ge(S["fin"], at(NCK * b))
                    if 1 <= c <= NCK:
                        mean(b, c - 1)
                    if 2 <= c <= NCK + 1:
                        var(b, c - 2)
                    if c >= 3:
                        keys_values(b, c - 3)
                choose(b)
                pe.wait_ge(S["vcopy"], at(NCK * (b + 1)))
                pe.wait_ge(S["vpad"], at(NCK * (b + 1)))
                pe.sem_inc(S["issue"], 1)
                with pe.Fori(0, NWIN) as r:
                    pe.wait_ge(S["qz"], at(NCK * b + r))
                    pe.matmul(bank[0][:, 0:CPX], wqkv[:, 0:C],
                              y[:, bass.ds(r * NWIN, NWIN), :], start=True, stop=True).then_inc(S["q"], 1)
                    pe.wait_ge(S["qz"], at(NCK * b + r + 1))
                    tap = DVE_TAPS
                    for v in range(NWIN + 2):
                        if v < NWIN:
                            scores(b, r, v)
                        while tap < min(25, DVE_TAPS + 2 * (v + 1)):
                            lepe(b, r, tap)
                            tap += 1
                        if 1 <= v <= NWIN:
                            turn_probs(b, r, v - 1)
                        if v >= 2:
                            weigh_values(b, r, v - 2)
                pe.wait_ge(S["osum"], at(NCK * (b + 1)))
                for c in range(NCK + 2):
                    if c < NCK:
                        out_proj(b, c)
                    if 1 <= c <= NCK:
                        mean2(b, c - 1)
                    if c >= 2:
                        var2(b, c - 2)
                pe.wait_ge(S["z"], at(NCK * (b + 1)))
                for c in range(NCK + 1):
                    if c < NCK:
                        mlp_in(b, c)
                    if c >= 1:
                        mlp_out(b, c - 1)

        @block.vector
        def _(dve):
            for n in ("tapped x1 dev rn y vpad ysum qkmc lcopy top topidx qz vtc nb rec pn oc orow osum x2 dev2 rn2 z fin".split()):
                dve.sem_inc(S[n], START)
            dve.wait_ge(S["const"], 144)
            for k in range(9):
                dve.tensor_scalar(diag3[:, k, :], ident[:], taps3[:, k:k + 1], None, ALU.mult).then_inc(S["diag"], 1)
            for k in range(25):
                dve.tensor_scalar(diag5[:, k, :], ident[:], taps5[:, k:k + 1], None, ALU.mult).then_inc(S["diag"], 1)
            dve.wait_ge(S["zero"], 4)

            rows = lambda a, c: a[:, ck(c)].rearrange("c (h w) -> c h w", w=W)
            z = y[:].rearrange("c w p -> c (w p)")

            def residual(b, c):
                dve.wait_ge(S["conv"], at(NCK * b + c + 1))
                dve.scalar_tensor_tensor(out=rows(x1, c), in0=bank[c % 2][:, 0:CPX].rearrange("c (h w) -> c h w", w=W), scalar=V["pos_b"],
                                         in1=padded[:, WIN * c + 1:WIN * c + 1 + WIN, 1:W + 1], op0=ALU.add, op1=ALU.add).then_inc(S["x1"], 1)

            def deviation(b, c):
                dve.wait_ge(S["mean"], at(NCK * b + c + 1))
                dve.tensor_tensor(dev[:, ck(c)], x1[:, ck(c)], bank[2 + c % 2][:, 0:CPX], ALU.subtract).then_inc(S["dev"], 1)

            def norm(b, c):
                i = NCK * b + c + 1
                dve.wait_ge(S["std"], at(i))
                dve.tensor_tensor(dev[:, ck(c)], dev[:, ck(c)], std[:, c % 2, :], ALU.mult).then_inc(S["rn"], 1)
                dve.wait_ge(S["rn"], at(i))
                dve.tensor_scalar(y[:, NWIN * c:NWIN * (c + 1), :].rearrange("c v (r q) -> c v r q", q=WIN),
                                  dev[:, ck(c)].rearrange("c (r v q) -> c v r q", r=WIN, v=NWIN),
                                  V["ln1_g"], V["ln1_b"], ALU.mult, ALU.add).then_inc(S["y"], 1)

            def image_values(b, c):
                dve.wait_ge(S["vcopy"], at(NCK * b + c + 1))
                dve.tensor_scalar(vpad[:, WIN * c + 2:WIN * (c + 1) + 2, 2:W + 2].rearrange("c r (v q) -> c v r q", q=WIN),
                                  bank[7][:, 0:CPX].rearrange("c (v r q) -> c v r q", r=WIN, q=WIN), V["v_b"], None, ALU.add).then_inc(S["vpad"], 1)

            def choose(b):
                dve.wait_ge(S["y"], at(NCK * (b + 1)))
                dve.tensor_reduce(ysum[:], y[:], AX.X, ALU.add).then_inc(S["ysum"], 1)
                dve.wait_ge(S["qkm"], at(b + 1))
                dve.tensor_scalar(qm[:], bank[0][:, 0:NW], 1.0 / WPX, V["q_b"], ALU.mult, ALU.add).then_inc(S["qkmc"], 1)
                dve.tensor_scalar(km[:], bank[1][:, 0:NW], 1.0 / WPX, V["k_b"], ALU.mult, ALU.add).then_inc(S["qkmc"], 1)
                dve.wait_ge(S["logit"], at(b + 1))
                dve.tensor_scalar(logit[:], bank[2][0:NW, 0:NW], QSCALE, None, ALU.mult).then_inc(S["lcopy"], 1)
                dve.wait_ge(S["lcopy"], at(b + 1))
                dve.sem_inc(S["issue"], 1)
                dve.max(top[:], logit[:]).then_inc(S["top"], 1)
                dve.wait_ge(S["top"], at(b + 1))
                dve.sem_inc(S["issue"], 1)
                dve.max_index(top_at[:], top[:], logit[:]).then_inc(S["topidx"], 1)

            def queries(b, r):
                dve.wait_ge(S["q"], at(NCK * b + r + 1))
                dve.wait_ge(S["s"], at(NW * b + NWIN * r))
                for h in range(HEADS):
                    p = slice(HD * h, HD * (h + 1))
                    last = dve.tensor_scalar(qz[p, :, h, :], bank[0][p, 0:CPX].rearrange("c (v p) -> c v p", p=WPX),
                                             vec[p, VEC0.index("q_b"):VEC0.index("q_b") + 1], QSCALE, ALU.add, ALU.mult)
                last.then_inc(S["qz"], 1)

            def score_max(b, r, v):
                n = b * NW + r * NWIN + v
                dve.wait_ge(S["s"], at(n + 1))
                dve.wait_ge(S["exp"], at(n - before(v) + 1))
                dve.tensor_reduce(nmax[:, v % 2, :], bank[1 + v % 2][:].rearrange("c (g k) -> c g k", g=2), AX.X, ALU.max,
                                  negate=True).then_inc(S["nb"], 1)

            def turned_values(b, r, v):
                n = b * NW + r * NWIN + v
                dve.wait_ge(S["vt"], at(n + 1))
                dve.wait_ge(S["pv"], at(n - before(v) + 1))
                dve.tensor_copy(vT[:, v % 2].rearrange("c g p -> c (g p)"), bank[3][:, 0:2 * C]).then_inc(S["vtc"], 1)

            def normalise(b, r, v):
                n = b * NW + r * NWIN + v
                dve.wait_ge(S["exp"], at(n + 1))
                dve.reciprocal(inv[:, v % 2, :], tot[:, v % 2, :]).then_inc(S["rec"], 1)
                dve.wait_ge(S["rec"], at(n + 1))
                for g in range(2):
                    last = dve.tensor_scalar(prob[:, v % 2, g, :], prob[:, v % 2, g, :], inv[:, v % 2, g:g + 1], None, ALU.mult)
                last.then_inc(S["pn"], 1)

            def outputs(b, r, v):
                n = b * NW + r * NWIN + v
                dve.wait_ge(S["pv"], at(n + 1))
                dve.wait_ge(S["tapped"], at(DVE_TAPS * (NCK * b + r) + taps_by(v + 2)))
                for h in range(HEADS):
                    p = slice(HD * h, HD * (h + 1))
                    here = orow[p, :, WIN * v:WIN * (v + 1)]
                    last = dve.tensor_tensor(here, here, bank[6][p, h * WPX:(h + 1) * WPX].rearrange("c (r q) -> c r q", q=WIN), ALU.add)
                last.then_inc(S["oc"], 1)

            def taps_by(step):
                return min(DVE_TAPS, 2 * (step + 1))

            def tap(b, r, k, done):
                src = vpad[:, bass.ds(r * WIN + k // 5, WIN), k % 5:k % 5 + W]
                if k == 0:
                    dve.wait_ge(S["osum"], at(NCK * b + r))
                    dve.tensor_scalar(orow[:], src, taps5[:, 0:1], V["lepe_b"], ALU.mult, ALU.add).then_inc(S["tapped"], 1)
                else:
                    dve.wait_ge(S["tapped"], at(DVE_TAPS * (NCK * b + r) + k))
                    if done > 0:
                        dve.wait_ge(S["oc"], at(NW * b + NWIN * r + done))
                    dve.scalar_tensor_tensor(out=orow[:], in0=src, scalar=taps5[:, k:k + 1], in1=orow[:], op0=ALU.mult, op1=ALU.add)\
                       .then_inc(S["tapped"], 1)

            def row_sum(b, r):
                dve.wait_ge(S["lepe"], at(NCK * b + r + 1))
                dve.wait_ge(S["oc"], at(NW * b + NWIN * r + NWIN))
                dve.tensor_tensor(oimg[:, bass.ds(r * CPX, CPX)], bank[7][:, 0:CPX], orow[:].rearrange("c r w -> c (r w)"),
                                  ALU.add).then_inc(S["osum"], 1)

            def residual2(b, c):
                dve.wait_ge(S["wo"], at(NCK * b + c + 1))
                dve.scalar_tensor_tensor(out=dev[:, ck(c)], in0=bank[c % 2][:, 0:CPX], scalar=V["wo_b"], in1=x1[:, ck(c)],
                                         op0=ALU.add, op1=ALU.add).then_inc(S["x2"], 1)

            def deviation2(b, c):
                dve.wait_ge(S["mean2"], at(NCK * b + c + 1))
                dve.tensor_tensor(z[:, ck(c)], dev[:, ck(c)], bank[2][:, 0:CPX], ALU.subtract).then_inc(S["dev2"], 1)

            def norm2(b, c):
                i = NCK * b + c + 1
                dve.wait_ge(S["std2"], at(i))
                dve.tensor_tensor(z[:, ck(c)], z[:, ck(c)], std[:, c % 2, :], ALU.mult).then_inc(S["rn2"], 1)
                dve.wait_ge(S["rn2"], at(i))
                dve.tensor_scalar(z[:, ck(c)], z[:, ck(c)], V["ln2_g"], V["ln2_b"], ALU.mult, ALU.add).then_inc(S["z"], 1)

            def finish(b, c):
                dve.wait_ge(S["m2"], at(NCK * b + c + 1))
                dve.scalar_tensor_tensor(out=oimg[:, ck(c)], in0=bank[7 if c % 2 else 3][:, 0:CPX], scalar=V["mlp_b2"], in1=dev[:, ck(c)],
                                         op0=ALU.add, op1=ALU.add).then_inc(S["fin"], 1)

            with dve.Fori(0, B) as b:
                dve.wait_ge(S["pad"], b + 1)
                for c in range(NCK + 3):
                    if c < NCK:
                        residual(b, c)
                    if 1 <= c <= NCK:
                        deviation(b, c - 1)
                    if 2 <= c <= NCK + 1:
                        norm(b, c - 2)
                    if c >= 3:
                        image_values(b, c - 3)
                choose(b)
                with dve.Fori(0, NWIN) as r:
                    queries(b, r)
                    for v in range(NWIN + 2):
                        for k in range(taps_by(v - 1) if v else 0, taps_by(v)):
                            tap(b, r, k, max(0, v - 2))
                        if v < NWIN:
                            score_max(b, r, v)
                        if 1 <= v <= NWIN:
                            normalise(b, r, v - 1)
                        if v < NWIN:
                            turned_values(b, r, v)
                        if v >= 2:
                            outputs(b, r, v - 2)
                    dve.wait_ge(S["stored"], 16 * b + START)
                    dve.sem_inc(S["issue"], 1)
                    row_sum(b, r)
                for c in range(NCK + 2):
                    if c < NCK:
                        residual2(b, c)
                    if 1 <= c <= NCK:
                        deviation2(b, c - 1)
                    if c >= 2:
                        norm2(b, c - 2)
                for c in range(NCK):
                    finish(b, c)

        @block.scalar
        def _(act):
            for n in ("sq std log log2 kcopy vcopy exp ptc sq2 std2 gelu padfree".split()):
                act.sem_inc(S[n], START)
            act.wait_ge(S["zero"], 4)
            act.wait_ge(S["const"], 144)
            z = y[:].rearrange("c w p -> c (w p)")

            def square(b, c):
                act.wait_ge(S["dev"], at(NCK * b + c + 1))
                if c >= 2:
                    act.wait_ge(S["var"], at(NCK * b + c - 1))
                act.activation(sq[:, c % 2, :], dev[:, ck(c)], ACT.Square).then_inc(S["sq"], 1)

            def deviate(b, c):
                act.wait_ge(S["var"], at(NCK * b + c + 1))
                if c >= 2:
                    act.wait_ge(S["rn"], at(NCK * b + c - 1))
                act.activation(std[:, c % 2, :], bank[4 + c % 2][:, 0:CPX], ACT.Ln, bias=eps[:]).then_inc(S["log"], 1)
                act.wait_ge(S["log"], at(NCK * b + c + 1))
                act.activation(std[:, c % 2, :], std[:, c % 2, :], ACT.Exp, scale=-0.5).then_inc(S["std"], 1)

            def copy_kv(b, c):
                act.wait_ge(S["kv"], at(NCK * b + c + 1))
                for t, s, bias in ((0, "kcopy", "k_b"), (1, "vcopy", "v_b")):
                    act.activation(kv[:, NWIN * c:NWIN * (c + 1), t, :], bank[6 + t][:, 0:CPX].rearrange("c (v p) -> c v p", p=WPX),
                                   ACT.Identity, bias=V[bias]).then_inc(S[s], 1)

            def exponent(b, r, v):
                n = b * NW + r * NWIN + v
                act.wait_ge(S["nb"], at(n + 1))
                act.wait_ge(S["pt"], at(n - before(v) + 1))
                for g in range(2):
                    last = act.activation(prob[:, v % 2, g, :], bank[1 + v % 2][:, g * 256:(g + 1) * 256], ACT.Exp,
                                          bias=nmax[:, v % 2, g:g + 1], accum_out=tot[:, v % 2, g:g + 1])
                last.then_inc(S["exp"], 1)

            def copy_probs(b, r, v):
                n = b * NW + r * NWIN + v
                act.wait_ge(S["pt"], at(n + 1))
                act.wait_ge(S["pv"], at(n - before(v) + 1))
                act.activation(probT[:, v % 2].rearrange("c g p -> c (g p)"), bank[4 + v % 2][:], ACT.Copy).then_inc(S["ptc"], 1)

            def square2(b, c):
                act.wait_ge(S["dev2"], at(NCK * b + c + 1))
                if c >= 2:
                    act.wait_ge(S["var2"], at(NCK * b + c - 1))
                act.activation(sq[:, c % 2, :], z[:, ck(c)], ACT.Square).then_inc(S["sq2"], 1)

            def deviate2(b, c):
                act.wait_ge(S["var2"], at(NCK * b + c + 1))
                if c >= 2:
                    act.wait_ge(S["rn2"], at(NCK * b + c - 1))
                act.activation(std[:, c % 2, :], bank[3 + c % 2][:, 0:CPX], ACT.Ln, bias=eps[:]).then_inc(S["log2"], 1)
                act.wait_ge(S["log2"], at(NCK * b + c + 1))
                act.activation(std[:, c % 2, :], std[:, c % 2, :], ACT.Exp, scale=-0.5).then_inc(S["std2"], 1)

            def gelu(b, c):
                act.wait_ge(S["m1"], at(NCK * b + c + 1))
                if c >= 2:
                    act.wait_ge(S["m2"], at(NCK * b + c - 1))
                for j in range(HID):
                    last = act.activation(hid[:, c % 2, j, :], bank[4 + j][:, 0:CPX], ACT.Gelu, bias=V[f"mlp_b1_{j}"])
                last.then_inc(S["gelu"], 1)

            def pad(b):
                act.wait_ge(S["load"], 16 * b + 16)
                act.activation(padded[:, 1:H + 1, 1:W + 1], flat[:].rearrange("c (h w) -> c h w", w=W), ACT.Copy).then_inc(S["pad"], 1)
                act.wait_ge(S["pad"], b + 1)
                act.sem_inc(S["padfree"], 1)

            def image(b, more):
                for c in range(NCK + 3):
                    if 1 <= c <= NCK:
                        square(b, c - 1)
                    if 2 <= c <= NCK + 1:
                        deviate(b, c - 2)
                    if c >= 3:
                        copy_kv(b, c - 3)
                with act.Fori(0, NWIN) as r:
                    for v in range(NWIN + 1):
                        if v < NWIN:
                            exponent(b, r, v)
                        if v >= 1:
                            copy_probs(b, r, v - 1)
                if more:
                    act.wait_ge(S["x1"], at(NCK * (b + 1)))
                    pad(b + 1)
                for c in range(NCK + 2):
                    if 1 <= c <= NCK:
                        square2(b, c - 1)
                    if c >= 2:
                        deviate2(b, c - 2)
                for c in range(NCK):
                    gelu(b, c)

            pad(0)
            with act.Fori(0, B - 1) as b:
                image(b, True)
            image(B - 1, False)



VEC0 = ["pos_b", "ln1_g", "ln1_b", "q_b", "k_b", "v_b", "lepe_b", "wo_b", "ln2_g", "ln2_b", "mlp_b2", "mlp_b1_0", "mlp_b1_1", "mlp_b1_2"]
KX = W // 2 + 1
SHRINK = 0.01
KXG = [(0, 8), (8, 8), (16, 8), (24, KX - 24)]
STAGES = [("fw", HW // TPX), ("fh", KX), ("ih", KX), ("iw", HW // TPX)]


def groups_of_four(units):
    return [(k, min(4, units - k)) for k in range(0, units, 4)]


def fourier_phase(nc, B, conv_d, x_img, w, out_img, peak_d):
    with ExitStack() as ctx:
        sb = lambda name, shape, dt=F32: ctx.enter_context(nc.sbuf_tensor("fo_" + name, shape, dt))
        ps = lambda name, shape, dt=F32: ctx.enter_context(nc.psum_tensor("fo_" + name, shape, dt))
        sem = lambda name: ctx.enter_context(nc.semaphore("fo_" + name))
        ident = sb("ident", [C, C])
        group_mean = sb("group_mean", [C, C])
        vec = sb("vec", [C, len(VEC2)])
        V = {n: vec[:, k:k + 1] for k, n in enumerate(VEC2)}
        mats = {"fw": sb("m_fw", [2 * W, 4 * KX]), "fh": sb("m_fh", [2 * H, 2 * H]), "ih": sb("m_ih", [2 * H, 2 * H]), "iw": sb("m_iw", [4 * KX, 2 * W])}
        blocks = sb("blocks", [C, 4, C])
        minus = sb("minus", [C, 2, C])
        eps = sb("eps", [C, 1])
        conv = sb("conv", [C, NCK, CPX])
        xin = sb("xin", [C, HW])
        scratch = sb("scratch", [C, HW])
        img = sb("img", [C, HW])
        half = sb("half", [C, KX * H * 2])
        freq = sb("freq", [C, 2, KX, H])
        mixed = sb("mixed", [C, KX, 2, H])
        res = sb("res", [C, HW])
        turned = sb("turned", [C, 2, 4, C])
        hid = sb("hid", [C, 2, 2, 448])
        val = sb("val", [C, 2, 2, 448])
        cut = sb("cut", [C, 2, 448])
        pro = sb("pro", [C, 2, 448])
        prx = sb("prx", [C, 2, 448])
        stat = sb("stat", [C, 8])
        peak = sb("peak", [C, 2])
        bank = [ps(f"bank{k}", [C, 512]) for k in range(8)]
        names = ("const zero load loadfree sum sq m1 m2 small gn relu turn turnc prod prodc l1 relu1 l2 val shrunk cut pr yr px yi "
                 "peak stored neg issue root").split()
        S = {n: sem(n) for n in names}
        block = ctx.enter_context(nc.Block())
        GR = sum(len(groups_of_four(u)) for _, u in STAGES)
        first = {}
        k = 0
        for name, u in STAGES:
            first[name] = k
            k += len(groups_of_four(u))
        MX = len(KXG)

        def dest(name, g0, m):
            if name == "fw":
                return half[:].rearrange("c (k h p) -> c k (h p)", k=KX, p=2)[:, :, 4 * g0:4 * (g0 + m)].rearrange("c k (t q) -> c t k q", q=4)
            if name == "fh":
                return freq[:, :, g0:g0 + m, :].rearrange("c p k y -> c k p y")
            if name == "ih":
                return half[:].rearrange("c (h k p) -> c k h p", k=KX, p=2)[:, g0:g0 + m, :, :]

        def columns(name, g, m):
            n = mats[name].shape[1]
            b = bank[2 + (first[name] + g) % 2][:, 0:m * n]
            if name == "fw":
                return b.rearrange("c (t k q) -> c t k q", t=m, q=4)
            if name == "fh":
                return b.rearrange("c (k p y) -> c k p y", k=m, p=2)
            if name == "ih":
                return b.rearrange("c (k h p) -> c k h p", k=m, p=2)
            return b

        def unit(name, t):
            if name == "fw":
                return img[:, t * TPX:(t + 1) * TPX]
            if name == "fh":
                return half[:, t * 2 * H:(t + 1) * 2 * H]
            if name == "ih":
                return mixed[:, t, :, :].rearrange("c p y -> c (p y)")
            return half[:, t * 4 * KX:(t + 1) * 4 * KX]

        @block.sync
        def _(sp):
            for dst, src in ((ident, "ident"), (group_mean, "group_mean"), (vec, "vec2"), (mats["fw"], "dft_fw"), (mats["fh"], "dft_fh"),
                             (mats["ih"], "dft_ih"), (mats["iw"], "dft_iw"), (blocks, "blocks")):
                sp.dma_start(dst[:], w[src]).then_inc(S["const"], 16)
            with sp.Fori(0, B) as b:
                sp.wait_ge(S["gn"], at(b))
                sp.dma_start(conv[:], conv_d[bass.ds(b, 1)].rearrange("o k c n -> c (o k) n")).then_inc(S["load"], 16)
                sp.dma_start(xin[:], x_img[bass.ds(b, 1)].rearrange("o c n -> (o c) n")).then_inc(S["load"], 16)

        @block.gpsimd
        def _(pool):
            pool.memset(eps[:], GN_EPS).then_inc(S["zero"], 1)
            pool.memset(peak[:], 0.0).then_inc(S["zero"], 1)
            pool.sem_inc(S["px"], START)
            pool.sem_inc(S["yi"], START)
            with pool.Fori(0, B) as b:
                for m, (k0, kn) in enumerate(KXG):
                    n = kn * H
                    part = lambda a: a.rearrange("c k y -> c (k y)")
                    pool.wait_ge(S["shrunk"], at(MX * b + m + 1))
                    pool.wait_ge(S["yi"], at(MX * b + m))
                    pool.tensor_tensor(prx[:, 0, 0:n], val[:, m % 2, 0, 0:n], part(freq[:, 1, k0:k0 + kn, :]), ALU.mult)
                    pool.tensor_tensor(prx[:, 1, 0:n], val[:, m % 2, 1, 0:n], part(freq[:, 0, k0:k0 + kn, :]), ALU.mult).then_inc(S["px"], 1)
                    pool.wait_ge(S["px"], at(MX * b + m + 1))
                    pool.tensor_tensor(mixed[:, k0:k0 + kn, 1, :], prx[:, 0, 0:n].rearrange("c (k y) -> c k y", y=H),
                                       prx[:, 1, 0:n].rearrange("c (k y) -> c k y", y=H), ALU.add).then_inc(S["yi"], 1)

        @block.tensor
        def _(pe):
            for n in "m1 m2 turn prod l1 l2".split():
                pe.sem_inc(S[n], START)
            pe.wait_ge(S["const"], 128)
            pe.wait_ge(S["neg"], 1)

            def turn(b, name, g):
                n = GR * b + first[name] + g
                g0, m = groups_of_four(dict(STAGES)[name])[g]
                pe.wait_ge(S["turnc"], at(n - 1))
                for k in range(m):
                    src = unit(name, g0 + k)
                    last = pe.transpose(bank[(first[name] + g) % 2][0:src.shape[1], k * C:(k + 1) * C], src, ident[:])
                last.then_inc(S["turn"], 1)

            def product(b, name, g):
                n = GR * b + first[name] + g
                g0, m = groups_of_four(dict(STAGES)[name])[g]
                rows, cols = mats[name].shape
                pe.wait_ge(S["turnc"], at(n + 1))
                pe.wait_ge(S["prodc"], at(n - 1))
                for k in range(m):
                    last = pe.matmul(bank[2 + (first[name] + g) % 2][:, k * cols:(k + 1) * cols],
                                     turned[0:rows, (first[name] + g) % 2, k, :], mats[name][:], start=True, stop=True)
                last.then_inc(S["prod"], 1)

            def transform(b, name):
                G = len(groups_of_four(dict(STAGES)[name]))
                for g in range(G + 1):
                    if g < G:
                        turn(b, name, g)
                    if g >= 1:
                        product(b, name, g - 1)

            def mix_first(b, m):
                k0, kn = KXG[m]
                n = kn * H
                part = lambda p: freq[:, p, k0:k0 + kn, :].rearrange("c k y -> c (k y)")
                pe.wait_ge(S["relu1"], at(MX * b + m))
                for o, terms in enumerate((((blocks[:, 0], 0), (minus[:, 0], 1)), ((blocks[:, 0], 1), (blocks[:, 1], 0)))):
                    for k, (mat, p) in enumerate(terms):
                        last = pe.matmul(bank[4 + o][:, 0:n], mat, part(p), start=(k == 0), stop=(k == 1))
                last.then_inc(S["l1"], 1)

            def mix_second(b, m):
                k0, kn = KXG[m]
                n = kn * H
                pe.wait_ge(S["relu1"], at(MX * b + m + 1))
                pe.wait_ge(S["val"], at(MX * b + m))
                for o, terms in enumerate((((blocks[:, 2], 0), (minus[:, 1], 1)), ((blocks[:, 2], 1), (blocks[:, 3], 0)))):
                    for k, (mat, p) in enumerate(terms):
                        last = pe.matmul(bank[6 + o][:, 0:n], mat, hid[:, m % 2, p, 0:n], start=(k == 0), stop=(k == 1))
                last.then_inc(S["l2"], 1)

            with pe.Fori(0, B) as b:
                pe.wait_ge(S["sum"], at(b + 1))
                pe.wait_ge(S["peak"], at(b))
                pe.matmul(bank[4][:, 0:1], group_mean[:], stat[:, 0:1], start=True, stop=True).then_inc(S["m1"], 1)
                pe.wait_ge(S["sq"], at(b + 1))
                pe.matmul(bank[5][:, 0:1], group_mean[:], stat[:, 2:3], start=True, stop=True).then_inc(S["m2"], 1)
                pe.wait_ge(S["relu"], at(b + 1))
                transform(b, "fw")
                pe.wait_ge(S["prodc"], at(GR * b + first["fh"]))
                transform(b, "fh")
                pe.wait_ge(S["prodc"], at(GR * b + first["ih"]))
                for m in range(MX + 1):
                    if m < MX:
                        mix_first(b, m)
                    if m >= 1:
                        mix_second(b, m - 1)
                pe.wait_ge(S["yr"], at(MX * (b + 1)))
                pe.wait_ge(S["yi"], at(MX * (b + 1)))
                transform(b, "ih")
                pe.wait_ge(S["prodc"], at(GR * b + first["iw"]))
                transform(b, "iw")

        @block.vector
        def _(dve):
            for n in "small gn prodc shrunk cut pr yr peak".split():
                dve.sem_inc(S[n], START)
            dve.wait_ge(S["const"], 128)
            dve.wait_ge(S["zero"], 2)
            dve.tensor_scalar(minus[:, 0], blocks[:, 1], -1.0, None, ALU.mult)
            dve.tensor_scalar(minus[:, 1], blocks[:, 3], -1.0, None, ALU.mult).then_inc(S["neg"], 1)

            def collect(b, name):
                for g, (g0, m) in enumerate(groups_of_four(dict(STAGES)[name])):
                    n = GR * b + first[name] + g
                    dve.wait_ge(S["prod"], at(n + 1))
                    if name == "iw":
                        px = slice(g0 * TPX, (g0 + m) * TPX)
                        dve.tensor_tensor(res[:, px], columns(name, g, m), img[:, px], ALU.add).then_inc(S["prodc"], 1)
                    else:
                        dve.tensor_copy(dest(name, g0, m), columns(name, g, m)).then_inc(S["prodc"], 1)

            def shrink(b, m):
                k0, kn = KXG[m]
                n = kn * H
                i = MX * b + m + 1
                v = val[:, m % 2, :, 0:n]
                dve.wait_ge(S["val"], at(i))
                dve.tensor_scalar(cut[:, :, 0:n], v, SHRINK, -SHRINK, ALU.min, ALU.max).then_inc(S["cut"], 1)
                dve.wait_ge(S["cut"], at(i))
                dve.tensor_tensor(v, v, cut[:, :, 0:n], ALU.subtract).then_inc(S["shrunk"], 1)
                dve.wait_ge(S["shrunk"], at(i))
                dve.tensor_tensor(pro[:, :, 0:n], v, freq[:, :, k0:k0 + kn, :].rearrange("c p k y -> c p (k y)"), ALU.mult).then_inc(S["pr"], 1)
                dve.wait_ge(S["pr"], at(i))
                dve.tensor_tensor(mixed[:, k0:k0 + kn, 0, :], pro[:, 0, 0:n].rearrange("c (k y) -> c k y", y=H),
                                  pro[:, 1, 0:n].rearrange("c (k y) -> c k y", y=H), ALU.subtract).then_inc(S["yr"], 1)

            with dve.Fori(0, B) as b:
                def small(k, instruction):
                    instruction.then_inc(S["small"], 1)
                    dve.wait_ge(S["small"], at(5 * b + k))

                dve.wait_ge(S["m1"], at(b + 1))
                small(1, dve.tensor_scalar(stat[:, 1:2], bank[4][:, 0:1], -1.0, None, ALU.mult))
                dve.wait_ge(S["relu"], at(b))
                dve.wait_ge(S["load"], 32 * b + 32)
                dve.wait_ge(S["m2"], at(b + 1))
                dve.wait_ge(S["root"], b + 1)
                small(2, dve.reciprocal(stat[:, 4:5], stat[:, 3:4]))
                small(3, dve.tensor_tensor(stat[:, 5:6], stat[:, 4:5], V["gamma"], ALU.mult))
                small(4, dve.scalar_tensor_tensor(out=stat[:, 6:7], in0=stat[:, 5:6], scalar=stat[:, 1:2], in1=V["beta"], op0=ALU.mult, op1=ALU.add))
                dve.scalar_tensor_tensor(out=img[:], in0=conv[:].rearrange("c k n -> c (k n)"), scalar=stat[:, 5:6], in1=xin[:],
                                         op0=ALU.mult, op1=ALU.add).then_inc(S["gn"], 1)
                collect(b, "fw")
                collect(b, "fh")
                for m in range(MX):
                    shrink(b, m)
                collect(b, "ih")
                dve.wait_ge(S["stored"], 16 * b + START)
                collect(b, "iw")
                dve.wait_ge(S["prodc"], at(GR * (b + 1)))
                small(5, dve.tensor_reduce(peak[:, 1:2], res[:], AX.X, ALU.max, apply_absolute_value=True))
                dve.tensor_tensor(peak[:, 0:1], peak[:, 0:1], peak[:, 1:2], ALU.max).then_inc(S["peak"], 1)

        @block.scalar
        def _(act):
            for n in "sum sq relu turnc relu1 val stored".split():
                act.sem_inc(S[n], START)
            act.wait_ge(S["const"], 128)
            act.wait_ge(S["zero"], 2)

            def copy_turned(b, name):
                for g, (g0, m) in enumerate(groups_of_four(dict(STAGES)[name])):
                    n = GR * b + first[name] + g
                    rows = mats[name].shape[0]
                    act.wait_ge(S["turn"], at(n + 1))
                    act.wait_ge(S["prod"], at(n - 1))
                    act.activation(turned[0:rows, (first[name] + g) % 2, 0:m, :], bank[(first[name] + g) % 2][0:rows, 0:m * C].rearrange("r (k c) -> r k c", c=C),
                                   ACT.Copy).then_inc(S["turnc"], 1)

            def mix(b):
                for m in range(MX + 1):
                    if m < MX:
                        n = KXG[m][1] * H
                        act.wait_ge(S["l1"], at(MX * b + m + 1))
                        if m >= 2:
                            act.wait_ge(S["l2"], at(MX * b + m - 1))
                        act.activation(hid[:, m % 2, 0, 0:n], bank[4][:, 0:n], ACT.Relu, bias=V["b1r"])
                        act.activation(hid[:, m % 2, 1, 0:n], bank[5][:, 0:n], ACT.Relu, bias=V["b1i"]).then_inc(S["relu1"], 1)
                    if m >= 1:
                        j = m - 1
                        n = KXG[j][1] * H
                        act.wait_ge(S["l2"], at(MX * b + j + 1))
                        if j >= 2:
                            act.wait_ge(S["yr"], at(MX * b + j - 1))
                            act.wait_ge(S["yi"], at(MX * b + j - 1))
                        act.activation(val[:, j % 2, 0, 0:n], bank[6][:, 0:n], ACT.Identity, bias=V["b2r"])
                        act.activation(val[:, j % 2, 1, 0:n], bank[7][:, 0:n], ACT.Identity, bias=V["b2i"]).then_inc(S["val"], 1)

            with act.Fori(0, B) as b:
                act.wait_ge(S["load"], 32 * b + 32)
                act.activation(scratch[:], conv[:].rearrange("c k n -> c (k n)"), ACT.Copy, accum_out=stat[:, 0:1]).then_inc(S["sum"], 1)
                act.wait_ge(S["small"], at(5 * b + 1))
                act.wait_ge(S["sum"], at(b + 1))
                act.activation(scratch[:], conv[:].rearrange("c k n -> c (k n)"), ACT.Square, bias=stat[:, 1:2], accum_out=stat[:, 2:3]).then_inc(S["sq"], 1)
                act.wait_ge(S["m2"], at(b + 1))
                act.activation(stat[:, 3:4], bank[5][:, 0:1], ACT.Sqrt, bias=eps[:]).then_inc(S["root"], 1)
                act.wait_ge(S["gn"], at(b + 1))
                act.activation(img[:], img[:], ACT.Relu, bias=stat[:, 6:7]).then_inc(S["relu"], 1)
                copy_turned(b, "fw")
                copy_turned(b, "fh")
                mix(b)
                copy_turned(b, "ih")
                copy_turned(b, "iw")
                act.wait_ge(S["prodc"], at(GR * (b + 1)))
                act.dma_start(out_img[bass.ds(b, 1)].rearrange("o c n -> (o c) n"), res[:]).then_inc(S["stored"], 16)
            act.wait_ge(S["peak"], at(B))
            act.wait_ge(S["stored"], 16 * B + START)
            act.dma_start(peak_d, peak[:, 0:1]).then_inc(S["stored"], 16)
            act.wait_ge(S["stored"], 16 * B + 16 + START)


VEC2 = ["gamma", "beta", "b1r", "b1i", "b2r", "b2i"]


def transform_matrices():
    import numpy as np
    n = np.arange(W)
    root = np.sqrt(float(W))
    fw = np.zeros((2, W, KX, 2, 2))
    ang = 2 * np.pi * np.outer(n, np.arange(KX)) / W
    for r in range(2):
        fw[r, :, :, r, 0] = np.cos(ang) / root
        fw[r, :, :, r, 1] = -np.sin(ang) / root
    ang = 2 * np.pi * np.outer(n, n) / H
    co, si = np.cos(ang) / root, np.sin(ang) / root
    fh = np.zeros((H, 2, 2, H))
    fh[:, 0, 0], fh[:, 0, 1], fh[:, 1, 0], fh[:, 1, 1] = co, -si, si, co
    ih = np.zeros((2, H, H, 2))
    ih[0, :, :, 0], ih[0, :, :, 1], ih[1, :, :, 0], ih[1, :, :, 1] = co, si, -si, co
    iw = np.zeros((2, KX, 2, 2, W))
    ang = 2 * np.pi * np.outer(np.arange(KX), n) / W
    weight = np.full((KX, 1), 2.0)
    weight[0] = weight[-1] = 1.0
    sine = np.sin(ang)
    sine[0] = sine[-1] = 0.0
    for r in range(2):
        iw[r, :, 0, r] = weight * np.cos(ang) / root
        iw[r, :, 1, r] = -weight * sine / root
    f = lambda a, r, c: np.ascontiguousarray(a.reshape(r, c).astype(np.float32))
    return {"dft_fw": f(fw, 2 * W, 4 * KX), "dft_fh": f(fh, 2 * H, 2 * H), "dft_ih": f(ih, 2 * H, 2 * H), "dft_iw": f(iw, 4 * KX, 2 * W)}
Q8, Q4 = 127.0, 7.0
VEC3 = ["b1", "pb1", "b2", "pb2"]


def quantised_phase(nc, B, x_img, peak_d, w, out_img):
    with ExitStack() as ctx:
        sb = lambda name, shape, dt=F32: ctx.enter_context(nc.sbuf_tensor("qu_" + name, shape, dt))
        ps = lambda name, shape, dt=F32: ctx.enter_context(nc.psum_tensor("qu_" + name, shape, dt))
        ident = sb("ident", [C, C])
        vec = sb("vec", [C, len(VEC3)])
        V = {n: vec[:, k:k + 1] for k, n in enumerate(VEC3)}
        raw = {"w1": sb("raw_w1", [C, 9]), "p1": sb("raw_p1", [C, C]), "w2": sb("raw_w2", [C, 9]), "p2": sb("raw_p2", [C, C])}
        whole = {n: sb("whole_" + n, list(a.shape)) for n, a in raw.items()}
        point = {n: sb("point_" + n, [C, C], BF16) for n in ("p1", "p2")}
        diag = {n: sb("diag_" + n, [C, 9, C], BF16) for n in ("w1", "w2")}
        peaks = sb("peaks", [C, 5])
        tops = sb("tops", [C, 5])
        scale = sb("scale", [C, 5])
        inv = sb("inv", [C, 5])
        hi = sb("hi", [C, 2])
        lo = sb("lo", [C, 2])
        few = sb("few", [C, 16])
        held = sb("held", [C, B * HW], I16)
        held_q = held[:].bitcast(BF16)
        xin = sb("xin", [C, 2, HW])
        real = sb("real", [C, 2, HW])
        padded = sb("padded", [C, 2, HP, HP], BF16)
        quant = sb("quant", [C, 2, HW], BF16)
        relued = sb("relued", [C, 4, CPX])
        chunk_hi = sb("chunk_hi", [C, NCK])
        bank = [ps(f"bank{k}", [C, 512]) for k in range(8)]
        ck = lambda c: slice(c * CPX, (c + 1) * CPX)
        back4 = lambda c: {0: 3, 1: 3, 2: 3, 3: NCK}.get(c, 4)
        img = lambda b: bass.ds(b * HW, HW)
        rows = lambda a: a.rearrange("c (h w) -> c h w", w=W)

        def scales(name, program):
            with ExitStack() as inner:
                s_step = inner.enter_context(nc.semaphore(f"qu_{name}_step"))
                s_ask = inner.enter_context(nc.semaphore(f"qu_{name}_ask"))
                s_top = inner.enter_context(nc.semaphore(f"qu_{name}_top"))
                s_in = inner.enter_context(nc.semaphore(f"qu_{name}_in"))
                block = inner.enter_context(nc.Block())
                loads, before, width, after = program

                @block.sync
                def _(sp):
                    for dst, src in loads:
                        sp.dma_start(dst, src).then_inc(s_in, 16)

                @block.gpsimd
                def _(pool):
                    if name == "start":
                        pool.memset(padded[:], 0.0).then_inc(s_in, 1)
                    pool.wait_ge(s_ask, 1)
                    pool.partition_all_reduce(tops[:, 0:width], peaks[:, 0:width], C, bass.bass_isa.ReduceOp.max).then_inc(s_top, 1)

                @block.vector
                def _(dve):
                    count = [0]

                    def step(instruction):
                        count[0] += 1
                        instruction.then_inc(s_step, 1)
                        dve.wait_ge(s_step, count[0])

                    dve.wait_ge(s_in, 16 * len(loads) + (name == "start"))
                    before(dve, step)
                    dve.sem_inc(s_ask, 1)
                    dve.wait_ge(s_top, 1)
                    after(dve, step)

        def start_before(dve, step):
            for k, n in enumerate(("w1", "p1", "w2", "p2")):
                step(dve.tensor_reduce(peaks[:, k + 1:k + 2], raw[n][:], AX.X, ALU.max, apply_absolute_value=True))

        def start_after(dve, step):
            step(dve.tensor_scalar(scale[:, 0:1], tops[:, 0:1], 1.0 / Q8, 1e-8, ALU.mult, ALU.max))
            step(dve.tensor_scalar(scale[:, 1:5], tops[:, 1:5], 1.0 / Q4, 1e-8, ALU.mult, ALU.max))
            step(dve.reciprocal(inv[:], scale[:]))
            for k, n in enumerate(("w1", "p1", "w2", "p2")):
                q = whole[n][:]
                step(dve.tensor_scalar(q, raw[n][:], inv[:, k + 1:k + 2], ROUND, ALU.mult, ALU.add))
                step(dve.tensor_scalar(q, q, ROUND, Q4, ALU.subtract, ALU.min))
                if n in point:
                    step(dve.tensor_scalar(point[n][:], q, -Q4 - 1.0, None, ALU.max))
                else:
                    step(dve.tensor_scalar(q, q, -Q4 - 1.0, None, ALU.max))
                    for t in range(9):
                        step(dve.tensor_scalar(diag[n][:, t, :], ident[:], q[:, t:t + 1], None, ALU.mult))
            step(dve.tensor_tensor(few[:, 0:1], scale[:, 0:1], scale[:, 1:2], ALU.mult))

        def ends_before(bias):
            def before(dve, step):
                step(dve.scalar_tensor_tensor(out=few[:, 2:3], in0=hi[:, 0:1], scalar=few[:, 0:1], in1=V[bias], op0=ALU.mult, op1=ALU.add))
                step(dve.scalar_tensor_tensor(out=few[:, 3:4], in0=lo[:, 0:1], scalar=few[:, 0:1], in1=V[bias], op0=ALU.mult, op1=ALU.add))
                step(dve.tensor_reduce(peaks[:, 0:1], few[:, 2:4], AX.X, ALU.max, apply_absolute_value=True))
            return before

        def relu_before(bias):
            def before(dve, step):
                step(dve.scalar_tensor_tensor(out=few[:, 2:3], in0=hi[:, 0:1], scalar=few[:, 0:1], in1=V[bias], op0=ALU.mult, op1=ALU.add))
                step(dve.tensor_scalar(peaks[:, 0:1], few[:, 2:3], 0.0, None, ALU.max))
            return before

        def next_after(bias, k):
            def after(dve, step):
                step(dve.tensor_scalar(scale[:, 0:1], tops[:, 0:1], 1.0 / Q8, 1e-8, ALU.mult, ALU.max))
                step(dve.reciprocal(inv[:, 0:1], scale[:, 0:1]))
                step(dve.tensor_tensor(few[:, 4:5], few[:, 0:1], inv[:, 0:1], ALU.mult))
                step(dve.tensor_tensor(few[:, 5:6], V[bias], inv[:, 0:1], ALU.mult))
                step(dve.tensor_tensor(few[:, 0:1], scale[:, 0:1], scale[:, k:k + 1], ALU.mult))
            return after

        def sums_pass(first):
            with ExitStack() as inner:
                tag = "a" if first else "c"
                names = "load real quant sums copied point best free issue".split()
                S = {n: inner.enter_context(nc.semaphore(f"qu_{tag}_{n}")) for n in names}
                s_load = [inner.enter_context(nc.semaphore(f"qu_{tag}_load{j}")) for j in range(2)]
                block = inner.enter_context(nc.Block())
                dw = diag["w1" if first else "w2"]

                if first:
                    @block.sync
                    def _(sp):
                        with sp.Fori(0, B // 2) as pair:
                            for j in range(2):
                                b = pair * 2 + j
                                sp.wait_ge(S["real"], at(b - 1))
                                sp.dma_start(xin[:, j, :], x_img[bass.ds(b, 1)].rearrange("o c n -> (o c) n")).then_inc(s_load[j], 16)

                @block.tensor
                def _(pe):
                    pe.sem_inc(S["sums"], START)
                    pe.sem_inc(S["point"], START)
                    with pe.Fori(0, B // 2) as pair:
                        for j in range(2):
                            b = pair * 2 + j
                            if not first:
                                for c in range(NCK):
                                    pe.wait_ge(S["real"], at(NCK * b + c - back4(c) + 1))
                                    pe.matmul(bank[c % 4][:, 0:CPX], point["p1"][:], held_q[:, bass.ds(b * HW + c * CPX, CPX)],
                                              start=True, stop=True).then_inc(S["point"], 1)
                            pe.wait_ge(S["quant"], at((b + 1) * (1 if first else NCK)))
                            for c in range(NCK):
                                pe.wait_ge(S["copied"], at(NCK * b + c - back4(c) + 1))
                                for k in range(9):
                                    last = pe.matmul(bank[4 + c % 4][:, 0:CPX], dw[:, k, :],
                                                     padded[:, j, WIN * c + k // 3:WIN * c + k // 3 + WIN, k % 3:k % 3 + W], start=(k == 0), stop=(k == 8))
                                last.then_inc(S["sums"], 1)

                @block.scalar
                def _(act):
                    act.sem_inc(S["real"], START)
                    act.sem_inc(S["copied"], START)

                    def collect(b):
                        act.wait_ge(S["best"], at(b))
                        for c in range(NCK):
                            act.wait_ge(S["sums"], at(NCK * b + c + 1))
                            act.sem_inc(S["issue"], 1)
                            act.activation(held[:, bass.ds(b * HW + c * CPX, CPX)], bank[4 + c % 4][:, 0:CPX], ACT.Copy).then_inc(S["copied"], 1)

                    with act.Fori(0, B // 2) as pair:
                        for j in range(2):
                            b = pair * 2 + j
                            if first:
                                act.wait_ge(s_load[j], 16 * pair + 16)
                                act.wait_ge(S["quant"], at(b - 1))
                                act.activation(real[:, j, :], xin[:, j, :], ACT.Copy, scale=inv[:, 0:1]).then_inc(S["real"], 1)
                            else:
                                for c in range(NCK):
                                    act.wait_ge(S["point"], at(NCK * b + c + 1))
                                    act.wait_ge(S["quant"], at(NCK * b + c - NCK + 1))
                                    act.activation(real[:, 0, ck(c)], bank[c % 4][:, 0:CPX], ACT.Relu, bias=few[:, 5:6], scale=few[:, 4:5]).then_inc(S["real"], 1)
                            collect(b)

                @block.vector
                def _(dve):
                    dve.sem_inc(S["quant"], START)
                    dve.sem_inc(S["best"], START)
                    dve.memset(hi[:], -3.0e38).then_inc(S["free"], 1)
                    dve.memset(lo[:], 3.0e38).then_inc(S["free"], 1)
                    dve.wait_ge(S["free"], 2)

                    def search(b):
                        dve.wait_ge(S["copied"], at(NCK * (b + 1)))
                        dve.tensor_reduce(hi[:, 1:2], held[:, img(b)], AX.X, ALU.max).then_inc(S["free"], 1)
                        dve.tensor_reduce(lo[:, 1:2], held[:, img(b)], AX.X, ALU.min).then_inc(S["free"], 1)
                        dve.wait_ge(S["free"], 4 * b + 4)
                        dve.tensor_tensor(hi[:, 0:1], hi[:, 0:1], hi[:, 1:2], ALU.max).then_inc(S["free"], 1)
                        dve.tensor_tensor(lo[:, 0:1], lo[:, 0:1], lo[:, 1:2], ALU.min).then_inc(S["free"], 1)
                        dve.wait_ge(S["free"], 4 * b + 6)
                        dve.sem_inc(S["best"], 1)

                    with dve.Fori(0, B // 2) as pair:
                        for j in range(2):
                            b = pair * 2 + j
                            dve.wait_ge(S["sums"], at(NCK * b - NCK))
                            if first:
                                dve.wait_ge(S["real"], at(b + 1))
                                dve.tensor_scalar(padded[:, j, 1:H + 1, 1:W + 1], rows(real[:, j, :]), ROUND, ROUND, ALU.add, ALU.subtract).then_inc(S["quant"], 1)
                            else:
                                for c in range(NCK):
                                    dve.wait_ge(S["real"], at(NCK * b + c + 1))
                                    dve.tensor_scalar(padded[:, j, WIN * c + 1:WIN * (c + 1) + 1, 1:W + 1], rows(real[:, 0, ck(c)]),
                                                      ROUND, ROUND, ALU.add, ALU.subtract).then_inc(S["quant"], 1)
                            search(b)

        def peak_pass():
            with ExitStack() as inner:
                S = {n: inner.enter_context(nc.semaphore(f"qu_b_{n}")) for n in "real quant point best free issue".split()}
                block = inner.enter_context(nc.Block())

                @block.scalar
                def _(act):
                    act.sem_inc(S["real"], START)
                    with act.Fori(0, B // 2) as pair:
                        for j in range(2):
                            b = pair * 2 + j
                            act.wait_ge(S["quant"], at(b - 1))
                            act.sem_inc(S["issue"], 1)
                            act.activation(real[:, j, :], held[:, img(b)], ACT.Identity, bias=few[:, 5:6], scale=few[:, 4:5]).then_inc(S["real"], 1)

                @block.tensor
                def _(pe):
                    pe.sem_inc(S["point"], START)
                    with pe.Fori(0, B) as b:
                        pe.wait_ge(S["quant"], at(b + 1))
                        for c in range(NCK):
                            pe.wait_ge(S["best"], at(NCK * b + c - NCK + 1))
                            pe.matmul(bank[c][:, 0:CPX], point["p1"][:], held_q[:, bass.ds(b * HW + c * CPX, CPX)],
                                      start=True, stop=True).then_inc(S["point"], 1)

                @block.vector
                def _(dve):
                    dve.sem_inc(S["quant"], START)
                    dve.sem_inc(S["best"], START)
                    dve.memset(hi[:], -3.0e38).then_inc(S["free"], 1)
                    dve.wait_ge(S["free"], 1)
                    with dve.Fori(0, B // 2) as pair:
                        for j in range(2):
                            b = pair * 2 + j
                            dve.wait_ge(S["real"], at(b + 1))
                            dve.tensor_scalar(held_q[:, img(b)], real[:, j, :], ROUND, ROUND, ALU.add, ALU.subtract).then_inc(S["quant"], 1)
                            for c in range(NCK):
                                dve.wait_ge(S["point"], at(NCK * b + c + 1))
                                dve.tensor_reduce(chunk_hi[:, c:c + 1], bank[c][:, 0:CPX], AX.X, ALU.max).then_inc(S["best"], 1)
                            dve.wait_ge(S["best"], at(NCK * (b + 1)))
                            dve.tensor_reduce(hi[:, 1:2], chunk_hi[:], AX.X, ALU.max).then_inc(S["free"], 1)
                            dve.wait_ge(S["free"], 2 * b + 2)
                            dve.tensor_tensor(hi[:, 0:1], hi[:, 0:1], hi[:, 1:2], ALU.max).then_inc(S["free"], 1)
                            dve.wait_ge(S["free"], 2 * b + 3)

        def last_pass():
            with ExitStack() as inner:
                S = {n: inner.enter_context(nc.semaphore(f"qu_d_{n}")) for n in "real quant point relued added issue".split()}
                s_load = [inner.enter_context(nc.semaphore(f"qu_d_load{j}")) for j in range(2)]
                s_stored = [inner.enter_context(nc.semaphore(f"qu_d_stored{j}")) for j in range(2)]
                block = inner.enter_context(nc.Block())

                @block.gpsimd
                def _(pool):
                    for j in range(2):
                        pool.sem_inc(s_stored[j], START)
                    with pool.Fori(0, B // 2) as pair:
                        for j in range(2):
                            b = pair * 2 + j
                            pool.wait_ge(s_stored[j], at(16 * pair))
                            pool.sem_inc(S["issue"], 1)
                            pool.dma_start(xin[:, j, :], x_img[bass.ds(b, 1)].rearrange("o c n -> (o c) n")).then_inc(s_load[j], 16)

                @block.scalar
                def _(act):
                    act.sem_inc(S["real"], START)
                    act.sem_inc(S["relued"], START)

                    def scaled(b, j):
                        act.wait_ge(S["quant"], at(b - 1))
                        act.sem_inc(S["issue"], 1)
                        act.activation(real[:, j, :], held[:, img(b)], ACT.Identity, bias=few[:, 5:6], scale=few[:, 4:5]).then_inc(S["real"], 1)

                    with act.Fori(0, B // 2) as pair:
                        for j in range(2):
                            b = pair * 2 + j
                            scaled(b, j)
                            for c in range(NCK):
                                act.wait_ge(S["point"], at(NCK * b + c + 1))
                                act.wait_ge(S["added"], at(NCK * b + c - back4(c) + 1))
                                act.activation(relued[:, c % 4, :], bank[c][:, 0:CPX], ACT.Relu, bias=V["pb2"], scale=few[:, 0:1]).then_inc(S["relued"], 1)

                @block.tensor
                def _(pe):
                    pe.sem_inc(S["point"], START)
                    with pe.Fori(0, B // 2) as pair:
                        for j in range(2):
                            b = pair * 2 + j
                            pe.wait_ge(S["quant"], at(b + 1))
                            for c in range(NCK):
                                pe.wait_ge(S["relued"], at(NCK * b + c - NCK + 1))
                                pe.matmul(bank[c][:, 0:CPX], point["p2"][:], quant[:, j, ck(c)], start=True, stop=True).then_inc(S["point"], 1)

                @block.vector
                def _(dve):
                    dve.sem_inc(S["quant"], START)
                    dve.sem_inc(S["added"], START)
                    with dve.Fori(0, B // 2) as pair:
                        for j in range(2):
                            b = pair * 2 + j
                            dve.wait_ge(S["real"], at(b + 1))
                            dve.wait_ge(S["point"], at(NCK * b - NCK))
                            dve.tensor_scalar(quant[:, j, :], real[:, j, :], ROUND, ROUND, ALU.add, ALU.subtract).then_inc(S["quant"], 1)
                            dve.wait_ge(s_load[j], 16 * pair + 16)
                            for c in range(NCK):
                                dve.wait_ge(S["relued"], at(NCK * b + c + 1))
                                dve.tensor_tensor(xin[:, j, ck(c)], xin[:, j, ck(c)], relued[:, c % 4, :], ALU.add).then_inc(S["added"], 1)

                @block.sync
                def _(sp):
                    with sp.Fori(0, B // 2) as pair:
                        for j in range(2):
                            b = pair * 2 + j
                            sp.wait_ge(S["added"], at(NCK * (b + 1)))
                            sp.dma_start(out_img[bass.ds(b, 1)].rearrange("o c n -> (o c) n"), xin[:, j, :]).then_inc(s_stored[j], 16)
                    for j in range(2):
                        sp.wait_ge(s_stored[j], at(16 * (B // 2)))

        loads = [(ident[:], w["ident"]), (vec[:], w["vec3"]), (peaks[:, 0:1], peak_d)] + [(raw[n][:], w["q_" + n]) for n in raw]
        scales("start", (loads, start_before, 5, start_after))
        sums_pass(True)
        scales("one", ([], ends_before("b1"), 1, next_after("b1", 2)))
        peak_pass()
        scales("two", ([], relu_before("pb1"), 1, next_after("pb1", 3)))
        sums_pass(False)
        scales("three", ([], ends_before("b2"), 1, next_after("b2", 4)))
        last_pass()


def program(nc, d, out):
    B = d["x"].shape[0]
    scratch = lambda name, shape: nc.dram_tensor("scratch_" + name, shape, F32).ap()
    after0 = scratch("after0", [B, C, HW])
    windows = scratch("windows", [B * NCK, C, (CH_ROWS + 2) * HP])
    table = scratch("table", [B * TROWS, 4 * C])
    conv = scratch("conv", [B * NCK, C, CPX])
    after2 = scratch("after2", [B, C, HW])
    peak = scratch("peak", [C, 1])
    attention_phase(nc, B, d["x"], d, after0)
    spread_phase(nc, B, after0, d["ident"], windows, table)
    deform_phase(nc, B * NCK, windows, table, d["base"], d["ident"], d["woff"], d["boff"], d["wdcn"], conv)
    fourier_phase(nc, B, conv.rearrange("(b k) c n -> b k c n", k=NCK), after0, d, after2, peak)
    quantised_phase(nc, B, after2, peak, d, out)


def lay_out(i):
    import numpy as np
    L0, L1, L2, L3 = ({k[8:]: v for k, v in i.items() if k.startswith(f"L{n}_conv_")} for n in range(4))
    B = i["x"].shape[0]
    third = lambda a: [a[k * C:(k + 1) * C] for k in range(3)]
    named0 = dict(L0, mlp_b1_0=third(L0["mlp_b1"])[0], mlp_b1_1=third(L0["mlp_b1"])[1], mlp_b1_2=third(L0["mlp_b1"])[2],
                  q_b=third(L0["qkv_b"])[0], k_b=third(L0["qkv_b"])[1], v_b=third(L0["qkv_b"])[2])
    tm, tr = L1["w_tm"].reshape(4, C, 9), L1["w_tr"].reshape(2, C, 9)
    order = lambda m, r: np.stack([m[0], m[2], m[1], m[3], r[0], r[1]])

    def block_diagonal(a):
        whole, n = np.zeros((C, C), np.float32), a.shape[1]
        for k in range(a.shape[0]):
            whole[k * n:(k + 1) * n, k * n:(k + 1) * n] = a[k]
        return whole

    group = np.arange(C) // 4
    named2 = {"gamma": L1["gn_gamma"], "beta": L1["gn_beta"], "b1r": L2["b1"][0].ravel(), "b1i": L2["b1"][1].ravel(),
              "b2r": L2["b2"][0].ravel(), "b2i": L2["b2"][1].ravel()}
    return {
        "x": i["x"].reshape(B, C, HW),
        "ident": np.eye(C, dtype=np.float32),
        "mean_of": np.full((C, C), 1.0 / C, np.float32),
        "vec0": np.stack([named0[n] for n in VEC0], 1),
        "taps3": L0["pos_w"].reshape(C, 9),
        "taps5": L0["lepe_w"].reshape(C, 25),
        "wqkv": L0["qkv_w"], "wo": L0["wo_w"], "w1": L0["mlp_w1"],
        "w2": L0["mlp_w2"].reshape(HID, C, C).transpose(1, 0, 2),
        "base": chunk_bases(B),
        "woff": order(tm, tr).transpose(1, 2, 0),
        "boff": np.broadcast_to(order(L1["b_tm"], L1["b_tr"]), (TPX, 6)),
        "wdcn": L1["w_dcn"].reshape(C, C, 9).transpose(1, 2, 0),
        "group_mean": ((group[:, None] == group) / (4.0 * HW)).astype(np.float32),
        "vec2": np.stack([named2[n] for n in VEC2], 1),
        "blocks": np.stack([block_diagonal(L2[n][p]) for n in ("w1", "w2") for p in range(2)], 1),
        **transform_matrices(),
        "vec3": np.stack([L3[n] for n in VEC3], 1),
        "q_w1": L3["w1"].reshape(C, 9), "q_w2": L3["w2"].reshape(C, 9),
        "q_p1": L3["p1"].reshape(C, C).T, "q_p2": L3["p2"].reshape(C, C).T,
    }


def kernel(**inputs):
    import numpy as np
    import concourse.bacc as bacc
    from concourse.bass_utils import run_bass_kernel_spmd

    nc = bacc.Bacc("TRN2", target_bir_lowering=False, num_devices=1)
    arrays = {n: np.ascontiguousarray(a) for n, a in lay_out({n: np.ascontiguousarray(a) for n, a in inputs.items()}).items()}
    d = {n: nc.dram_tensor("in_" + n, a.shape, mybir.dt.from_np(a.dtype), kind="ExternalInput").ap() for n, a in arrays.items()}
    shape = inputs["x"].shape
    out = nc.dram_tensor("out", shape, F32, kind="ExternalOutput").ap()
    program(nc, d, out.rearrange("b c h w -> b c (h w)"))
    r = run_bass_kernel_spmd(nc, [{"in_" + n: a for n, a in arrays.items()}], core_ids=[0])
    return r.results[0]["out"]
```

```python
from contextlib import ExitStack, contextmanager

import concourse.bass as bass
from concourse import mybir

F32 = mybir.dt.float32
BF16 = mybir.dt.bfloat16
I32 = mybir.dt.int32
I16 = mybir.dt.int16
U32 = mybir.dt.uint32
ALU = mybir.AluOpType
ACT = mybir.ActivationFunctionType
AX = mybir.AxisListType

C = 128
H = W = 56
HW = H * W
HP = H + 2
CH_ROWS = 8
NCK = H // CH_ROWS
CPX = CH_ROWS * W
TPX = 2 * W
TILES = CPX // TPX
TW = W + 1
TROWS = TW * TW
ROUND = 12582912.0
GN_EPS = 1e-5
START = 8


def at(i):
    return START + i


@contextmanager
def cleared_semaphore(nc, name):
    handle = nc.alloc_semaphore(name=name)
    yield handle
    nc.clear_and_free_semaphores([handle])


def spread_phase(nc, B, x_img, ident_d, windows, table):
    with ExitStack() as ctx:
        sb = lambda name, shape, dt=F32: ctx.enter_context(nc.sbuf_tensor(name, shape, dt))
        ps = lambda name, shape, dt=F32: ctx.enter_context(nc.psum_tensor(name, shape, dt))
        sem = lambda name: ctx.enter_context(nc.semaphore(name))
        ident = sb("sp_ident", [C, C])
        flat = sb("sp_flat", [C, 2, HW])
        padded = sb("sp_padded", [C, 2, HP, HP])
        turned = sb("sp_turned", [TPX, 2, HW // TPX, C])
        zeros = sb("sp_zeros", [B, TW, 2 * C])
        bank = [ps(f"sp_bank{k}", [TPX, 4, C]) for k in range(4)]
        s_const, s_zero, s_bank, s_turned, s_padded, s_edge, s_bfree = map(
            sem, ["sp_const", "sp_zero", "sp_bank", "sp_turned", "sp_padded", "sp_edge", "sp_bfree"])
        s_loaded, s_table, s_win = ([sem(f"sp_{n}{j}") for j in range(2)] for n in ("loaded", "table", "win"))
        GROUPS = HW // TPX // 4
        tab = table.rearrange("(b y x) (k c) -> b y x k c", b=B, y=TW, k=4)
        block = ctx.enter_context(nc.Block())

        @block.sync
        def _(sp):
            sp.dma_start(ident[:], ident_d).then_inc(s_const, 16)
            with sp.Fori(0, B // 2) as pair:
                b = pair * 2
                for j in range(2):
                    sp.wait_ge(s_turned, at(b + j - 1))
                    sp.wait_ge(s_padded, at(b + j - 1))
                    sp.dma_start(flat[:, j, :], x_img[bass.ds(b + j, 1)].rearrange("o c n -> (o c) n")).then_inc(s_loaded[j], 16)

        @block.tensor
        def _(pe):
            pe.wait_ge(s_const, 16)
            with pe.Fori(0, B // 2) as pair:
                b = pair * 2
                for j in range(2):
                    pe.wait_ge(s_loaded[j], 16 * pair + 16)
                    for g in range(GROUPS):
                        pe.wait_ge(s_bfree, (b + j) * GROUPS + g + 1)
                        for k in range(4):
                            t = 4 * g + k
                            last = pe.transpose(bank[(j * GROUPS + g) % 2][:, k, :], flat[:, j, t * TPX:(t + 1) * TPX], ident[:])
                        last.then_inc(s_bank, 1)

        @block.vector
        def _(dve):
            dve.sem_inc(s_bfree, 2)
            dve.sem_inc(s_turned, START)
            with dve.Fori(0, B // 2) as pair:
                b = pair * 2
                for j in range(2):
                    dve.wait_ge(s_table[j], at(128 * pair))
                    for g in range(GROUPS):
                        dve.wait_ge(s_bank, (b + j) * GROUPS + g + 1)
                        last = dve.tensor_copy(turned[:, j, 4 * g:4 * g + 4, :], bank[(j * GROUPS + g) % 2][:])
                        last.then_inc(s_bfree, 1)
                    dve.wait_ge(s_bfree, 2 + (b + j + 1) * GROUPS)
                    dve.sem_inc(s_turned, 1)

        @block.scalar
        def _(act):
            act.wait_ge(s_zero, 2)
            act.sem_inc(s_padded, START)
            for j in range(2):
                act.sem_inc(s_win[j], START)
                act.sem_inc(s_table[j], START)
            with act.Fori(0, B // 2) as pair:
                b = pair * 2
                for j in range(2):
                    act.wait_ge(s_loaded[j], 16 * pair + 16)
                    act.wait_ge(s_win[j], at(16 * NCK * pair))
                    act.activation(padded[:, j, 1:H + 1, 1:W + 1],
                                   flat[:, j, :].rearrange("c (h w) -> c h w", w=W), ACT.Copy).then_inc(s_padded, 1)
                    act.wait_ge(s_padded, at(b + j + 1))
                    for c in range(NCK):
                        act.dma_start(windows[bass.ds((b + j) * NCK + c, 1)].rearrange("o c n -> (o c) n"),
                                      padded[:, j, CH_ROWS * c:CH_ROWS * c + 10, :].rearrange("c h w -> c (h w)")).then_inc(s_win[j], 16)
                    act.wait_ge(s_turned, at(b + j + 1))
                    for dy in range(2):
                        for dx in range(2):
                            for r in range(2):
                                rows = tab[bass.ds(b + j, 1), r + 1 - dy:r + 1 - dy + H - 1:2, 1 - dx:1 - dx + W, 2 * dy + dx, :]
                                act.dma_start(rows.rearrange("o y x c -> x (o y) c"),
                                               turned[r * W:(r + 1) * W, j, :, :]).then_inc(s_table[j], 16)
            for j in range(2):
                act.wait_ge(s_win[j], at(16 * NCK * B // 2))
                act.wait_ge(s_table[j], at(128 * B // 2))

        @block.gpsimd
        def _(pool):
            pool.memset(zeros[:], 0.0).then_inc(s_zero, 1)
            pool.memset(padded[:], 0.0).then_inc(s_zero, 1)
            pool.wait_ge(s_zero, 2)
            for y, x, k in ((0, slice(0, TW), slice(0, 2)), (H, slice(0, TW), slice(2, 4))):
                pool.dma_start(tab[:, y, x, k, :].rearrange("b x k c -> b x (k c)"), zeros[:, :, :]).then_inc(s_edge, 16)
            for x, k, y0 in ((0, 0, 1), (0, 2, 0), (W, 1, 1), (W, 3, 0)):
                pool.dma_start(tab[:, y0:y0 + H, x, k, :], zeros[:, 0:H, 0:C]).then_inc(s_edge, 16)
            pool.wait_ge(s_edge, 96)


PE_TAPS = 6
ACT_DIAGS = 13


def deform_phase(nc, N, windows, table, base_d, ident_d, woff_d, boff_d, wdcn_d, conv_out):
    with ExitStack() as ctx:
        sb = lambda name, shape, dt=F32: ctx.enter_context(nc.sbuf_tensor("df_" + name, shape, dt))
        ps = lambda name, shape, dt=F32: ctx.enter_context(nc.psum_tensor("df_" + name, shape, dt))
        ident = sb("ident", [C, C])
        woff = sb("woff", [C, 9, 6])
        boff = sb("boff", [TPX, 6])
        wdcn = sb("wdcn", [C, 9, C])
        win = sb("win", [C, CH_ROWS + 2, HP])
        base = sb("base", [TPX, 9])
        off_rows = sb("off_rows", [6, CPX])
        off = sb("off", [TPX, 3, TILES, 2])
        ctr = sb("ctr", [TPX, TILES, 2])
        row = sb("row", [TPX, 3, TILES, 2])
        pos = sb("pos", [TPX, 3, 3, TILES, 2])
        cell = sb("cell", [TPX, 9, TILES, 2])
        frac = sb("frac", [TPX, 9, TILES, 2])
        rest = sb("rest", [TPX, 9, TILES, 2])
        lin = sb("lin", [TPX, 9, TILES])
        idx_next = sb("idx_next", [TPX, TILES, 9], I32)
        wt_next = sb("wt_next", [TPX, TILES, 9, 4])
        idx = sb("idx", [TPX, TILES, 9], I32)
        wt = sb("wt", [TPX, TILES, 9, 4])
        got = sb("got", [TPX, TILES, 9, 4 * C])
        diag = sb("diag", [TPX, 2, PE_TAPS * 4, TPX])
        part = sb("part", [TPX, 2, 9 - PE_TAPS, C])
        samp = sb("samp", [C, 9, CPX])
        yout = sb("yout", [C, CPX])
        p_rows = ps("p_rows", [6, CPX])
        p_off = ps("p_off", [TPX, TILES, 3, 2])
        p_samp = [ps(f"p_samp{k}", [C, 3, TPX]) for k in range(3)]
        p_conv = ps("p_conv", [C, CPX])
        names = "const win rows rowsc offs prep idx diag diag_act parts tile sampled copied conv y stored chain issue".split()
        S = {n: ctx.enter_context(nc.semaphore("df_" + n)) for n in names}
        s_got = [ctx.enter_context(nc.semaphore(f"df_got{t}")) for t in range(TILES)]
        s_turnstile = ctx.enter_context(nc.semaphore("df_turnstile"))
        PREP = 19
        block = ctx.enter_context(nc.Block())
        count = lambda i, t: TILES * i + t

        def over_chunks(eng, body):
            with eng.Fori(0, N - 2) as i:
                body(i, 2)
            body(N - 2, 1)
            body(N - 1, 0)

        @block.sync
        def _(sp):
            for dst, src in ((ident, ident_d), (woff, woff_d), (boff, boff_d), (wdcn, wdcn_d)):
                sp.dma_start(dst[:], src).then_inc(S["const"], 16)

            def load(i):
                sp.dma_start(win[:].rearrange("c h w -> c (h w)"), windows[bass.ds(i, 1)].rearrange("o c n -> (o c) n")).then_inc(S["win"], 16)
                sp.dma_start(base[:], base_d[bass.ds(i, 1)].rearrange("o p n -> (o p) n")).then_inc(S["win"], 16)

            load(0)
            with sp.Fori(0, N - 1) as i:
                sp.wait_ge(S["prep"], at(i + 1))
                load(i + 1)

        @block.tensor
        def _(pe):
            pe.sem_inc(S["tile"], TILES)
            for n in "rows offs conv".split():
                pe.sem_inc(S[n], START)
            pe.wait_ge(S["const"], 64)

            def offset_rows(i):
                pe.wait_ge(S["win"], 32 * i + 32)
                pe.wait_ge(S["rowsc"], at(i))
                for k in range(9):
                    last = pe.matmul(p_rows[:], woff[:, k, :], win[:, k // 3:k // 3 + CH_ROWS, k % 3:k % 3 + W], start=(k == 0), stop=(k == 8))
                last.then_inc(S["rows"], 1)

            def offset_turn(i):
                pe.wait_ge(S["rowsc"], at(i + 1))
                pe.wait_ge(S["prep"], at(i))
                for t in range(TILES):
                    last = pe.matmul(p_off[:, t, :, :].rearrange("p a b -> p (a b)"), off_rows[:, t * TPX:(t + 1) * TPX], ident[0:6, 0:6],
                                     start=True, stop=True)
                last.then_inc(S["offs"], 1)

            def tile(i, t):
                n = count(i, t)
                pe.wait_ge(s_got[t], 144 * i + 144)
                pe.wait_ge(S["diag"], n + 1)
                pe.wait_ge(S["diag_act"], n + 1)
                for g in range(3):
                    pe.wait_ge(S["copied"], 3 * n + g + 1)
                    if g == PE_TAPS // 3:
                        pe.wait_ge(S["parts"], n + 1)
                    for k in range(3):
                        tap = 3 * g + k
                        if tap < PE_TAPS:
                            for c in range(4):
                                last = pe.matmul(p_samp[g][:, k, :], got[:, t, tap, c * C:(c + 1) * C], diag[:, t % 2, 4 * tap + c, :],
                                                 start=(c == 0), stop=(c == 3))
                        else:
                            last = pe.transpose(p_samp[g][:, k, :], part[:, t % 2, tap - PE_TAPS, :], ident[0:TPX, 0:TPX])
                    last.then_inc(S["sampled"], 1)
                pe.wait_ge(S["sampled"], 3 * n + 3)
                pe.sem_inc(S["tile"], 1)

            def conv(i):
                pe.wait_ge(S["copied"], 3 + 12 * i + 12)
                pe.wait_ge(S["y"], at(i))
                for k in range(9):
                    last = pe.matmul(p_conv[:], wdcn[:, k, :], samp[:, k, :], start=(k == 0), stop=(k == 8))
                last.then_inc(S["conv"], 1)

            def chunk(i, ahead):
                tile(i, 0)
                tile(i, 1)
                if ahead == 2:
                    offset_rows(i + 2)
                tile(i, 2)
                if ahead == 2:
                    offset_turn(i + 2)
                tile(i, 3)
                conv(i)

            for i in range(2):
                offset_rows(i)
                offset_turn(i)
            over_chunks(pe, chunk)

        @block.vector
        def _(dve):
            dve.wait_ge(S["const"], 64)
            dve.sem_inc(S["prep"], START)

            def prepare(i):
                n = [0]

                def step(instruction):
                    n[0] += 1
                    instruction.then_inc(S["chain"], 1)
                    dve.wait_ge(S["chain"], PREP * i + n[0])

                dve.wait_ge(S["offs"], at(i + 1))
                dve.wait_ge(S["win"], 32 * i + 32)
                step(dve.tensor_tensor(off[:].rearrange("p k t j -> p t k j"), p_off[:],
                                       boff[:].rearrange("p (k j) -> p k j", j=2).unsqueeze(1).to_broadcast([TPX, TILES, 3, 2]), ALU.add))
                step(dve.tensor_tensor(ctr[:], off[:, 2], base[:, 0:8].rearrange("p (t j) -> p t j", j=2), ALU.add))
                step(dve.tensor_tensor(row[:, 0], ctr[:], off[:, 0], ALU.subtract))
                step(dve.tensor_copy(row[:, 1], ctr[:]))
                step(dve.tensor_tensor(row[:, 2], ctr[:], off[:, 0], ALU.add))
                rows = row[:].rearrange("p k t j -> p k (t j)")
                side = off[:, 1].rearrange("p t j -> p (t j)").unsqueeze(1).to_broadcast([TPX, 3, 2 * TILES])
                for kx, op in ((0, ALU.subtract), (2, ALU.add)):
                    step(dve.tensor_tensor(pos[:, :, kx].rearrange("p k t j -> p k (t j)"), rows, side, op))
                step(dve.tensor_copy(pos[:, :, 1].rearrange("p k t j -> p k (t j)"), rows))
                flat = lambda a: a.rearrange("p a t j -> p (a t j)")
                p = pos[:].rearrange("p a b t j -> p (a b t j)")
                step(dve.tensor_scalar(p, p, 0.0, float(W + 1), ALU.max, ALU.min))
                step(dve.tensor_scalar(flat(cell[:]), p, 0.5, 0.0, ALU.subtract, ALU.max))
                step(dve.tensor_scalar(flat(cell[:]), flat(cell[:]), ROUND, ROUND, ALU.add, ALU.subtract))
                step(dve.tensor_tensor(flat(frac[:]), p, flat(cell[:]), ALU.subtract))
                step(dve.tensor_scalar(flat(rest[:]), flat(frac[:]), -1.0, 1.0, ALU.mult, ALU.add))
                step(dve.scalar_tensor_tensor(out=lin[:], in0=cell[:, :, :, 0], scalar=float(TW), in1=cell[:, :, :, 1], op0=ALU.mult, op1=ALU.add))
                step(dve.tensor_scalar(idx_next[:].rearrange("p t k -> p k t"), lin[:], base[:, 8:9], None, ALU.add))
                for c, (a, b) in enumerate(((rest, rest), (rest, frac), (frac, rest), (frac, frac))):
                    step(dve.tensor_tensor(wt_next[:, :, :, c].rearrange("p t k -> p k t"), a[:, :, :, 0], b[:, :, :, 1], ALU.mult))
                assert n[0] == PREP
                dve.sem_inc(S["prep"], 1)

            def publish(i, t):
                dve.tensor_copy(idx[:, t, :], idx_next[:, t, :]).then_inc(S["idx"], 1)
                dve.tensor_copy(wt[:, t], wt_next[:, t]).then_inc(S["idx"], 1)

            def diagonals(i, t):
                n = count(i, t)
                dve.wait_ge(S["idx"], 2 * n + 2)
                dve.wait_ge(S["tile"], n + 3)
                for m in range(ACT_DIAGS, 4 * PE_TAPS):
                    last = dve.tensor_scalar(diag[:, t % 2, m, :], ident[0:TPX, 0:TPX], wt[:, t, m // 4, m % 4:m % 4 + 1], None, ALU.mult)
                last.then_inc(S["diag"], 1)

            def weigh(i, t):
                n = count(i, t)
                K = 9 - PE_TAPS
                dve.wait_ge(s_got[t], 144 * i + 144)
                dve.wait_ge(S["tile"], n + 3)
                for c in range(4):
                    for k in range(K):
                        tap = PE_TAPS + k
                        src, weight = got[:, t, tap, c * C:(c + 1) * C], wt[:, t, tap, c:c + 1]
                        if c == 0:
                            last = dve.tensor_scalar(part[:, t % 2, k, :], src, weight, None, ALU.mult)
                        else:
                            last = dve.scalar_tensor_tensor(out=part[:, t % 2, k, :], in0=src, scalar=weight, in1=part[:, t % 2, k, :],
                                                            op0=ALU.mult, op1=ALU.add)
                    if c < 3:
                        last.then_inc(S["issue"], 1)
                        dve.wait_ge(S["issue"], 3 * n + c + 1)
                last.then_inc(S["parts"], 1)

            def chunk(i, ahead):
                for t in range(TILES):
                    weigh(i, t)
                    if t + 1 < TILES:
                        diagonals(i, t + 1)
                    elif ahead:
                        diagonals(i + 1, 0)
                    if ahead:
                        dve.wait_ge(S["parts"], count(i, t) + 1)
                        dve.wait_ge(S["diag_act"], count(i, t) + 1)
                        publish(i + 1, t)
                if ahead == 2:
                    dve.wait_ge(S["idx"], 2 * count(i + 2, 0))
                    prepare(i + 2)

            prepare(0)
            for t in range(TILES):
                publish(0, t)
            dve.wait_ge(S["idx"], 2 * TILES)
            prepare(1)
            diagonals(0, 0)
            over_chunks(dve, chunk)

        @block.gpsimd
        def _(pool):
            with pool.Fori(0, N) as i:
                for t in range(TILES):
                    pool.wait_ge(S["idx"], 2 * count(i, t) + 1)
                    pool.wait_ge(S["tile"], count(i, t) + 1)
                    pool.sem_inc(s_turnstile, 1)
                    for k in range(9):
                        pool.indirect_dma_start(out=got[:, t, k, :], out_offset=None, in_=table[:, :],
                                                in_offset=bass.IndirectOffsetOnAxis(ap=idx[:, t, k:k + 1], axis=0)).then_inc(s_got[t], 16)

        @block.scalar
        def _(act):
            act.sem_inc(S["copied"], 3)
            for n in "y stored rowsc".split():
                act.sem_inc(S[n], START)
            act.wait_ge(S["const"], 64)

            def diagonals(i, t):
                n = count(i, t)
                act.wait_ge(S["idx"], 2 * n + 2)
                act.wait_ge(S["tile"], n + 3)
                for m in range(ACT_DIAGS):
                    last = act.activation(diag[:, t % 2, m, :], ident[0:TPX, 0:TPX], ACT.Copy, scale=wt[:, t, m // 4, m % 4:m % 4 + 1])
                last.then_inc(S["diag_act"], 1)

            def copy_rows(i):
                act.wait_ge(S["rows"], at(i + 1))
                act.wait_ge(S["offs"], at(i))
                act.activation(off_rows[:], p_rows[:], ACT.Copy).then_inc(S["rowsc"], 1)

            def copy_samples(i, t):
                for g in range(3):
                    act.wait_ge(S["sampled"], 3 * count(i, t) + g + 1)
                    if t == 0 and g == 0:
                        act.wait_ge(S["conv"], at(i))
                    act.activation(samp[:, 3 * g:3 * g + 3, t * TPX:(t + 1) * TPX], p_samp[g][:], ACT.Copy).then_inc(S["copied"], 1)

            def chunk(i, ahead):
                for t in range(TILES):
                    if t + 1 < TILES:
                        diagonals(i, t + 1)
                    copy_samples(i, t)
                    if t == 1 and ahead == 2:
                        copy_rows(i + 2)
                if ahead:
                    diagonals(i + 1, 0)
                act.wait_ge(S["conv"], at(i + 1))
                act.wait_ge(S["stored"], at(16 * i))
                act.activation(yout[:], p_conv[:], ACT.Copy).then_inc(S["y"], 1)
                act.wait_ge(S["y"], at(i + 1))
                act.dma_start(conv_out[bass.ds(i, 1)].rearrange("o c n -> (o c) n"), yout[:]).then_inc(S["stored"], 16)

            for i in range(2):
                copy_rows(i)
            diagonals(0, 0)
            over_chunks(act, chunk)
            act.wait_ge(S["stored"], at(16 * N))


def chunk_bases(B):
    import numpy as np
    base = np.zeros((B * NCK, TPX, 9), np.float32)
    p = np.arange(TPX)
    for i in range(B * NCK):
        b, c = divmod(i, NCK)
        for t in range(TILES):
            base[i, :, 2 * t] = CH_ROWS * c + 2 * t + p // W + 1
            base[i, :, 2 * t + 1] = p % W + 1
        base[i, :, 8] = b * TROWS
    return base
WIN = 8
NWIN = H // WIN
NW = NWIN * NWIN
WPX = WIN * WIN
HEADS = 4
HD = C // HEADS
TOPK = 4
DVE_TAPS = 16
LAST_TAPS = 10
DVE_TAPS3 = 4
HID = 3
LN_EPS = 1e-6
QSCALE = float(C) ** -0.5


def attention_phase(nc, B, x_d, w, out_img):
    with ExitStack() as ctx:
        ctx.callback(nc.all_engine_barrier)
        sb = lambda name, shape, dt=F32: ctx.enter_context(nc.sbuf_tensor("at_" + name, shape, dt))
        ps = lambda name, shape, dt=F32: ctx.enter_context(nc.psum_tensor("at_" + name, shape, dt))
        sem = lambda name: ctx.enter_context(cleared_semaphore(nc, "at_" + name))
        ident = sb("ident", [C, C])
        mean_of = sb("mean_of", [C, C])
        vec = sb("vec", [C, len(VEC0)])
        taps3 = sb("taps3", [C, 9])
        taps5 = sb("taps5", [C, 25])
        diag3 = sb("diag3", [C, 9, C])
        diag5 = sb("diag5", [C, 25, C])
        wqkv = sb("wqkv", [C, 3 * C])
        wo = sb("wo", [C, C])
        w1 = sb("w1", [C, HID * C])
        w2 = sb("w2", [C, HID, C])
        eps = sb("eps", [C, 1])
        flat = sb("flat", [C, HW])
        padded = sb("padded", [C, HP, HP])
        x1 = sb("x1", [C, HW])
        dev = sb("dev", [C, HW])
        y = sb("y", [C, NW, WPX])
        kv = sb("kv", [C, NW, 2, WPX])
        vpad = sb("vpad", [C, H + 4, W + 4])
        oimg = sb("oimg", [C, HW])
        sq = sb("sq", [C, 2, CPX])
        ysum = sb("ysum", [C, NW])
        qm = sb("qm", [C, NW])
        km = sb("km", [C, NW])
        logit = sb("logit", [NW, NW])
        top = sb("top", [NW, 8])
        top_at = sb("top_at", [NW, 8], U32)
        chosen = sb("chosen", [1, NW * TOPK], U32)
        qz = sb("qz", [C, 2, NWIN, HEADS, WPX])
        qb = sb("qb", [C, 1])
        kvsel = sb("kvsel", [C, 2, 2, TOPK, WPX])
        prob = sb("prob", [C, 2, 2, TOPK * WPX])
        probT = sb("probT", [C, 2, 4, C])
        vT = sb("vT", [C, 2, 2, C])
        nmax = sb("nmax", [C, 2, 2])
        tot = sb("tot", [C, 2, 2])
        inv = sb("inv", [C, 2, 2])
        hid = sb("hid", [C, 2, HID, CPX])
        bank = [ps(f"bank{k}", [C, 512]) for k in range(8)]

        names = ("const zero log log2 posed tapped diag load padfree pad conv x1 mean dev sq var std rn y kv kcopy vcopy vpad ysum qkm qkmc logit lcopy "
                 "top topidx issue sel issue_pe q qz s vt vtc nb exp rec pn pt ptc pv oc lepe lepe2 qb wo x2 mean2 dev2 sq2 var2 std2 rn2 z "
                 "m1 gelu m2 fin stored chosen").split()
        S = {n: sem(n) for n in names}
        block = ctx.enter_context(nc.Block())

        def buf(odd, v):
            return (odd + v) % 2

        def each_row(engine, row):
            row(0, 0, True, False)
            with engine.Fori(0, (NWIN - 3) // 2) as j:
                row(2 * j + 1, 1, False, False)
                row(2 * j + 2, 0, False, False)
            row(NWIN - 2, 1, False, False)
            row(NWIN - 1, 0, False, True)

        def share(total, v):
            return total * v // NWIN

        def std1(c):
            return kv[:].rearrange("c w t p -> c (w t p)")[:, 2 * CPX * c:2 * CPX * c + CPX]

        def std2(c):
            return x1[:, ck(c)]

        GROUPS = ((0, 4), (4, NCK))

        def kv_bank(c, t):
            return bank[(6, 6, 0, 2)[c if c < 4 else 1 + (c - 4) % 3] + t]

        def kv_before(c):
            return {0: 0, 1: 1, 2: 0, 3: 0}.get(c, c - 2)

        def ck(c):
            return slice(c * CPX, (c + 1) * CPX)

        V = {n: vec[:, k:k + 1] for k, n in enumerate(VEC0)}

        @block.sync
        def _(sp):
            for dst, src in ((ident, w["ident"]), (mean_of, w["mean_of"]), (vec, w["vec0"]), (taps3, w["taps3"]), (taps5, w["taps5"]),
                             (wqkv, w["wqkv"]), (wo, w["wo"]), (w1, w["w1"]), (w2, w["w2"])):
                sp.dma_start(dst[:], src).then_inc(S["const"], 16)
            def load(b):
                sp.dma_start(flat[:], x_d[bass.ds(b, 1)].rearrange("o c n -> (o c) n")).then_inc(S["load"], 16)

            load(0)

            def serve(b, more):
                if more:
                    sp.wait_ge(S["padfree"], at(b + 1))
                    load(b + 1)
                sp.wait_ge(S["topidx"], at(b + 1))
                sp.dma_start(chosen[:].rearrange("o (w k) -> o w k", k=TOPK), top_at[:, 0:TOPK]).then_inc(S["chosen"], 16)
                sp.wait_ge(S["fin"], at(NCK * (b + 1)))
                sp.dma_start(out_img[bass.ds(b, 1)].rearrange("o c n -> (o c) n"), oimg[:]).then_inc(S["stored"], 16)

            with sp.Fori(0, B - 1) as b:
                serve(b, True)
            serve(B - 1, False)
            sp.wait_ge(S["stored"], 16 * B + START)

        @block.gpsimd
        def _(pool):
            pool.memset(vpad[:], 0.0).then_inc(S["zero"], 1)
            pool.memset(padded[:], 0.0).then_inc(S["zero"], 1)
            pool.memset(qz[:], 0.0).then_inc(S["zero"], 1)
            pool.memset(eps[:], LN_EPS).then_inc(S["zero"], 1)
            pool.sem_inc(S["sel"], START)
            pool.sem_inc(S["stored"], START)
            with pool.Fori(0, B) as b:
                pool.wait_ge(S["chosen"], 16 * b + 16)
                pool.wait_ge(S["vcopy"], at(NCK * (b + 1)))
                pool.sem_inc(S["issue"], 1)

                def row(r, odd, first, last):
                    for v in range(NWIN):
                        n = b * NW + r * NWIN + v
                        pool.wait_ge(S["vt"], at(n - 1))
                        pool.sem_inc(S["issue"], 1)
                        for k in range(TOPK):
                            src = pool.value_load(chosen[0:1, bass.ds(r * (NWIN * TOPK) + (v * TOPK + k), 1)], min_val=0, max_val=NW - 1)
                            copy = pool.tensor_copy(kvsel[:, buf(odd, v), :, k, :], kv[:, bass.ds(src, 1), :, :].rearrange("c o t p -> c (o t) p"))
                        copy.then_inc(S["sel"], 1)

                each_row(pool, row)

        @block.tensor
        def _(pe):
            for n in ("conv mean var kv qkm logit q s vt pt pv lepe lepe2 wo mean2 var2 m1 m2".split()):
                pe.sem_inc(S[n], START)
            pe.wait_ge(S["diag"], 34)
            pe.wait_ge(S["const"], 144)

            def conv(b, c):
                if c >= 2:
                    pe.wait_ge(S["x1"], at(NCK * b + c - 1))
                for k in range(DVE_TAPS3, 9):
                    last = pe.matmul(bank[c % 2][:, 0:CPX], diag3[:, k, :],
                                     padded[:, WIN * c + k // 3:WIN * c + k // 3 + WIN, k % 3:k % 3 + W], start=(k == DVE_TAPS3), stop=(k == 8))
                last.then_inc(S["conv"], 1)

            def mean(b, c):
                pe.wait_ge(S["x1"], at(NCK * b + c + 1))
                if c >= 2:
                    pe.wait_ge(S["dev"], at(NCK * b + c - 1))
                pe.matmul(bank[2 + c % 2][:, 0:CPX], mean_of[:], x1[:, ck(c)], start=True, stop=True).then_inc(S["mean"], 1)

            def var(b, c):
                pe.wait_ge(S["sq"], at(NCK * b + c + 1))
                if c >= 2:
                    pe.wait_ge(S["log"], at(NCK * b + c - 1))
                pe.matmul(bank[4 + c % 2][:, 0:CPX], mean_of[:], sq[:, c % 2, :], start=True, stop=True).then_inc(S["var"], 1)

            def keys_values(b, c):
                pe.wait_ge(S["y"], at(NCK * b + c + 1))
                if kv_before(c):
                    pe.wait_ge(S["vcopy"], at(NCK * b + kv_before(c)))
                    pe.wait_ge(S["vpad"], at(NCK * b + kv_before(c)))
                for t in range(2):
                    last = pe.matmul(kv_bank(c, t)[:, 0:CPX], wqkv[:, (1 + t) * C:(2 + t) * C],
                                     y[:, NWIN * c:NWIN * (c + 1), :], start=True, stop=True)
                last.then_inc(S["kv"], 1)

            def choose(b):
                pe.wait_ge(S["ysum"], at(NCK * (b + 1)))
                pe.wait_ge(S["vpad"], at(NCK * (b + 1)))
                for t in range(2):
                    last = pe.matmul(bank[t][:, 0:NW], wqkv[:, t * C:(t + 1) * C], ysum[:], start=True, stop=True)
                last.then_inc(S["qkm"], 1)
                pe.wait_ge(S["qkmc"], at(2 * b + 2))
                pe.matmul(bank[2][0:NW, 0:NW], qm[:], km[:], start=True, stop=True).then_inc(S["logit"], 1)

            def queries(b, r):
                pe.wait_ge(S["qz"], at(2 * (NCK * b + r)))
                pe.matmul(bank[0][:, 0:CPX], wqkv[:, 0:C], y[:, bass.ds(r * NWIN, NWIN), :], start=True, stop=True).then_inc(S["q"], 1)

            def scores(n, i, odd, v):
                pe.wait_ge(S["sel"], at(n + 1))
                pe.wait_ge(S["exp"], at(n - 1))
                for g in range(2):
                    last = pe.matmul(bank[1 + i][:, g * 256:(g + 1) * 256], qz[:, odd, v, 2 * g:2 * g + 2, :].rearrange("c h p -> c (h p)"),
                                     kvsel[:, i, 0, :, :].rearrange("c k p -> c (k p)"), start=True, stop=True)
                last.then_inc(S["s"], 1)

            def turn_values(n, i):
                pe.wait_ge(S["vtc"], at(n))
                for g in range(2):
                    last = pe.transpose(bank[3][:, g * C:(g + 1) * C],
                                        kvsel[:, i, 1, 2 * g:2 * g + 2, :].rearrange("c k p -> c (k p)"), ident[:])
                last.then_inc(S["vt"], 1)

            def turn_probs(n, i):
                pe.wait_ge(S["pn"], at(n + 1))
                pe.wait_ge(S["ptc"], at(n - 1))
                for kh in range(2):
                    for g in range(2):
                        last = pe.transpose(bank[4 + i][:, (2 * kh + g) * C:(2 * kh + g + 1) * C],
                                            prob[:, i, g, kh * C:(kh + 1) * C], ident[:])
                last.then_inc(S["pt"], 1)

            def weigh_values(n, i):
                pe.wait_ge(S["ptc"], at(n + 1))
                pe.wait_ge(S["vtc"], at(n + 1))
                pe.wait_ge(S["oc"], at(n))
                pe.sem_inc(S["issue_pe"], 1)
                for h in range(HEADS):
                    p = slice(HD * h, HD * (h + 1))
                    for kh in range(2):
                        last = pe.matmul(bank[6][p, 0:WPX], vT[:, i, kh, p], probT[:, i, 2 * kh + h // 2, h % 2 * WPX:(h % 2 + 1) * WPX],
                                         start=(kh == 0), stop=(kh == 1))
                last.then_inc(S["pv"], 1)

            def lepe(b, r, taps, first=False):
                for k in taps:
                    if k == DVE_TAPS and not first:
                        pe.wait_ge(S["tapped"], at(DVE_TAPS * (NCK * b + r - 1) + 1))
                    mm = pe.matmul(bank[7][:, 0:CPX], diag5[:, k, :], vpad[:, bass.ds(r * WIN + k // 5, WIN), k % 5:k % 5 + W],
                                   start=(k == DVE_TAPS), stop=(k == 24))
                    if k == 24:
                        mm.then_inc(S["lepe"], 1)

            def lepe_last(b, taps):
                for k in taps:
                    if k == LAST_TAPS:
                        pe.wait_ge(S["tapped"], at(DVE_TAPS * (NCK * (b + 1) - 1) + 1))
                    mm = pe.matmul(bank[7][:, 0:CPX], diag5[:, k, :], vpad[:, (NCK - 1) * WIN + k // 5:NCK * WIN + k // 5, k % 5:k % 5 + W],
                                   start=(k == LAST_TAPS), stop=(k == DVE_TAPS - 1))
                    if k == DVE_TAPS - 1:
                        mm.then_inc(S["lepe2"], 1)

            def out_proj(b, c):
                if c >= 2:
                    pe.wait_ge(S["x2"], at(NCK * b + c - 1))
                pe.matmul(bank[c % 2][:, 0:CPX], wo[:], oimg[:, ck(c)], start=True, stop=True).then_inc(S["wo"], 1)

            def mean2(b, c):
                pe.wait_ge(S["x2"], at(NCK * b + c + 1))
                if c >= 1:
                    pe.wait_ge(S["dev2"], at(NCK * b + c))
                pe.matmul(bank[2][:, 0:CPX], mean_of[:], dev[:, ck(c)], start=True, stop=True).then_inc(S["mean2"], 1)

            def var2(b, c):
                pe.wait_ge(S["sq2"], at(NCK * b + c + 1))
                if c >= 2:
                    pe.wait_ge(S["log2"], at(NCK * b + c - 1))
                pe.matmul(bank[3 + c % 2][:, 0:CPX], mean_of[:], sq[:, c % 2, :], start=True, stop=True).then_inc(S["var2"], 1)

            z = y[:].rearrange("c w p -> c (w p)")

            def mlp_in(b, c):
                pe.wait_ge(S["z"], at(NCK * b + c + 1))
                if c >= 1:
                    pe.wait_ge(S["gelu"], at(NCK * b + c))
                for j in range(HID):
                    last = pe.matmul(bank[4 + j][:, 0:CPX], w1[:, j * C:(j + 1) * C], z[:, ck(c)], start=True, stop=True)
                last.then_inc(S["m1"], 1)

            def mlp_out(b, c):
                pe.wait_ge(S["gelu"], at(NCK * b + c + 1))
                if c >= 2:
                    pe.wait_ge(S["fin"], at(NCK * b + c - 1))
                for j in range(HID):
                    last = pe.matmul(bank[7 if c % 2 else 3][:, 0:CPX], w2[:, j, :], hid[:, c % 2, j, :], start=(j == 0), stop=(j == HID - 1))
                last.then_inc(S["m2"], 1)

            with pe.Fori(0, B) as b:
                pe.wait_ge(S["pad"], b + 1)
                for c in range(NCK + 2):
                    if c < NCK:
                        conv(b, c)
                    if c == 1:
                        pe.wait_ge(S["fin"], at(NCK * b))
                    if 1 <= c <= NCK:
                        mean(b, c - 1)
                    if c >= 2:
                        var(b, c - 2)
                    if c >= NCK - 1:
                        keys_values(b, c - (NCK - 1))
                for c in range(3, NCK):
                    keys_values(b, c)
                choose(b)
                pe.wait_ge(S["vcopy"], at(NCK * (b + 1)))
                pe.wait_ge(S["vpad"], at(NCK * (b + 1)))
                pe.sem_inc(S["issue"], 1)
                queries(b, 0)
                lepe(b, 0, range(DVE_TAPS, 25), first=True)
                pe.wait_ge(S["qz"], at(2 * NCK * b + 2))

                def row(r, odd, first, last):
                    for v in range(NWIN):
                        n = b * NW + r * NWIN + v
                        if v == 0 and not first:
                            pe.wait_ge(S["qz"], at(2 * (NCK * b + r + 1)))
                        scores(n, buf(odd, v), odd, v)
                        if not first or v >= 2:
                            weigh_values(n - 2, buf(odd, v))
                        turn_values(n, buf(odd, v))
                        if not first or v >= 1:
                            turn_probs(n - 1, buf(odd, v + 1))
                        if last and 1 <= v < NWIN - 1:
                            more = DVE_TAPS - LAST_TAPS
                            lepe_last(b, range(LAST_TAPS + more * (v - 1) // (NWIN - 2), LAST_TAPS + more * v // (NWIN - 2)))
                        if not last:
                            if v >= 1:
                                pe_taps = 25 - DVE_TAPS
                                lepe(b, r + 1, range(DVE_TAPS + pe_taps * (v - 1) // (NWIN - 1), DVE_TAPS + pe_taps * v // (NWIN - 1)))
                            if v == 3:
                                queries(b, r + 1)

                each_row(pe, row)
                n = NW * b + NW
                weigh_values(n - 2, 1)
                turn_probs(n - 1, 0)
                weigh_values(n - 1, 0)
                pe.wait_ge(S["oc"], at(NW * (b + 1)))
                for c in range(NCK + 2):
                    if c < NCK:
                        out_proj(b, c)
                    if 1 <= c <= NCK:
                        mean2(b, c - 1)
                    if c >= 2:
                        var2(b, c - 2)
                for c in range(NCK + 1):
                    if c < NCK:
                        mlp_in(b, c)
                    if c >= 1:
                        mlp_out(b, c - 1)

        @block.vector
        def _(dve):
            for n in ("posed tapped x1 dev rn y vpad ysum qkmc lcopy top topidx nb rec pn oc x2 dev2 rn2 z fin".split()):
                dve.sem_inc(S[n], START)
            dve.wait_ge(S["const"], 144)
            for k in range(9):
                dve.tensor_scalar(diag3[:, k, :], ident[:], taps3[:, k:k + 1], None, ALU.mult).then_inc(S["diag"], 1)
            for k in range(25):
                dve.tensor_scalar(diag5[:, k, :], ident[:], taps5[:, k:k + 1], None, ALU.mult).then_inc(S["diag"], 1)
            dve.wait_ge(S["zero"], 3)
            dve.tensor_scalar(qb[:], V["q_b"], QSCALE, None, ALU.mult).then_inc(S["qb"], 1)

            rows = lambda a, c: a[:, ck(c)].rearrange("c (h w) -> c h w", w=W)
            z = y[:].rearrange("c w p -> c (w p)")

            def residual(b, c):
                for k in range(DVE_TAPS3):
                    if k:
                        dve.wait_ge(S["posed"], at(DVE_TAPS3 * (NCK * b + c) + k))
                    start = padded[:, WIN * c + 1:WIN * c + 1 + WIN, 1:W + 1] if k == 0 else rows(x1, c)
                    dve.scalar_tensor_tensor(out=rows(x1, c), in0=padded[:, WIN * c + k // 3:WIN * c + k // 3 + WIN, k % 3:k % 3 + W],
                                             scalar=taps3[:, k:k + 1], in1=start, op0=ALU.mult, op1=ALU.add).then_inc(S["posed"], 1)
                dve.wait_ge(S["posed"], at(DVE_TAPS3 * (NCK * b + c + 1)))
                dve.wait_ge(S["conv"], at(NCK * b + c + 1))
                dve.scalar_tensor_tensor(out=rows(x1, c), in0=bank[c % 2][:, 0:CPX].rearrange("c (h w) -> c h w", w=W), scalar=V["pos_b"],
                                         in1=rows(x1, c), op0=ALU.add, op1=ALU.add).then_inc(S["x1"], 1)

            def deviation(b, c):
                dve.wait_ge(S["mean"], at(NCK * b + c + 1))
                dve.tensor_tensor(dev[:, ck(c)], x1[:, ck(c)], bank[2 + c % 2][:, 0:CPX], ALU.subtract).then_inc(S["dev"], 1)

            def norm(b, c):
                i = NCK * b + c + 1
                dve.wait_ge(S["std"], at(i))
                dve.tensor_tensor(dev[:, ck(c)], dev[:, ck(c)], std1(c), ALU.mult).then_inc(S["rn"], 1)
                dve.wait_ge(S["rn"], at(i))
                dve.tensor_scalar(y[:, NWIN * c:NWIN * (c + 1), :].rearrange("c v (r q) -> c v r q", q=WIN),
                                  dev[:, ck(c)].rearrange("c (r v q) -> c v r q", r=WIN, v=NWIN),
                                  V["ln1_g"], V["ln1_b"], ALU.mult, ALU.add).then_inc(S["y"], 1)
                dve.wait_ge(S["y"], at(i))
                dve.tensor_reduce(ysum[:, NWIN * c:NWIN * (c + 1)], y[:, NWIN * c:NWIN * (c + 1), :], AX.X, ALU.add).then_inc(S["ysum"], 1)

            def image_values(b, c):
                dve.wait_ge(S["vcopy"], at(NCK * b + c + 1))
                dve.tensor_scalar(vpad[:, WIN * c + 2:WIN * (c + 1) + 2, 2:W + 2].rearrange("c r (v q) -> c v r q", q=WIN),
                                  kv_bank(c, 1)[:, 0:CPX].rearrange("c (v r q) -> c v r q", r=WIN, q=WIN), V["v_b"], None, ALU.add).then_inc(S["vpad"], 1)

            def choose(b):
                dve.wait_ge(S["qkm"], at(b + 1))
                dve.tensor_scalar(qm[:], bank[0][:, 0:NW], 1.0 / WPX, V["q_b"], ALU.mult, ALU.add).then_inc(S["qkmc"], 1)
                dve.tensor_scalar(km[:], bank[1][:, 0:NW], 1.0 / WPX, V["k_b"], ALU.mult, ALU.add).then_inc(S["qkmc"], 1)
                dve.wait_ge(S["logit"], at(b + 1))
                dve.tensor_scalar(logit[:], bank[2][0:NW, 0:NW], QSCALE, None, ALU.mult).then_inc(S["lcopy"], 1)
                dve.wait_ge(S["lcopy"], at(b + 1))
                dve.sem_inc(S["issue"], 1)
                dve.max(top[:], logit[:]).then_inc(S["top"], 1)
                dve.wait_ge(S["top"], at(b + 1))
                dve.sem_inc(S["issue"], 1)
                dve.max_index(top_at[:], top[:], logit[:]).then_inc(S["topidx"], 1)

            def score_max(n, i):
                dve.wait_ge(S["s"], at(n + 1))
                dve.wait_ge(S["exp"], at(n - 1))
                dve.tensor_reduce(nmax[:, i, :], bank[1 + i][:].rearrange("c (g k) -> c g k", g=2), AX.X, ALU.max,
                                  negate=True).then_inc(S["nb"], 1)

            def normalise(n, i):
                dve.wait_ge(S["exp"], at(n + 1))
                dve.reciprocal(inv[:, i, :], tot[:, i, :]).then_inc(S["rec"], 1)
                dve.wait_ge(S["rec"], at(n + 1))
                for g in range(2):
                    last = dve.tensor_scalar(prob[:, i, g, :], prob[:, i, g, :], inv[:, i, g:g + 1], None, ALU.mult)
                last.then_inc(S["pn"], 1)

            def sums(r):
                return oimg[:, bass.ds(r * CPX, CPX)].rearrange("c (r w) -> c r w", w=W)

            def outputs(n, r, v, tapped):
                dve.wait_ge(S["pv"], at(n + 1))
                dve.wait_ge(S["tapped"], at(tapped))
                here = sums(r)[:, :, WIN * v:WIN * (v + 1)]
                dve.scalar_tensor_tensor(out=here, in0=bank[6][:, 0:WPX].rearrange("c (r q) -> c r q", q=WIN), scalar=V["lepe_b"],
                                         in1=here, op0=ALU.add, op1=ALU.add).then_inc(S["oc"], 1)

            def tap(b, r, k, v):
                if k == 0:
                    dve.wait_ge(S["lepe"], at(NCK * b + r + 1))
                else:
                    dve.wait_ge(S["tapped"], at(DVE_TAPS * (NCK * b + r) + k))
                    if v >= 2:
                        dve.wait_ge(S["oc"], at(NW * b + NWIN * r + v - 1))
                start = bank[7][:, 0:CPX].rearrange("c (r w) -> c r w", w=W) if k == 0 else sums(r)
                dve.scalar_tensor_tensor(out=sums(r), in0=vpad[:, bass.ds(r * WIN + k // 5, WIN), k % 5:k % 5 + W],
                                         scalar=taps5[:, k:k + 1], in1=start, op0=ALU.mult, op1=ALU.add).then_inc(S["tapped"], 1)

            def rest_of_taps(b, r):
                dve.wait_ge(S["lepe2"], at(b + 1))
                dve.wait_ge(S["tapped"], at(DVE_TAPS * (NCK * b + r) + LAST_TAPS))
                dve.wait_ge(S["oc"], at(NW * b + NWIN * r + NWIN - 2))
                dve.tensor_tensor(sums(r), sums(r), bank[7][:, 0:CPX].rearrange("c (r w) -> c r w", w=W), ALU.add)\
                   .then_inc(S["tapped"], DVE_TAPS - LAST_TAPS)

            def residual2(b, c):
                dve.wait_ge(S["wo"], at(NCK * b + c + 1))
                dve.scalar_tensor_tensor(out=dev[:, ck(c)], in0=bank[c % 2][:, 0:CPX], scalar=V["wo_b"], in1=x1[:, ck(c)],
                                         op0=ALU.add, op1=ALU.add).then_inc(S["x2"], 1)

            def deviation2(b, c):
                dve.wait_ge(S["mean2"], at(NCK * b + c + 1))
                dve.tensor_tensor(z[:, ck(c)], dev[:, ck(c)], bank[2][:, 0:CPX], ALU.subtract).then_inc(S["dev2"], 1)

            def norm2(b, c):
                i = NCK * b + c + 1
                dve.wait_ge(S["std2"], at(i))
                dve.tensor_tensor(z[:, ck(c)], z[:, ck(c)], std2(c), ALU.mult).then_inc(S["rn2"], 1)
                dve.wait_ge(S["rn2"], at(i))
                dve.tensor_scalar(z[:, ck(c)], z[:, ck(c)], V["ln2_g"], V["ln2_b"], ALU.mult, ALU.add).then_inc(S["z"], 1)

            def finish(b, c):
                dve.wait_ge(S["m2"], at(NCK * b + c + 1))
                dve.scalar_tensor_tensor(out=oimg[:, ck(c)], in0=bank[7 if c % 2 else 3][:, 0:CPX], scalar=V["mlp_b2"], in1=dev[:, ck(c)],
                                         op0=ALU.add, op1=ALU.add).then_inc(S["fin"], 1)

            with dve.Fori(0, B) as b:
                dve.wait_ge(S["pad"], b + 1)
                for c in range(NCK + 1):
                    if c == NCK - 1:
                        norm(b, 0)
                    if c == NCK:
                        norm(b, 1)
                    if c < NCK:
                        residual(b, c)
                    if c >= 1:
                        deviation(b, c - 1)
                image_values(b, 0)
                norm(b, 2)
                norm(b, 3)
                image_values(b, 1)
                for c in range(4, NCK):
                    norm(b, c)
                    image_values(b, c - 2)
                image_values(b, NCK - 2)
                image_values(b, NCK - 1)
                choose(b)
                dve.wait_ge(S["stored"], 16 * b + START)
                dve.sem_inc(S["issue"], 1)

                def row(r, odd, first, last):
                    for v in range(NWIN):
                        n = b * NW + r * NWIN + v
                        score_max(n, buf(odd, v))
                        taps = LAST_TAPS if last else DVE_TAPS
                        done, end = share(taps, v), share(taps, v + 1)
                        if v >= 2:
                            outputs(n - 2, r, v - 2, DVE_TAPS * (NCK * b + r) + done)
                        elif not first:
                            outputs(n - 2, r - 1, v - 2 + NWIN, DVE_TAPS * (NCK * b + r))
                        tap(b, r, done, v)
                        normalise(n, buf(odd, v))
                        for k in range(done + 1, end):
                            tap(b, r, k, v)
                    if last:
                        rest_of_taps(b, r)

                each_row(dve, row)
                for v in (NWIN - 2, NWIN - 1):
                    outputs(NW * b + NW - NWIN + v, NWIN - 1, v, DVE_TAPS * NCK * (b + 1))
                for c in range(NCK + 1):
                    if c < NCK:
                        residual2(b, c)
                    if c >= 1:
                        deviation2(b, c - 1)
                for c in range(NCK):
                    norm2(b, c)
                for c in range(NCK):
                    finish(b, c)

        @block.scalar
        def _(act):
            for n in ("sq std log log2 kcopy vcopy qz vtc exp ptc sq2 std2 gelu padfree".split()):
                act.sem_inc(S[n], START)
            act.wait_ge(S["zero"], 4)
            act.wait_ge(S["qb"], 1)
            act.wait_ge(S["const"], 144)
            z = y[:].rearrange("c w p -> c (w p)")

            def square(b, c):
                act.wait_ge(S["dev"], at(NCK * b + c + 1))
                if c >= 2:
                    act.wait_ge(S["var"], at(NCK * b + c - 1))
                act.activation(sq[:, c % 2, :], dev[:, ck(c)], ACT.Square).then_inc(S["sq"], 1)

            def log_var(b, c):
                act.wait_ge(S["var"], at(NCK * b + c + 1))
                act.activation(std1(c), bank[4 + c % 2][:, 0:CPX], ACT.Ln, bias=eps[:]).then_inc(S["log"], 1)

            def deviate(b, c):
                act.wait_ge(S["log"], at(NCK * b + c + 1))
                act.activation(std1(c), std1(c), ACT.Exp, scale=-0.5).then_inc(S["std"], 1)

            def copy_kv(b, c):
                act.wait_ge(S["kv"], at(NCK * b + c + 1))
                for t, s, bias in ((0, "kcopy", "k_b"), (1, "vcopy", "v_b")):
                    act.activation(kv[:, NWIN * c:NWIN * (c + 1), t, :], kv_bank(c, t)[:, 0:CPX].rearrange("c (v p) -> c v p", p=WPX),
                                   ACT.Identity, bias=V[bias]).then_inc(S[s], 1)

            def queries(b, r, heads, odd, first=False):
                act.wait_ge(S["q"], at(NCK * b + r + 1))
                act.wait_ge(S["s"], at(NW * b) if first else at(NW * b + NWIN * (r - 1)))
                for h in heads:
                    p = slice(HD * h, HD * (h + 1))
                    last = act.activation(qz[p, odd, :, h, :], bank[0][p, 0:CPX].rearrange("c (v p) -> c v p", p=WPX),
                                          ACT.Identity, bias=qb[p, :], scale=QSCALE)
                last.then_inc(S["qz"], 1)

            def exponent(n, i):
                act.wait_ge(S["nb"], at(n + 1))
                act.wait_ge(S["pt"], at(n - 1))
                for g in range(2):
                    last = act.activation(prob[:, i, g, :], bank[1 + i][:, g * 256:(g + 1) * 256], ACT.Exp,
                                          bias=nmax[:, i, g:g + 1], accum_out=tot[:, i, g:g + 1])
                last.then_inc(S["exp"], 1)

            def turned_values(n, i):
                act.wait_ge(S["vt"], at(n + 1))
                act.wait_ge(S["pv"], at(n - 1))
                act.activation(vT[:, i].rearrange("c g p -> c (g p)"), bank[3][:, 0:2 * C], ACT.Copy).then_inc(S["vtc"], 1)

            def copy_probs(n, i):
                act.wait_ge(S["pt"], at(n + 1))
                act.wait_ge(S["pv"], at(n - 1))
                act.activation(probT[:, i].rearrange("c g p -> c (g p)"), bank[4 + i][:], ACT.Copy).then_inc(S["ptc"], 1)

            def square2(b, c):
                act.wait_ge(S["dev2"], at(NCK * b + c + 1))
                if c >= 2:
                    act.wait_ge(S["var2"], at(NCK * b + c - 1))
                act.activation(sq[:, c % 2, :], z[:, ck(c)], ACT.Square).then_inc(S["sq2"], 1)

            def log_var2(b, c):
                act.wait_ge(S["var2"], at(NCK * b + c + 1))
                act.activation(std2(c), bank[3 + c % 2][:, 0:CPX], ACT.Ln, bias=eps[:]).then_inc(S["log2"], 1)

            def deviate2(b, c):
                act.wait_ge(S["log2"], at(NCK * b + c + 1))
                act.activation(std2(c), std2(c), ACT.Exp, scale=-0.5).then_inc(S["std2"], 1)

            def gelu(b, c):
                act.wait_ge(S["m1"], at(NCK * b + c + 1))
                if c >= 2:
                    act.wait_ge(S["m2"], at(NCK * b + c - 1))
                for j in range(HID):
                    last = act.activation(hid[:, c % 2, j, :], bank[4 + j][:, 0:CPX], ACT.Gelu, bias=V[f"mlp_b1_{j}"])
                last.then_inc(S["gelu"], 1)

            def pad(b):
                act.wait_ge(S["load"], 16 * b + 16)
                act.activation(padded[:, 1:H + 1, 1:W + 1], flat[:].rearrange("c (h w) -> c h w", w=W), ACT.Copy).then_inc(S["pad"], 1)
                act.wait_ge(S["pad"], b + 1)
                act.sem_inc(S["padfree"], 1)

            def image(b, more):
                for c in range(1, NCK + 2):
                    if c <= NCK:
                        square(b, c - 1)
                    if c >= 2:
                        log_var(b, c - 2)
                    if c - 1 == GROUPS[0][1]:
                        for k in range(*GROUPS[0]):
                            deviate(b, k)
                    if c >= NCK:
                        copy_kv(b, c - NCK)
                for k in range(*GROUPS[1]):
                    deviate(b, k)
                for c in range(2, NCK):
                    copy_kv(b, c)
                queries(b, 0, range(0, 2), 0, first=True)
                queries(b, 0, range(2, 4), 0, first=True)

                def row(r, odd, first, last):
                    for v in range(NWIN):
                        n = b * NW + r * NWIN + v
                        if not first or v >= 1:
                            copy_probs(n - 1, buf(odd, v + 1))
                        exponent(n, buf(odd, v))
                        turned_values(n, buf(odd, v))
                        if not last and v in (4, 5):
                            queries(b, r + 1, range(2 * v - 8, 2 * v - 6), 1 - odd)

                each_row(act, row)
                copy_probs(NW * b + NW - 1, 0)
                if more:
                    act.wait_ge(S["x1"], at(NCK * (b + 1)))
                    pad(b + 1)
                for c in range(1, NCK + 2):
                    if c <= NCK:
                        square2(b, c - 1)
                    if c >= 2:
                        log_var2(b, c - 2)
                for c in range(NCK):
                    deviate2(b, c)
                for c in range(NCK):
                    gelu(b, c)

            pad(0)
            with act.Fori(0, B - 1) as b:
                image(b, True)
            image(B - 1, False)



VEC0 = ["pos_b", "ln1_g", "ln1_b", "q_b", "k_b", "v_b", "lepe_b", "wo_b", "ln2_g", "ln2_b", "mlp_b2", "mlp_b1_0", "mlp_b1_1", "mlp_b1_2"]
KX = W // 2 + 1
SHRINK = 0.01
KXG = [(0, 8), (8, 8), (16, 8), (24, KX - 24)]
STAGES = [("fw", HW // TPX), ("fh", KX), ("ih", KX), ("iw", HW // TPX)]


def groups_of_four(units):
    return [(k, min(4, units - k)) for k in range(0, units, 4)]


def fourier_phase(nc, B, conv_d, x_img, w, out_img, peak_d):
    with ExitStack() as ctx:
        sb = lambda name, shape, dt=F32: ctx.enter_context(nc.sbuf_tensor("fo_" + name, shape, dt))
        ps = lambda name, shape, dt=F32: ctx.enter_context(nc.psum_tensor("fo_" + name, shape, dt))
        sem = lambda name: ctx.enter_context(nc.semaphore("fo_" + name))
        ident = sb("ident", [C, C])
        group_mean = sb("group_mean", [C, C])
        vec = sb("vec", [C, len(VEC2)])
        V = {n: vec[:, k:k + 1] for k, n in enumerate(VEC2)}
        mats = {"fw": sb("m_fw", [2 * W, 4 * KX]), "fh": sb("m_fh", [2 * H, 2 * H]), "ih": sb("m_ih", [2 * H, 2 * H]), "iw": sb("m_iw", [4 * KX, 2 * W])}
        blocks = sb("blocks", [C, 4, C])
        minus = sb("minus", [C, 2, C])
        eps = sb("eps", [C, 1])
        conv = sb("conv", [C, NCK, CPX])
        xin = sb("xin", [C, HW])
        scratch = sb("scratch", [C, HW])
        img = sb("img", [C, HW])
        half = sb("half", [C, KX * H * 2])
        freq = sb("freq", [C, 2, KX, H])
        mixed = sb("mixed", [C, KX, 2, H])
        res = sb("res", [C, HW])
        turned = sb("turned", [C, 2, 4, C])
        hid = sb("hid", [C, 2, 2, 448])
        val = sb("val", [C, 2, 2, 448])
        cut = sb("cut", [C, 2, 448])
        pro = sb("pro", [C, 2, 448])
        prx = sb("prx", [C, 2, 448])
        stat = sb("stat", [C, 8])
        peak = sb("peak", [C, 2])
        bank = [ps(f"bank{k}", [C, 512]) for k in range(8)]
        names = ("const zero load loadfree sum sq m1 m2 small gn relu turn turnc prod prodc l1 relu1 l2 val shrunk cut pr yr px yi "
                 "peak peaks held stored neg issue root").split()
        S = {n: sem(n) for n in names}
        block = ctx.enter_context(nc.Block())
        GR = sum(len(groups_of_four(u)) for _, u in STAGES)
        first = {}
        k = 0
        for name, u in STAGES:
            first[name] = k
            k += len(groups_of_four(u))
        MX = len(KXG)
        PIECES = [slice(k * HW // 4, (k + 1) * HW // 4) for k in range(4)]

        def images(eng, body):
            with eng.Fori(0, B - 1) as b:
                body(b, True)
            body(B - 1, False)


        def dest(name, g0, m):
            if name == "fw":
                return half[:].rearrange("c (k h p) -> c k (h p)", k=KX, p=2)[:, :, 4 * g0:4 * (g0 + m)].rearrange("c k (t q) -> c t k q", q=4)
            if name == "fh":
                return freq[:, :, g0:g0 + m, :].rearrange("c p k y -> c k p y")
            if name == "ih":
                return half[:].rearrange("c (h k p) -> c k h p", k=KX, p=2)[:, g0:g0 + m, :, :]

        def columns(name, g, m):
            n = mats[name].shape[1]
            b = bank[2 + (first[name] + g) % 2][:, 0:m * n]
            if name == "fw":
                return b.rearrange("c (t k q) -> c t k q", t=m, q=4)
            if name == "fh":
                return b.rearrange("c (k p y) -> c k p y", k=m, p=2)
            if name == "ih":
                return b.rearrange("c (k h p) -> c k h p", k=m, p=2)
            return b

        def unit(name, t):
            if name == "fw":
                return img[:, t * TPX:(t + 1) * TPX]
            if name == "fh":
                return half[:, t * 2 * H:(t + 1) * 2 * H]
            if name == "ih":
                return mixed[:, t, :, :].rearrange("c p y -> c (p y)")
            return half[:, t * 4 * KX:(t + 1) * 4 * KX]

        @block.sync
        def _(sp):
            for dst, src in ((ident, "ident"), (group_mean, "group_mean"), (vec, "vec2"), (mats["fw"], "dft_fw"), (mats["fh"], "dft_fh"),
                             (mats["ih"], "dft_ih"), (mats["iw"], "dft_iw"), (blocks, "blocks")):
                sp.dma_start(dst[:], w[src]).then_inc(S["const"], 16)
            with sp.Fori(0, B) as b:
                sp.wait_ge(S["gn"], at(b))
                sp.dma_start(conv[:], conv_d[bass.ds(b, 1)].rearrange("o k c n -> c (o k) n")).then_inc(S["load"], 16)
                sp.dma_start(xin[:], x_img[bass.ds(b, 1)].rearrange("o c n -> (o c) n")).then_inc(S["load"], 16)

        @block.gpsimd
        def _(pool):
            pool.memset(eps[:], GN_EPS).then_inc(S["zero"], 1)
            pool.memset(peak[:], 0.0).then_inc(S["zero"], 1)
            pool.sem_inc(S["px"], START)
            pool.sem_inc(S["yi"], START)
            pool.sem_inc(S["held"], START)
            with pool.Fori(0, B) as b:
                pool.wait_ge(S["relu"], at(b + 1))
                pool.wait_ge(S["stored"], 16 * b + START)
                pool.wait_ge(S["peak"], at(b))
                pool.sem_inc(S["issue"], 1)
                pool.tensor_copy(res[:], img[:]).then_inc(S["held"], 1)
                for m, (k0, kn) in enumerate(KXG):
                    n = kn * H
                    part = lambda a: a.rearrange("c k y -> c (k y)")
                    pool.wait_ge(S["shrunk"], at(MX * b + m + 1))
                    pool.wait_ge(S["yi"], at(MX * b + m))
                    pool.tensor_tensor(prx[:, 0, 0:n], val[:, m % 2, 0, 0:n], part(freq[:, 1, k0:k0 + kn, :]), ALU.mult)
                    pool.tensor_tensor(prx[:, 1, 0:n], val[:, m % 2, 1, 0:n], part(freq[:, 0, k0:k0 + kn, :]), ALU.mult).then_inc(S["px"], 1)
                    pool.wait_ge(S["px"], at(MX * b + m + 1))
                    pool.tensor_tensor(mixed[:, k0:k0 + kn, 1, :], prx[:, 0, 0:n].rearrange("c (k y) -> c k y", y=H),
                                       prx[:, 1, 0:n].rearrange("c (k y) -> c k y", y=H), ALU.add).then_inc(S["yi"], 1)

        @block.tensor
        def _(pe):
            for n in "m1 m2 turn prod l1 l2".split():
                pe.sem_inc(S[n], START)
            pe.wait_ge(S["const"], 128)
            pe.wait_ge(S["neg"], 1)

            def turn(b, name, g):
                n = GR * b + first[name] + g
                g0, m = groups_of_four(dict(STAGES)[name])[g]
                pe.wait_ge(S["turnc"], at(n - 1))
                for k in range(m):
                    src = unit(name, g0 + k)
                    last = pe.transpose(bank[(first[name] + g) % 2][0:src.shape[1], k * C:(k + 1) * C], src, ident[:])
                last.then_inc(S["turn"], 1)

            def product(b, name, g):
                n = GR * b + first[name] + g
                g0, m = groups_of_four(dict(STAGES)[name])[g]
                rows, cols = mats[name].shape
                pe.wait_ge(S["turnc"], at(n + 1))
                pe.wait_ge(S["prodc"], at(n - 1))
                for k in range(m):
                    last = pe.matmul(bank[2 + (first[name] + g) % 2][:, k * cols:(k + 1) * cols],
                                     turned[0:rows, (first[name] + g) % 2, k, :], mats[name][:], start=True, stop=True)
                last.then_inc(S["prod"], 1)

            def transform(b, name, before=lambda g: None):
                G = len(groups_of_four(dict(STAGES)[name]))
                for g in range(G + 1):
                    if g < G:
                        before(g)
                        turn(b, name, g)
                    if g >= 1:
                        product(b, name, g - 1)

            def mix_first(b, m):
                k0, kn = KXG[m]
                n = kn * H
                part = lambda p: freq[:, p, k0:k0 + kn, :].rearrange("c k y -> c (k y)")
                pe.wait_ge(S["relu1"], at(MX * b + m))
                for o, terms in enumerate((((blocks[:, 0], 0), (minus[:, 0], 1)), ((blocks[:, 0], 1), (blocks[:, 1], 0)))):
                    for k, (mat, p) in enumerate(terms):
                        last = pe.matmul(bank[4 + o][:, 0:n], mat, part(p), start=(k == 0), stop=(k == 1))
                last.then_inc(S["l1"], 1)

            def mix_second(b, m):
                k0, kn = KXG[m]
                n = kn * H
                pe.wait_ge(S["relu1"], at(MX * b + m + 1))
                pe.wait_ge(S["val"], at(MX * b + m))
                for o, terms in enumerate((((blocks[:, 2], 0), (minus[:, 1], 1)), ((blocks[:, 2], 1), (blocks[:, 3], 0)))):
                    for k, (mat, p) in enumerate(terms):
                        last = pe.matmul(bank[6 + o][:, 0:n], mat, hid[:, m % 2, p, 0:n], start=(k == 0), stop=(k == 1))
                last.then_inc(S["l2"], 1)

            def mean(b):
                pe.wait_ge(S["sum"], at(b + 1))
                pe.matmul(bank[7][:, 0:1], group_mean[:], stat[:, 0:1], start=True, stop=True).then_inc(S["m1"], 1)
                pe.wait_ge(S["small"], at(4 * b + 1))

            def variance(b):
                pe.wait_ge(S["sq"], at(b + 1))
                pe.matmul(bank[4][:, 0:1], group_mean[:], stat[:, 2:3], start=True, stop=True).then_inc(S["m2"], 1)

            def image(b, more):
                pe.wait_ge(S["relu"], at(b + 1))
                transform(b, "fw")
                pe.wait_ge(S["prodc"], at(GR * b + first["fh"]))
                transform(b, "fh")
                pe.wait_ge(S["prodc"], at(GR * b + first["ih"]))
                for m in range(MX + 1):
                    if m < MX:
                        mix_first(b, m)
                    if m == 0 and more:
                        pe.wait_ge(S["val"], at(MX * b))
                        mean(b + 1)
                    if m >= 1:
                        mix_second(b, m - 1)

                def mixed_by(g):
                    pe.wait_ge(S["yr"], at(MX * b + g // 2 + 1))
                    pe.wait_ge(S["yi"], at(MX * b + g // 2 + 1))
                    if g == 1 and more:
                        variance(b + 1)

                transform(b, "ih", mixed_by)
                pe.wait_ge(S["prodc"], at(GR * b + first["iw"]))
                transform(b, "iw")

            mean(0)
            variance(0)
            images(pe, image)

        @block.vector
        def _(dve):
            for n in "small peaks gn prodc shrunk cut pr yr peak".split():
                dve.sem_inc(S[n], START)
            dve.wait_ge(S["const"], 128)
            dve.wait_ge(S["zero"], 2)
            dve.tensor_scalar(minus[:, 0], blocks[:, 1], -1.0, None, ALU.mult)
            dve.tensor_scalar(minus[:, 1], blocks[:, 3], -1.0, None, ALU.mult).then_inc(S["neg"], 1)

            def collect(b, name, between=lambda g: None):
                for g, (g0, m) in enumerate(groups_of_four(dict(STAGES)[name])):
                    n = GR * b + first[name] + g
                    dve.wait_ge(S["prod"], at(n + 1))
                    if name == "iw":
                        px = slice(g0 * TPX, (g0 + m) * TPX)
                        dve.tensor_tensor(res[:, px], columns(name, g, m), res[:, px], ALU.add).then_inc(S["prodc"], 1)
                    else:
                        dve.tensor_copy(dest(name, g0, m), columns(name, g, m)).then_inc(S["prodc"], 1)
                    between(g)

            def shrink(b, m):
                k0, kn = KXG[m]
                n = kn * H
                i = MX * b + m + 1
                v = val[:, m % 2, :, 0:n]
                dve.wait_ge(S["val"], at(i))
                dve.tensor_scalar(cut[:, :, 0:n], v, SHRINK, -SHRINK, ALU.min, ALU.max).then_inc(S["cut"], 1)
                dve.wait_ge(S["cut"], at(i))
                dve.tensor_tensor(v, v, cut[:, :, 0:n], ALU.subtract).then_inc(S["shrunk"], 1)
                dve.wait_ge(S["shrunk"], at(i))
                dve.tensor_tensor(pro[:, :, 0:n], v, freq[:, :, k0:k0 + kn, :].rearrange("c p k y -> c p (k y)"), ALU.mult).then_inc(S["pr"], 1)
                dve.wait_ge(S["pr"], at(i))
                dve.tensor_tensor(mixed[:, k0:k0 + kn, 0, :], pro[:, 0, 0:n].rearrange("c (k y) -> c k y", y=H),
                                  pro[:, 1, 0:n].rearrange("c (k y) -> c k y", y=H), ALU.subtract).then_inc(S["yr"], 1)

            def small(b, k, instruction):
                instruction.then_inc(S["small"], 1)
                dve.wait_ge(S["small"], at(4 * b + k))

            def minus_mean(b):
                dve.wait_ge(S["m1"], at(b + 1))
                small(b, 1, dve.tensor_scalar(stat[:, 1:2], bank[7][:, 0:1], -1.0, None, ALU.mult))

            def scale_and_shift(b):
                dve.wait_ge(S["relu"], at(b))
                dve.wait_ge(S["root"], b + 1)
                small(b, 2, dve.reciprocal(stat[:, 4:5], stat[:, 3:4]))
                small(b, 3, dve.tensor_tensor(stat[:, 5:6], stat[:, 4:5], V["gamma"], ALU.mult))
                small(b, 4, dve.scalar_tensor_tensor(out=stat[:, 6:7], in0=stat[:, 5:6], scalar=stat[:, 1:2], in1=V["beta"], op0=ALU.mult, op1=ALU.add))

            def norm(px):
                return dve.scalar_tensor_tensor(out=img[:, px], in0=conv[:].rearrange("c k n -> c (k n)")[:, px], scalar=stat[:, 5:6],
                                                in1=xin[:, px], op0=ALU.mult, op1=ALU.add)

            def image(b, more):
                collect(b, "fw")
                collect(b, "fh")
                if more:
                    minus_mean(b + 1)
                for m in range(MX):
                    shrink(b, m)
                if more:
                    scale_and_shift(b + 1)
                    dve.wait_ge(S["held"], at(b + 1))

                def norm_next(g):
                    if more and g % 2 and g // 2 < len(PIECES):
                        piece = norm(PIECES[g // 2])
                        if g // 2 == len(PIECES) - 1:
                            piece.then_inc(S["gn"], 1)

                collect(b, "ih", norm_next)
                dve.wait_ge(S["held"], at(b + 1))
                collect(b, "iw")
                dve.wait_ge(S["prodc"], at(GR * (b + 1)))
                dve.tensor_reduce(peak[:, 1:2], res[:], AX.X, ALU.max, apply_absolute_value=True).then_inc(S["peaks"], 1)
                dve.wait_ge(S["peaks"], at(b + 1))
                dve.tensor_tensor(peak[:, 0:1], peak[:, 0:1], peak[:, 1:2], ALU.max).then_inc(S["peak"], 1)

            minus_mean(0)
            scale_and_shift(0)
            norm(slice(0, HW)).then_inc(S["gn"], 1)
            images(dve, image)

        @block.scalar
        def _(act):
            for n in "sum sq relu turnc relu1 val stored".split():
                act.sem_inc(S[n], START)
            act.wait_ge(S["const"], 128)
            act.wait_ge(S["zero"], 2)

            def copy_turned(b, name, between=lambda g: None):
                for g, (g0, m) in enumerate(groups_of_four(dict(STAGES)[name])):
                    n = GR * b + first[name] + g
                    rows = mats[name].shape[0]
                    act.wait_ge(S["turn"], at(n + 1))
                    act.wait_ge(S["prod"], at(n - 1))
                    act.activation(turned[0:rows, (first[name] + g) % 2, 0:m, :], bank[(first[name] + g) % 2][0:rows, 0:m * C].rearrange("r (k c) -> r k c", c=C),
                                   ACT.Copy).then_inc(S["turnc"], 1)
                    between(g)

            def mix(b):
                for m in range(MX + 1):
                    if m < MX:
                        n = KXG[m][1] * H
                        act.wait_ge(S["l1"], at(MX * b + m + 1))
                        if m >= 2:
                            act.wait_ge(S["l2"], at(MX * b + m - 1))
                        act.activation(hid[:, m % 2, 0, 0:n], bank[4][:, 0:n], ACT.Relu, bias=V["b1r"])
                        act.activation(hid[:, m % 2, 1, 0:n], bank[5][:, 0:n], ACT.Relu, bias=V["b1i"]).then_inc(S["relu1"], 1)
                    if m >= 1:
                        j = m - 1
                        n = KXG[j][1] * H
                        act.wait_ge(S["l2"], at(MX * b + j + 1))
                        if j >= 2:
                            act.wait_ge(S["yr"], at(MX * b + j - 1))
                            act.wait_ge(S["yi"], at(MX * b + j - 1))
                        act.activation(val[:, j % 2, 0, 0:n], bank[6][:, 0:n], ACT.Identity, bias=V["b2r"])
                        act.activation(val[:, j % 2, 1, 0:n], bank[7][:, 0:n], ACT.Identity, bias=V["b2i"]).then_inc(S["val"], 1)

            def sum_values(b):
                act.wait_ge(S["load"], 32 * b + 32)
                act.activation(scratch[:], conv[:].rearrange("c k n -> c (k n)"), ACT.Copy, accum_out=stat[:, 0:1]).then_inc(S["sum"], 1)

            def sum_squares(b):
                act.wait_ge(S["small"], at(4 * b + 1))
                act.wait_ge(S["sum"], at(b + 1))
                act.activation(scratch[:], conv[:].rearrange("c k n -> c (k n)"), ACT.Square, bias=stat[:, 1:2], accum_out=stat[:, 2:3]).then_inc(S["sq"], 1)

            def root(b):
                act.wait_ge(S["m2"], at(b + 1))
                act.activation(stat[:, 3:4], bank[4][:, 0:1], ACT.Sqrt, bias=eps[:]).then_inc(S["root"], 1)

            def positive(b, px):
                return act.activation(img[:, px], img[:, px], ACT.Relu, bias=stat[:, 6:7])

            def image(b, more):
                copy_turned(b, "fw")
                copy_turned(b, "fh")
                if more:
                    sum_values(b + 1)
                mix(b)
                if more:
                    sum_squares(b + 1)
                    root(b + 1)
                copy_turned(b, "ih")
                if more:
                    act.wait_ge(S["gn"], at(b + 2))

                def positive_next(g):
                    if more and g < len(PIECES):
                        piece = positive(b + 1, PIECES[g])
                        if g == len(PIECES) - 1:
                            piece.then_inc(S["relu"], 1)

                copy_turned(b, "iw", positive_next)
                act.wait_ge(S["prodc"], at(GR * (b + 1)))
                act.dma_start(out_img[bass.ds(b, 1)].rearrange("o c n -> (o c) n"), res[:]).then_inc(S["stored"], 16)

            sum_values(0)
            sum_squares(0)
            root(0)
            act.wait_ge(S["gn"], at(1))
            positive(0, slice(0, HW)).then_inc(S["relu"], 1)
            images(act, image)
            act.wait_ge(S["peak"], at(B))
            act.wait_ge(S["stored"], 16 * B + START)
            act.dma_start(peak_d, peak[:, 0:1]).then_inc(S["stored"], 16)
            act.wait_ge(S["stored"], 16 * B + 16 + START)


VEC2 = ["gamma", "beta", "b1r", "b1i", "b2r", "b2i"]


def transform_matrices():
    import numpy as np
    n = np.arange(W)
    root = np.sqrt(float(W))
    fw = np.zeros((2, W, KX, 2, 2))
    ang = 2 * np.pi * np.outer(n, np.arange(KX)) / W
    for r in range(2):
        fw[r, :, :, r, 0] = np.cos(ang) / root
        fw[r, :, :, r, 1] = -np.sin(ang) / root
    ang = 2 * np.pi * np.outer(n, n) / H
    co, si = np.cos(ang) / root, np.sin(ang) / root
    fh = np.zeros((H, 2, 2, H))
    fh[:, 0, 0], fh[:, 0, 1], fh[:, 1, 0], fh[:, 1, 1] = co, -si, si, co
    ih = np.zeros((2, H, H, 2))
    ih[0, :, :, 0], ih[0, :, :, 1], ih[1, :, :, 0], ih[1, :, :, 1] = co, si, -si, co
    iw = np.zeros((2, KX, 2, 2, W))
    ang = 2 * np.pi * np.outer(np.arange(KX), n) / W
    weight = np.full((KX, 1), 2.0)
    weight[0] = weight[-1] = 1.0
    sine = np.sin(ang)
    sine[0] = sine[-1] = 0.0
    for r in range(2):
        iw[r, :, 0, r] = weight * np.cos(ang) / root
        iw[r, :, 1, r] = -weight * sine / root
    f = lambda a, r, c: np.ascontiguousarray(a.reshape(r, c).astype(np.float32))
    return {"dft_fw": f(fw, 2 * W, 4 * KX), "dft_fh": f(fh, 2 * H, 2 * H), "dft_ih": f(ih, 2 * H, 2 * H), "dft_iw": f(iw, 4 * KX, 2 * W)}
Q8, Q4 = 127.0, 7.0
VEC3 = ["b1", "pb1", "b2", "pb2"]


def quantised_phase(nc, B, x_img, peak_d, w, out_img):
    with ExitStack() as ctx:
        sb = lambda name, shape, dt=F32: ctx.enter_context(nc.sbuf_tensor("qu_" + name, shape, dt))
        ps = lambda name, shape, dt=F32: ctx.enter_context(nc.psum_tensor("qu_" + name, shape, dt))
        ident = sb("ident", [C, C])
        vec = sb("vec", [C, len(VEC3)])
        V = {n: vec[:, k:k + 1] for k, n in enumerate(VEC3)}
        raw = {"w1": sb("raw_w1", [C, 9]), "p1": sb("raw_p1", [C, C]), "w2": sb("raw_w2", [C, 9]), "p2": sb("raw_p2", [C, C])}
        whole = {n: sb("whole_" + n, list(a.shape)) for n, a in raw.items()}
        point = {n: sb("point_" + n, [C, C], BF16) for n in ("p1", "p2")}
        diag = {n: sb("diag_" + n, [C, 9, C], BF16) for n in ("w1", "w2")}
        peaks = sb("peaks", [C, 5])
        tops = sb("tops", [C, 5])
        scale = sb("scale", [C, 5])
        inv = sb("inv", [C, 5])
        hi = sb("hi", [C, 2])
        lo = sb("lo", [C, 2])
        few = sb("few", [C, 16])
        held = sb("held", [C, B * HW], I16)
        held_q = held[:].bitcast(BF16)
        xin = sb("xin", [C, 2, HW])
        real = sb("real", [C, 2, HW])
        padded = sb("padded", [C, 2, HP, HP], BF16)
        quant = sb("quant", [C, 2, HW], BF16)
        relued = sb("relued", [C, 4, CPX])
        chunk_hi = sb("chunk_hi", [C, NCK])
        bank = [ps(f"bank{k}", [C, 512]) for k in range(8)]
        ck = lambda c: slice(c * CPX, (c + 1) * CPX)
        back4 = lambda c: {0: 3, 1: 3, 2: 3, 3: NCK}.get(c, 4)
        img = lambda b: bass.ds(b * HW, HW)
        rows = lambda a: a.rearrange("c (h w) -> c h w", w=W)

        def one_ahead(eng, start, finish):
            start(0, 0)
            if B > 2:
                with eng.Fori(0, B // 2 - 1) as pair:
                    start(pair, 1)
                    finish(pair, 0)
                    start(pair + 1, 0)
                    finish(pair, 1)
            start(B // 2 - 1, 1)
            finish(B // 2 - 1, 0)
            finish(B // 2 - 1, 1)

        def scales(name, program):
            with ExitStack() as inner:
                s_step = inner.enter_context(nc.semaphore(f"qu_{name}_step"))
                s_ask = inner.enter_context(nc.semaphore(f"qu_{name}_ask"))
                s_top = inner.enter_context(nc.semaphore(f"qu_{name}_top"))
                s_in = inner.enter_context(nc.semaphore(f"qu_{name}_in"))
                block = inner.enter_context(nc.Block())
                loads, before, width, after = program

                @block.sync
                def _(sp):
                    for dst, src in loads:
                        sp.dma_start(dst, src).then_inc(s_in, 16)

                @block.gpsimd
                def _(pool):
                    if name == "start":
                        pool.memset(padded[:], 0.0).then_inc(s_in, 1)
                    pool.wait_ge(s_ask, 1)
                    pool.partition_all_reduce(tops[:, 0:width], peaks[:, 0:width], C, bass.bass_isa.ReduceOp.max).then_inc(s_top, 1)

                @block.vector
                def _(dve):
                    count = [0]

                    def step(instruction):
                        count[0] += 1
                        instruction.then_inc(s_step, 1)
                        dve.wait_ge(s_step, count[0])

                    dve.wait_ge(s_in, 16 * len(loads) + (name == "start"))
                    before(dve, step)
                    dve.sem_inc(s_ask, 1)
                    dve.wait_ge(s_top, 1)
                    after(dve, step)

        def start_before(dve, step):
            for k, n in enumerate(("w1", "p1", "w2", "p2")):
                step(dve.tensor_reduce(peaks[:, k + 1:k + 2], raw[n][:], AX.X, ALU.max, apply_absolute_value=True))

        def start_after(dve, step):
            step(dve.tensor_scalar(scale[:, 0:1], tops[:, 0:1], 1.0 / Q8, 1e-8, ALU.mult, ALU.max))
            step(dve.tensor_scalar(scale[:, 1:5], tops[:, 1:5], 1.0 / Q4, 1e-8, ALU.mult, ALU.max))
            step(dve.reciprocal(inv[:], scale[:]))
            for k, n in enumerate(("w1", "p1", "w2", "p2")):
                q = whole[n][:]
                step(dve.tensor_scalar(q, raw[n][:], inv[:, k + 1:k + 2], ROUND, ALU.mult, ALU.add))
                step(dve.tensor_scalar(q, q, ROUND, Q4, ALU.subtract, ALU.min))
                if n in point:
                    step(dve.tensor_scalar(point[n][:], q, -Q4 - 1.0, None, ALU.max))
                else:
                    step(dve.tensor_scalar(q, q, -Q4 - 1.0, None, ALU.max))
                    for t in range(9):
                        step(dve.tensor_scalar(diag[n][:, t, :], ident[:], q[:, t:t + 1], None, ALU.mult))
            step(dve.tensor_tensor(few[:, 0:1], scale[:, 0:1], scale[:, 1:2], ALU.mult))

        def ends_before(bias):
            def before(dve, step):
                step(dve.scalar_tensor_tensor(out=few[:, 2:3], in0=hi[:, 0:1], scalar=few[:, 0:1], in1=V[bias], op0=ALU.mult, op1=ALU.add))
                step(dve.scalar_tensor_tensor(out=few[:, 3:4], in0=lo[:, 0:1], scalar=few[:, 0:1], in1=V[bias], op0=ALU.mult, op1=ALU.add))
                step(dve.tensor_reduce(peaks[:, 0:1], few[:, 2:4], AX.X, ALU.max, apply_absolute_value=True))
            return before

        def relu_before(bias):
            def before(dve, step):
                step(dve.scalar_tensor_tensor(out=few[:, 2:3], in0=hi[:, 0:1], scalar=few[:, 0:1], in1=V[bias], op0=ALU.mult, op1=ALU.add))
                step(dve.tensor_scalar(peaks[:, 0:1], few[:, 2:3], 0.0, None, ALU.max))
            return before

        def next_after(bias, k):
            def after(dve, step):
                step(dve.tensor_scalar(scale[:, 0:1], tops[:, 0:1], 1.0 / Q8, 1e-8, ALU.mult, ALU.max))
                step(dve.reciprocal(inv[:, 0:1], scale[:, 0:1]))
                step(dve.tensor_tensor(few[:, 4:5], few[:, 0:1], inv[:, 0:1], ALU.mult))
                step(dve.tensor_tensor(few[:, 5:6], V[bias], inv[:, 0:1], ALU.mult))
                step(dve.tensor_tensor(few[:, 0:1], scale[:, 0:1], scale[:, k:k + 1], ALU.mult))
            return after

        def sums_pass(first):
            with ExitStack() as inner:
                tag = "a" if first else "c"
                names = "load real quant sums copied point best free issue".split()
                S = {n: inner.enter_context(nc.semaphore(f"qu_{tag}_{n}")) for n in names}
                s_load = [inner.enter_context(nc.semaphore(f"qu_{tag}_load{j}")) for j in range(2)]
                block = inner.enter_context(nc.Block())
                dw = diag["w1" if first else "w2"]

                if first:
                    @block.sync
                    def _(sp):
                        with sp.Fori(0, B // 2) as pair:
                            for j in range(2):
                                b = pair * 2 + j
                                sp.wait_ge(S["real"], at(b - 1))
                                sp.dma_start(xin[:, j, :], x_img[bass.ds(b, 1)].rearrange("o c n -> (o c) n")).then_inc(s_load[j], 16)

                @block.tensor
                def _(pe):
                    pe.sem_inc(S["sums"], START)
                    pe.sem_inc(S["point"], START)

                    def pointwise(pair, j):
                        b = pair * 2 + j
                        if not first:
                            for c in range(NCK):
                                pe.wait_ge(S["real"], at(NCK * b + c - back4(c) + 1))
                                pe.matmul(bank[c % 4][:, 0:CPX], point["p1"][:], held_q[:, bass.ds(b * HW + c * CPX, CPX)],
                                          start=True, stop=True).then_inc(S["point"], 1)

                    def depthwise(pair, j):
                        b = pair * 2 + j
                        pe.wait_ge(S["quant"], at((b + 1) * (1 if first else NCK)))
                        for c in range(NCK):
                            pe.wait_ge(S["copied"], at(NCK * b + c - back4(c) + 1))
                            for k in range(9):
                                last = pe.matmul(bank[4 + c % 4][:, 0:CPX], dw[:, k, :],
                                                 padded[:, j, WIN * c + k // 3:WIN * c + k // 3 + WIN, k % 3:k % 3 + W], start=(k == 0), stop=(k == 8))
                            last.then_inc(S["sums"], 1)

                    one_ahead(pe, pointwise, depthwise)

                @block.scalar
                def _(act):
                    act.sem_inc(S["real"], START)
                    act.sem_inc(S["copied"], START)

                    def collect(pair, j):
                        b = pair * 2 + j
                        act.wait_ge(S["best"], at(b))
                        for c in range(NCK):
                            act.wait_ge(S["sums"], at(NCK * b + c + 1))
                            act.sem_inc(S["issue"], 1)
                            act.activation(held[:, bass.ds(b * HW + c * CPX, CPX)], bank[4 + c % 4][:, 0:CPX], ACT.Copy).then_inc(S["copied"], 1)

                    def scaled(pair, j):
                        b = pair * 2 + j
                        if first:
                            act.wait_ge(s_load[j], 16 * pair + 16)
                            act.wait_ge(S["quant"], at(b - 1))
                            act.activation(real[:, j, :], xin[:, j, :], ACT.Copy, scale=inv[:, 0:1]).then_inc(S["real"], 1)
                        else:
                            for c in range(NCK):
                                act.wait_ge(S["point"], at(NCK * b + c + 1))
                                act.wait_ge(S["quant"], at(NCK * b + c - NCK + 1))
                                act.activation(real[:, 0, ck(c)], bank[c % 4][:, 0:CPX], ACT.Relu, bias=few[:, 5:6], scale=few[:, 4:5]).then_inc(S["real"], 1)

                    one_ahead(act, scaled, collect)

                @block.vector
                def _(dve):
                    dve.sem_inc(S["quant"], START)
                    dve.sem_inc(S["best"], START)
                    dve.memset(hi[:], -3.0e38).then_inc(S["free"], 1)
                    dve.memset(lo[:], 3.0e38).then_inc(S["free"], 1)
                    dve.wait_ge(S["free"], 2)

                    def search(pair, j):
                        b = pair * 2 + j
                        dve.wait_ge(S["copied"], at(NCK * (b + 1)))
                        dve.tensor_reduce(hi[:, 1:2], held[:, img(b)], AX.X, ALU.max).then_inc(S["free"], 1)
                        dve.tensor_reduce(lo[:, 1:2], held[:, img(b)], AX.X, ALU.min).then_inc(S["free"], 1)
                        dve.wait_ge(S["free"], 4 * b + 4)
                        dve.tensor_tensor(hi[:, 0:1], hi[:, 0:1], hi[:, 1:2], ALU.max).then_inc(S["free"], 1)
                        dve.tensor_tensor(lo[:, 0:1], lo[:, 0:1], lo[:, 1:2], ALU.min).then_inc(S["free"], 1)
                        dve.wait_ge(S["free"], 4 * b + 6)
                        dve.sem_inc(S["best"], 1)

                    def rounded(pair, j):
                        b = pair * 2 + j
                        dve.wait_ge(S["sums"], at(NCK * b - NCK))
                        if first:
                            dve.wait_ge(S["real"], at(b + 1))
                            dve.tensor_scalar(padded[:, j, 1:H + 1, 1:W + 1], rows(real[:, j, :]), ROUND, ROUND, ALU.add, ALU.subtract).then_inc(S["quant"], 1)
                        else:
                            for c in range(NCK):
                                dve.wait_ge(S["real"], at(NCK * b + c + 1))
                                dve.tensor_scalar(padded[:, j, WIN * c + 1:WIN * (c + 1) + 1, 1:W + 1], rows(real[:, 0, ck(c)]),
                                                  ROUND, ROUND, ALU.add, ALU.subtract).then_inc(S["quant"], 1)

                    one_ahead(dve, rounded, search)

        def peak_pass():
            with ExitStack() as inner:
                S = {n: inner.enter_context(nc.semaphore(f"qu_b_{n}")) for n in "real quant point best free issue".split()}
                block = inner.enter_context(nc.Block())

                @block.scalar
                def _(act):
                    act.sem_inc(S["real"], START)
                    with act.Fori(0, B // 2) as pair:
                        for j in range(2):
                            b = pair * 2 + j
                            act.wait_ge(S["quant"], at(b - 1))
                            act.sem_inc(S["issue"], 1)
                            act.activation(real[:, j, :], held[:, img(b)], ACT.Identity, bias=few[:, 5:6], scale=few[:, 4:5]).then_inc(S["real"], 1)

                @block.tensor
                def _(pe):
                    pe.sem_inc(S["point"], START)
                    with pe.Fori(0, B) as b:
                        pe.wait_ge(S["quant"], at(b + 1))
                        for c in range(NCK):
                            pe.wait_ge(S["best"], at(NCK * b + c - NCK + 1))
                            pe.matmul(bank[c][:, 0:CPX], point["p1"][:], held_q[:, bass.ds(b * HW + c * CPX, CPX)],
                                      start=True, stop=True).then_inc(S["point"], 1)

                @block.vector
                def _(dve):
                    dve.sem_inc(S["quant"], START)
                    dve.sem_inc(S["best"], START)
                    dve.memset(hi[:], -3.0e38).then_inc(S["free"], 1)
                    dve.wait_ge(S["free"], 1)

                    def rounded(pair, j):
                        b = pair * 2 + j
                        dve.wait_ge(S["real"], at(b + 1))
                        dve.tensor_scalar(held_q[:, img(b)], real[:, j, :], ROUND, ROUND, ALU.add, ALU.subtract).then_inc(S["quant"], 1)

                    def search(pair, j):
                        b = pair * 2 + j
                        for c in range(NCK):
                            dve.wait_ge(S["point"], at(NCK * b + c + 1))
                            dve.tensor_reduce(chunk_hi[:, c:c + 1], bank[c][:, 0:CPX], AX.X, ALU.max).then_inc(S["best"], 1)
                        dve.wait_ge(S["best"], at(NCK * (b + 1)))
                        dve.tensor_reduce(hi[:, 1:2], chunk_hi[:], AX.X, ALU.max).then_inc(S["free"], 1)
                        dve.wait_ge(S["free"], 2 * b + 2)
                        dve.tensor_tensor(hi[:, 0:1], hi[:, 0:1], hi[:, 1:2], ALU.max).then_inc(S["free"], 1)
                        dve.wait_ge(S["free"], 2 * b + 3)

                    one_ahead(dve, rounded, search)

        def last_pass():
            with ExitStack() as inner:
                S = {n: inner.enter_context(nc.semaphore(f"qu_d_{n}")) for n in "real quant point relued added issue".split()}
                s_load = [inner.enter_context(nc.semaphore(f"qu_d_load{j}")) for j in range(2)]
                s_stored = [inner.enter_context(nc.semaphore(f"qu_d_stored{j}")) for j in range(2)]
                block = inner.enter_context(nc.Block())

                @block.gpsimd
                def _(pool):
                    for j in range(2):
                        pool.sem_inc(s_stored[j], START)
                    with pool.Fori(0, B // 2) as pair:
                        for j in range(2):
                            b = pair * 2 + j
                            pool.wait_ge(s_stored[j], at(16 * pair))
                            pool.sem_inc(S["issue"], 1)
                            pool.dma_start(xin[:, j, :], x_img[bass.ds(b, 1)].rearrange("o c n -> (o c) n")).then_inc(s_load[j], 16)

                @block.scalar
                def _(act):
                    act.sem_inc(S["real"], START)
                    act.sem_inc(S["relued"], START)

                    def scaled(pair, j):
                        b = pair * 2 + j
                        act.wait_ge(S["quant"], at(b - 1))
                        act.sem_inc(S["issue"], 1)
                        act.activation(real[:, j, :], held[:, img(b)], ACT.Identity, bias=few[:, 5:6], scale=few[:, 4:5]).then_inc(S["real"], 1)

                    def positive(pair, j):
                        b = pair * 2 + j
                        for c in range(NCK):
                            act.wait_ge(S["point"], at(NCK * b + c + 1))
                            act.wait_ge(S["added"], at(NCK * b + c - back4(c) + 1))
                            act.activation(relued[:, c % 4, :], bank[c][:, 0:CPX], ACT.Relu, bias=V["pb2"], scale=few[:, 0:1]).then_inc(S["relued"], 1)

                    one_ahead(act, scaled, positive)

                @block.tensor
                def _(pe):
                    pe.sem_inc(S["point"], START)
                    with pe.Fori(0, B // 2) as pair:
                        for j in range(2):
                            b = pair * 2 + j
                            pe.wait_ge(S["quant"], at(b + 1))
                            for c in range(NCK):
                                pe.wait_ge(S["relued"], at(NCK * b + c - NCK + 1))
                                pe.matmul(bank[c][:, 0:CPX], point["p2"][:], quant[:, j, ck(c)], start=True, stop=True).then_inc(S["point"], 1)

                @block.vector
                def _(dve):
                    dve.sem_inc(S["quant"], START)
                    dve.sem_inc(S["added"], START)

                    def rounded(pair, j):
                        b = pair * 2 + j
                        dve.wait_ge(S["real"], at(b + 1))
                        dve.wait_ge(S["point"], at(NCK * b - NCK))
                        dve.tensor_scalar(quant[:, j, :], real[:, j, :], ROUND, ROUND, ALU.add, ALU.subtract).then_inc(S["quant"], 1)

                    def residual(pair, j):
                        b = pair * 2 + j
                        dve.wait_ge(s_load[j], 16 * pair + 16)
                        for c in range(NCK):
                            dve.wait_ge(S["relued"], at(NCK * b + c + 1))
                            dve.tensor_tensor(xin[:, j, ck(c)], xin[:, j, ck(c)], relued[:, c % 4, :], ALU.add).then_inc(S["added"], 1)

                    one_ahead(dve, rounded, residual)

                @block.sync
                def _(sp):
                    with sp.Fori(0, B // 2) as pair:
                        for j in range(2):
                            b = pair * 2 + j
                            sp.wait_ge(S["added"], at(NCK * (b + 1)))
                            sp.dma_start(out_img[bass.ds(b, 1)].rearrange("o c n -> (o c) n"), xin[:, j, :]).then_inc(s_stored[j], 16)
                    for j in range(2):
                        sp.wait_ge(s_stored[j], at(16 * (B // 2)))

        loads = [(ident[:], w["ident"]), (vec[:], w["vec3"]), (peaks[:, 0:1], peak_d)] + [(raw[n][:], w["q_" + n]) for n in raw]
        scales("start", (loads, start_before, 5, start_after))
        sums_pass(True)
        scales("one", ([], ends_before("b1"), 1, next_after("b1", 2)))
        peak_pass()
        scales("two", ([], relu_before("pb1"), 1, next_after("pb1", 3)))
        sums_pass(False)
        scales("three", ([], ends_before("b2"), 1, next_after("b2", 4)))
        last_pass()


def program(nc, d, out):
    B = d["x"].shape[0]
    scratch = lambda name, shape: nc.dram_tensor("scratch_" + name, shape, F32).ap()
    after0 = scratch("after0", [B, C, HW])
    windows = scratch("windows", [B * NCK, C, (CH_ROWS + 2) * HP])
    table = scratch("table", [B * TROWS, 4 * C])
    conv = scratch("conv", [B * NCK, C, CPX])
    after2 = scratch("after2", [B, C, HW])
    peak = scratch("peak", [C, 1])
    attention_phase(nc, B, d["x"], d, after0)
    spread_phase(nc, B, after0, d["ident"], windows, table)
    deform_phase(nc, B * NCK, windows, table, d["base"], d["ident"], d["woff"], d["boff"], d["wdcn"], conv)
    fourier_phase(nc, B, conv.rearrange("(b k) c n -> b k c n", k=NCK), after0, d, after2, peak)
    quantised_phase(nc, B, after2, peak, d, out)


def lay_out(i):
    import numpy as np
    L0, L1, L2, L3 = ({k[8:]: v for k, v in i.items() if k.startswith(f"L{n}_conv_")} for n in range(4))
    B = i["x"].shape[0]
    third = lambda a: [a[k * C:(k + 1) * C] for k in range(3)]
    named0 = dict(L0, mlp_b1_0=third(L0["mlp_b1"])[0], mlp_b1_1=third(L0["mlp_b1"])[1], mlp_b1_2=third(L0["mlp_b1"])[2],
                  q_b=third(L0["qkv_b"])[0], k_b=third(L0["qkv_b"])[1], v_b=third(L0["qkv_b"])[2])
    tm, tr = L1["w_tm"].reshape(4, C, 9), L1["w_tr"].reshape(2, C, 9)
    order = lambda m, r: np.stack([m[0], m[2], m[1], m[3], r[0], r[1]])

    def block_diagonal(a):
        whole, n = np.zeros((C, C), np.float32), a.shape[1]
        for k in range(a.shape[0]):
            whole[k * n:(k + 1) * n, k * n:(k + 1) * n] = a[k]
        return whole

    group = np.arange(C) // 4
    named2 = {"gamma": L1["gn_gamma"], "beta": L1["gn_beta"], "b1r": L2["b1"][0].ravel(), "b1i": L2["b1"][1].ravel(),
              "b2r": L2["b2"][0].ravel(), "b2i": L2["b2"][1].ravel()}
    return {
        "x": i["x"].reshape(B, C, HW),
        "ident": np.eye(C, dtype=np.float32),
        "mean_of": np.full((C, C), 1.0 / C, np.float32),
        "vec0": np.stack([named0[n] for n in VEC0], 1),
        "taps3": L0["pos_w"].reshape(C, 9),
        "taps5": L0["lepe_w"].reshape(C, 25),
        "wqkv": L0["qkv_w"], "wo": L0["wo_w"], "w1": L0["mlp_w1"],
        "w2": L0["mlp_w2"].reshape(HID, C, C).transpose(1, 0, 2),
        "base": chunk_bases(B),
        "woff": order(tm, tr).transpose(1, 2, 0),
        "boff": np.broadcast_to(order(L1["b_tm"], L1["b_tr"]), (TPX, 6)),
        "wdcn": L1["w_dcn"].reshape(C, C, 9).transpose(1, 2, 0),
        "group_mean": ((group[:, None] == group) / (4.0 * HW)).astype(np.float32),
        "vec2": np.stack([named2[n] for n in VEC2], 1),
        "blocks": np.stack([block_diagonal(L2[n][p]) for n in ("w1", "w2") for p in range(2)], 1),
        **transform_matrices(),
        "vec3": np.stack([L3[n] for n in VEC3], 1),
        "q_w1": L3["w1"].reshape(C, 9), "q_w2": L3["w2"].reshape(C, 9),
        "q_p1": L3["p1"].reshape(C, C).T, "q_p2": L3["p2"].reshape(C, C).T,
    }


def kernel(**inputs):
    import numpy as np
    import concourse.bacc as bacc
    from concourse.bass_utils import run_bass_kernel_spmd

    nc = bacc.Bacc("TRN2", target_bir_lowering=False, num_devices=1)
    arrays = {n: np.ascontiguousarray(a) for n, a in lay_out({n: np.ascontiguousarray(a) for n, a in inputs.items()}).items()}
    d = {n: nc.dram_tensor("in_" + n, a.shape, mybir.dt.from_np(a.dtype), kind="ExternalInput").ap() for n, a in arrays.items()}
    shape = inputs["x"].shape
    out = nc.dram_tensor("out", shape, F32, kind="ExternalOutput").ap()
    program(nc, d, out.rearrange("b c h w -> b c (h w)"))
    r = run_bass_kernel_spmd(nc, [{"in_" + n: a for n, a in arrays.items()}], core_ids=[0])
    return r.results[0]["out"]
```
